# Optimizing a Trainium2 kernel written in Bass

```python
import numpy as np
import jax
import jax.numpy as jnp

def _softmax(x, axis=-1):
    return jax.nn.softmax(x, axis=axis)

def _gelu(x):
    return jax.nn.gelu(x, approximate=True)

def _silu(x):
    return jax.nn.silu(x)

def _sigmoid(x):
    return jax.nn.sigmoid(x)

def _layernorm(x, axis=-1, eps=1e-05):
    m = jnp.mean(x, axis=axis, keepdims=True)
    v = jnp.var(x, axis=axis, keepdims=True)
    return (x - m) / jnp.sqrt(v + eps)

def _scatter_add(tgt, idx, src, axis=0):
    return tgt.at[idx].add(src)

def _segment_sum(src, seg, n):
    return jax.ops.segment_sum(src, seg, n)
kernel_name = 'mk_metaformer_d2_conv_nhwc768_r2_d189d4'

def setup_inputs(seed: int=0):
    np.random.seed(seed)
    _w = jnp.asarray

    def _rec_inputs():
        import jax
        import jax.numpy as jnp
        _gk = jax.random.key(seed)
        x = -0.0005963 + 1.001 * jax.random.normal(jax.random.fold_in(_gk, 1), (1, 32, 32, 384), jnp.float32)
        return x
    x = _rec_inputs()

    def _L0_conv_setup():
        import jax, jax.numpy as jnp
        import numpy as np
        NUM_HEADS = 12
        KEY_DIM = 32
        H = W = 32
        C = NUM_HEADS * KEY_DIM

        def _gather_rel_pos(rel_pos, q_size, k_size):
            q = jnp.arange(q_size)[:, None]
            k = jnp.arange(k_size)[None, :]
            idx = (q - k + (k_size - 1)).astype(jnp.int32)
            return rel_pos[idx]
        key = jax.random.key(seed)
        ks = jax.random.split(key, 7)
        return {'x': jax.random.normal(ks[0], (1, H, W, C), jnp.float32), 'qkv_w': jax.random.normal(ks[1], (C, 3 * C), jnp.float32) * C ** (-0.5), 'qkv_b': jax.random.normal(ks[2], (3 * C,), jnp.float32) * 0.02, 'proj_w': jax.random.normal(ks[3], (C, C), jnp.float32) * C ** (-0.5), 'proj_b': jax.random.normal(ks[4], (C,), jnp.float32) * 0.02, 'rel_pos_h': jax.random.normal(ks[5], (2 * H - 1, KEY_DIM), jnp.float32) * 0.02, 'rel_pos_w': jax.random.normal(ks[6], (2 * W - 1, KEY_DIM), jnp.float32) * 0.02}
    _L0_conv_all = _L0_conv_setup()
    _L0_conv_in = {k: v for k, v in _L0_conv_all.items() if k in ('qkv_w', 'qkv_b', 'proj_w', 'proj_b', 'rel_pos_h', 'rel_pos_w')}
    del _L0_conv_all

    def _L0_ffn_setup():
        import jax, jax.numpy as jnp
        import numpy as np
        ALPHA = 1.702
        LIMIT = 7.0
        TOP_K = 2
        B, S, H, E, I = (2, 512, 384, 8, 384)
        key = jax.random.key(seed)
        ks = jax.random.split(key, 7)
        scale = 0.02
        return {'hidden_states': jax.random.normal(ks[0], (B, S, H), dtype=jnp.float32), 'Wr': jax.random.normal(ks[1], (H, E), dtype=jnp.float32) * scale, 'br': jax.random.normal(ks[2], (E,), dtype=jnp.float32) * scale, 'Wgu': jax.random.normal(ks[3], (E, H, 2 * I), dtype=jnp.float32) * scale, 'bgu': jax.random.normal(ks[4], (E, 2 * I), dtype=jnp.float32) * scale, 'Wd': jax.random.normal(ks[5], (E, I, H), dtype=jnp.float32) * scale, 'bd': jax.random.normal(ks[6], (E, H), dtype=jnp.float32) * scale}
    _L0_ffn_all = _L0_ffn_setup()
    _L0_ffn_in = {k: v for k, v in _L0_ffn_all.items() if k in ('Wr', 'br', 'Wgu', 'bgu', 'Wd', 'bd')}
    del _L0_ffn_all

    def _L1_conv_setup():
        import jax, jax.numpy as jnp
        import numpy as np
        D_HEAD = 32
        KV_GROUPS = 3
        KSIZE = 7

        def _win_idx(L, ksize):
            start = jnp.clip(jnp.arange(L) - ksize // 2, 0, L - ksize)
            return start[:, None] + jnp.arange(ksize)[None, :]

        def _natten2d(q, k, v, ksize):
            H, W = (q.shape[2], q.shape[3])
            ih = _win_idx(H, ksize)
            iw = _win_idx(W, ksize)
            kg = k[:, :, ih[:, None, :, None], iw[None, :, None, :], :]
            vg = v[:, :, ih[:, None, :, None], iw[None, :, None, :], :]
            logits = jnp.einsum('nhije,nhijabe->nhijab', q, kg)
            n_, nh = logits.shape[:2]
            a = jax.nn.softmax(logits.reshape(n_, nh, H, W, ksize * ksize), axis=-1)
            a = a.reshape(logits.shape)
            return jnp.einsum('nhijab,nhijabe->nhije', a, vg)

        def _to_heads(p, nh, e):
            n, h, w, _ = p.shape
            return p.reshape(n, h, w, nh, e).transpose(0, 3, 1, 2, 4)
        key = jax.random.key(seed)
        k1, k2, k3 = jax.random.split(key, 3)
        x = jax.random.normal(k1, (2, 32, 32, 384), dtype=jnp.float32)
        w_qkv = jax.random.normal(k2, (640, 384), dtype=jnp.float32) * 0.02
        w_out = jax.random.normal(k3, (384, 384), dtype=jnp.float32) * 0.02
        return {'x': x, 'w_qkv': w_qkv, 'w_out': w_out}
    _L1_conv_all = _L1_conv_setup()
    _L1_conv_in = {k: v for k, v in _L1_conv_all.items() if k in ('w_qkv', 'w_out')}
    del _L1_conv_all

    def _L1_ffn_setup():
        import jax, jax.numpy as jnp
        import numpy as np
        K_ACTIVE = 2
        key = jax.random.key(seed)
        ks = jax.random.split(key, 9)
        B, S, D, F, E, NS = (2, 1024, 384, 768, 8, 1)
        sd = 1.0 / np.sqrt(D)
        sf = 1.0 / np.sqrt(F)
        return {'x': jax.random.normal(ks[0], (B, S, D), jnp.float32), 'Wg_s': jax.random.normal(ks[1], (NS, D, F), jnp.float32) * sd, 'Wu_s': jax.random.normal(ks[2], (NS, D, F), jnp.float32) * sd, 'Wd_s': jax.random.normal(ks[3], (NS, F, D), jnp.float32) * sf, 'Wg_r': jax.random.normal(ks[4], (E, D, F), jnp.float32) * sd, 'Wu_r': jax.random.normal(ks[5], (E, D, F), jnp.float32) * sd, 'Wd_r': jax.random.normal(ks[6], (E, F, D), jnp.float32) * sf, 'W_router': jax.random.normal(ks[7], (D, E), jnp.float32) * sd, 'expert_bias': jnp.zeros((E,), jnp.float32)}
    _L1_ffn_all = _L1_ffn_setup()
    _L1_ffn_in = {k: v for k, v in _L1_ffn_all.items() if k in ('Wg_s', 'Wu_s', 'Wd_s', 'Wg_r', 'Wu_r', 'Wd_r', 'W_router', 'expert_bias')}
    del _L1_ffn_all
    return {'x': x, 'L0_conv_qkv_w': _L0_conv_in['qkv_w'], 'L0_conv_qkv_b': _L0_conv_in['qkv_b'], 'L0_conv_proj_w': _L0_conv_in['proj_w'], 'L0_conv_proj_b': _L0_conv_in['proj_b'], 'L0_conv_rel_pos_h': _L0_conv_in['rel_pos_h'], 'L0_conv_rel_pos_w': _L0_conv_in['rel_pos_w'], 'L0_ffn_Wr': _L0_ffn_in['Wr'], 'L0_ffn_br': _L0_ffn_in['br'], 'L0_ffn_Wgu': _L0_ffn_in['Wgu'], 'L0_ffn_bgu': _L0_ffn_in['bgu'], 'L0_ffn_Wd': _L0_ffn_in['Wd'], 'L0_ffn_bd': _L0_ffn_in['bd'], 'L1_conv_w_qkv': _L1_conv_in['w_qkv'], 'L1_conv_w_out': _L1_conv_in['w_out'], 'L1_ffn_Wg_s': _L1_ffn_in['Wg_s'], 'L1_ffn_Wu_s': _L1_ffn_in['Wu_s'], 'L1_ffn_Wd_s': _L1_ffn_in['Wd_s'], 'L1_ffn_Wg_r': _L1_ffn_in['Wg_r'], 'L1_ffn_Wu_r': _L1_ffn_in['Wu_r'], 'L1_ffn_Wd_r': _L1_ffn_in['Wd_r'], 'L1_ffn_W_router': _L1_ffn_in['W_router'], 'L1_ffn_expert_bias': _L1_ffn_in['expert_bias']}

def reference(x, L0_conv_qkv_w, L0_conv_qkv_b, L0_conv_proj_w, L0_conv_proj_b, L0_conv_rel_pos_h, L0_conv_rel_pos_w, L0_ffn_Wr, L0_ffn_br, L0_ffn_Wgu, L0_ffn_bgu, L0_ffn_Wd, L0_ffn_bd, L1_conv_w_qkv, L1_conv_w_out, L1_ffn_Wg_s, L1_ffn_Wu_s, L1_ffn_Wd_s, L1_ffn_Wg_r, L1_ffn_Wu_r, L1_ffn_Wd_r, L1_ffn_W_router, L1_ffn_expert_bias):
    import jax
    import jax.numpy as jnp

    def _L0_conv_ref(x, qkv_w, qkv_b, proj_w, proj_b, rel_pos_h, rel_pos_w):
        import jax, jax.numpy as jnp
        import numpy as np
        NUM_HEADS = 12
        KEY_DIM = 32
        H = W = 32
        C = NUM_HEADS * KEY_DIM

        def _gather_rel_pos(rel_pos, q_size, k_size):
            q = jnp.arange(q_size)[:, None]
            k = jnp.arange(k_size)[None, :]
            idx = (q - k + (k_size - 1)).astype(jnp.int32)
            return rel_pos[idx]
        B, h, w, c = x.shape
        hw = h * w
        scale = KEY_DIM ** (-0.5)
        qkv = jnp.einsum('bhwc,cd->bhwd', x, qkv_w) + qkv_b
        qkv = qkv.reshape(B, hw, 3, NUM_HEADS, KEY_DIM)
        qkv = jnp.transpose(qkv, (2, 0, 3, 1, 4)).reshape(3, B * NUM_HEADS, hw, KEY_DIM)
        q, k, v = (qkv[0], qkv[1], qkv[2])
        attn = jnp.einsum('bqd,bkd->bqk', q * scale, k)
        Rh = _gather_rel_pos(rel_pos_h, h, h)
        Rw = _gather_rel_pos(rel_pos_w, w, w)
        rq = q.reshape(B * NUM_HEADS, h, w, KEY_DIM)
        rel_h = jnp.einsum('bhwc,hkc->bhwk', rq, Rh)
        rel_w = jnp.einsum('bhwc,wkc->bhwk', rq, Rw)
        attn = attn.reshape(B * NUM_HEADS, h, w, h, w)
        attn = attn + rel_h[..., :, None] + rel_w[..., None, :]
        attn = attn.reshape(B * NUM_HEADS, hw, hw)
        attn = jax.nn.softmax(attn, axis=-1)
        out = jnp.einsum('bqk,bkd->bqd', attn, v)
        out = out.reshape(B, NUM_HEADS, h, w, KEY_DIM)
        out = jnp.transpose(out, (0, 2, 3, 1, 4)).reshape(B, h, w, c)
        return jnp.einsum('bhwc,cd->bhwd', out, proj_w) + proj_b

    def _L0_ffn_ref(hidden_states, Wr, br, Wgu, bgu, Wd, bd):
        import jax, jax.numpy as jnp
        import numpy as np
        ALPHA = 1.702
        LIMIT = 7.0
        TOP_K = 2
        B, S, H, E, I = (2, 512, 384, 8, 384)
        logits = jnp.einsum('bsh,he->bse', hidden_states, Wr) + br
        topk_vals, topk_idx = jax.lax.top_k(logits, TOP_K)
        router_scores = jax.nn.softmax(topk_vals, axis=-1)
        gu = jnp.einsum('bsh,ehf->bsef', hidden_states, Wgu) + bgu
        gu = jnp.minimum(gu, LIMIT)
        gate = gu[..., :I]
        up = jnp.maximum(gu[..., I:], -LIMIT)
        glu = gate * jax.nn.sigmoid(gate * ALPHA)
        activated = (up + 1.0) * glu
        down = jnp.einsum('bsei,eih->bseh', activated, Wd) + bd
        sel = jnp.take_along_axis(down, topk_idx[..., None], axis=2)
        output = jnp.sum(sel * router_scores[..., None], axis=2)
        return output

    def _L1_conv_ref(x, w_qkv, w_out):
        import jax, jax.numpy as jnp
        import numpy as np
        D_HEAD = 32
        KV_GROUPS = 3
        KSIZE = 7

        def _win_idx(L, ksize):
            start = jnp.clip(jnp.arange(L) - ksize // 2, 0, L - ksize)
            return start[:, None] + jnp.arange(ksize)[None, :]

        def _natten2d(q, k, v, ksize):
            H, W = (q.shape[2], q.shape[3])
            ih = _win_idx(H, ksize)
            iw = _win_idx(W, ksize)
            kg = k[:, :, ih[:, None, :, None], iw[None, :, None, :], :]
            vg = v[:, :, ih[:, None, :, None], iw[None, :, None, :], :]
            logits = jnp.einsum('nhije,nhijabe->nhijab', q, kg)
            n_, nh = logits.shape[:2]
            a = jax.nn.softmax(logits.reshape(n_, nh, H, W, ksize * ksize), axis=-1)
            a = a.reshape(logits.shape)
            return jnp.einsum('nhijab,nhijabe->nhije', a, vg)

        def _to_heads(p, nh, e):
            n, h, w, _ = p.shape
            return p.reshape(n, h, w, nh, e).transpose(0, 3, 1, 2, 4)
        n, H, W, d_model = x.shape
        q_heads = d_model // D_HEAD
        kv_heads = q_heads // KV_GROUPS
        qkv = x @ w_qkv.T
        q, k, v = jnp.split(qkv, [q_heads * D_HEAD, (q_heads + kv_heads) * D_HEAD], axis=-1)
        q = _to_heads(q, q_heads, D_HEAD)
        k = jnp.tile(_to_heads(k, kv_heads, D_HEAD), (1, KV_GROUPS, 1, 1, 1))
        v = jnp.tile(_to_heads(v, kv_heads, D_HEAD), (1, KV_GROUPS, 1, 1, 1))
        q = q / D_HEAD ** 0.5
        o = _natten2d(q, k, v, KSIZE)
        o = o.transpose(0, 2, 3, 1, 4).reshape(n, H, W, d_model)
        return o @ w_out.T

    def _L1_ffn_ref(x, Wg_s, Wu_s, Wd_s, Wg_r, Wu_r, Wd_r, W_router, expert_bias):
        import jax, jax.numpy as jnp
        import numpy as np
        K_ACTIVE = 2
        B, S, D = x.shape
        E = Wg_r.shape[0]
        xf = x.reshape(-1, D)
        T = xf.shape[0]
        g_s = jax.nn.silu(jnp.einsum('td,edf->etf', xf, Wg_s))
        u_s = jnp.einsum('td,edf->etf', xf, Wu_s)
        shared_out = jnp.einsum('etf,efd->td', g_s * u_s, Wd_s)
        logits = xf @ W_router + expert_bias
        top_vals, top_idx = jax.lax.top_k(logits, K_ACTIVE)
        rw = jax.nn.softmax(top_vals, axis=-1)
        combine = jnp.zeros((T, E), xf.dtype).at[jnp.arange(T)[:, None], top_idx].set(rw)
        g_r = jax.nn.silu(jnp.einsum('td,edf->etf', xf, Wg_r))
        u_r = jnp.einsum('td,edf->etf', xf, Wu_r)
        out_e = jnp.einsum('etf,efd->etd', g_r * u_r, Wd_r)
        routed_out = jnp.einsum('etd,te->td', out_e, combine)
        return (shared_out + routed_out).reshape(B, S, D)

    def _gn(v, G=32, eps=1e-05):
        B_, H_, W_, C_ = v.shape
        g = v.reshape(B_, H_, W_, G, C_ // G)
        m = jnp.mean(g, axis=(1, 2, 4), keepdims=True)
        s = jnp.var(g, axis=(1, 2, 4), keepdims=True)
        return ((g - m) / jnp.sqrt(s + eps)).reshape(v.shape)

    def _ln_c(v, eps=1e-06):
        m = jnp.mean(v, axis=-1, keepdims=True)
        s = jnp.var(v, axis=-1, keepdims=True)
        return (v - m) / jnp.sqrt(s + eps)

    def _ln_t(v, eps=1e-05):
        m = jnp.mean(v, axis=-1, keepdims=True)
        s = jnp.var(v, axis=-1, keepdims=True)
        return (v - m) / jnp.sqrt(s + eps)

    def _to_tokens(v):
        B_, H_, W_, C_ = v.shape
        return v.reshape(B_, H_ * W_, C_)

    def _from_tokens(t, like):
        return t.reshape(like.shape)
    x = x + _L0_conv_ref(_ln_c(x), L0_conv_qkv_w, L0_conv_qkv_b, L0_conv_proj_w, L0_conv_proj_b, L0_conv_rel_pos_h, L0_conv_rel_pos_w)
    t = _to_tokens(x)
    t = t + _L0_ffn_ref(_ln_t(t), L0_ffn_Wr, L0_ffn_br, L0_ffn_Wgu, L0_ffn_bgu, L0_ffn_Wd, L0_ffn_bd)
    x = _from_tokens(t, x)
    x = x + _L1_conv_ref(_ln_c(x), L1_conv_w_qkv, L1_conv_w_out)
    t = _to_tokens(x)
    t = t + _L1_ffn_ref(_ln_t(t), L1_ffn_Wg_s, L1_ffn_Wu_s, L1_ffn_Wd_s, L1_ffn_Wg_r, L1_ffn_Wu_r, L1_ffn_Wd_r, L1_ffn_W_router, L1_ffn_expert_bias)
    x = _from_tokens(t, x)
    return x

_drawn_inputs = setup_inputs


def setup_inputs(seed=0):
    import zlib

    import numpy as np

    out = dict(_drawn_inputs(seed))
    spreads = {'L1_ffn_expert_bias': (0.0, 0.1)}
    factors = {'L0_conv_rel_pos_h': 2.728,
     'L0_conv_rel_pos_w': 2.73,
     'L0_ffn_br': 2.956,
     'L0_ffn_bgu': 3.118}
    for name, (base, spread) in spreads.items():
        noise = np.random.default_rng([zlib.crc32(name.encode()), seed]).standard_normal(out[name].shape)
        drawn = base * np.exp(spread * noise) if base else spread * noise
        out[name] = jnp.asarray(drawn.astype(out[name].dtype))
    for name, factor in factors.items():
        out[name] = (out[name] * factor).astype(out[name].dtype)
    return out
```

```python
from contextlib import ExitStack

import concourse.bass as bass
from concourse import mybir

F32 = mybir.dt.float32
I32 = mybir.dt.int32
U32 = mybir.dt.uint32
ACT = mybir.ActivationFunctionType
ALU = mybir.AluOpType
AX = mybir.AxisListType

P = 128
GRID = 32
T = GRID * GRID
NT = T // P
C = 384
KC = C // P
D = 32
G = P // D
QK_SCALE = D ** -0.5
BANK = 512
HALF = T // BANK
WIN = 7
MASKED = -float(2 ** 100)
E = 8
TOP = 2
ALPHA, LIMIT = 1.702, 7.0
ROUTED_BLOCKS = (TOP * T + E * (P - 1)) // P
REL = 2 * GRID - 1


class Steps:

    def __init__(self, eng, sem):
        self.eng, self.sem, self.n, self.off = eng, sem, 0, None

    def value(self):
        return self.n if self.off is None else self.off + self.n

    def wait(self, ins):
        self.n += 1
        ins.then_inc(self.sem, 1)
        self.eng.wait_ge(self.sem, self.value())

    def enter(self, turn, per_turn):
        self.first, self.per = self.n, per_turn
        self.off = turn * per_turn

    def leave(self, turns):
        assert self.n - self.first == self.per
        self.off = None
        self.n = self.first + self.per * turns


class Moe:

    def __init__(self, layer, inner, shared):
        self.layer, self.I, self.shared = layer, inner, shared
        self.IC = inner // P
        self.ordinals = E + shared
        self.first_routed = NT * shared
        self.blocks = self.first_routed + ROUTED_BLOCKS
        self.loads = 2 if shared else 4
        self.blocks_before = 0
        self.loads_before = 0


def build(nc, x, qkv_w, qk_b, v_b, proj_w, proj_b, rel_both, Wr0, br0, Wgu0, bgu0, Wd0, bd0,
          w_qkv1, w_out1, Wg_s, Wu_s, Wd_s, Wg_r, Wu_r, Wd_r, Wr1, br1, out, stop_after=4):
    ctx = ExitStack()
    base = [nc.sbuf_base + (-nc.sbuf_base) % 64]
    top = [0]

    def sb(name, shape, dt=F32):
        size = 2 if dt == mybir.dt.bfloat16 else 4
        for n in shape[1:]:
            size *= n
        t = nc.alloc_sbuf_tensor_at(name, shape, dt, offset=base[0])
        base[0] += size + (-size) % 64
        top[0] = max(top[0], base[0])
        return t

    moes = [Moe(0, 384, 0), Moe(1, 768, 1)]
    moes[1].blocks_before = moes[0].blocks
    moes[1].loads_before = moes[0].loads * moes[0].ordinals

    with ctx:
        def sem(name):
            return ctx.enter_context(nc.semaphore(name))

        X = sb("X", [P, NT, C])
        Xn = sb("Xn", [P, NT, C])
        expS = nc.alloc_sbuf_tensor_at("expS", [P, 4, 2 * BANK], F32, offset=base[0] - 4 * NT * C)
        base[0] += 4 * (4 * 2 * BANK - NT * C)
        XnT = sb("XnT", [P, KC, T])
        ident = sb("ident", [P, P])
        before = sb("before", [P, P])
        ones = sb("ones", [P, P])
        stats = sb("stats", [P, NT, 6])
        mv = sb("mv", [P, NT, 2])
        var_eps = sb("var_eps", [P, NT])
        std = sb("std", [P, NT])
        rstd = sb("rstd", [P, NT])
        router_w = sb("router_w", [P, 2, KC, E])
        router_b = sb("router_b", [P, 2, E])
        iota_e = sb("iota_e", [P, E])
        iota_blk = sb("iota_blk", [P, 32])
        thresholds = sb("thresholds", [P, 8])
        logits = sb("logits", [P, NT, E])
        top8 = sb("top8", [P, NT, 8])
        top8i = sb("top8i", [P, NT, 8], U32)
        top_f = sb("top_f", [P, NT, 2])
        gap = sb("gap", [P, NT])
        weight = sb("weight", [P, 2, NT])
        chosen = sb("chosen", [P, 2, NT, E])
        picked = sb("picked", [P, NT, E])
        tile_cum = [sb(f"tile_cum{i}", [P, NT, E]) for i in range(4)]
        blk_cum = [sb(f"blk_cum{i}", [P, E]) for i in range(4)]
        over = sb("over", [P, E, 8])
        n_blk = sb("n_blk", [P, E])
        start_row = sb("start_row", [P, E])
        place = sb("place", [P, NT, E])
        place_k = sb("place_k", [P, 2, NT, E])
        row_f = sb("row_f", [P, 2, NT])
        row_i = sb("row_i", [P, 2, NT], I32)
        blk_ge = sb("blk_ge", [P, 32, E])
        ord_f = sb("ord_f", [P, 32])
        end_f = sb("end_f", [P, 16])
        ord_i = [sb(f"ord_i{n}", [P, 32], I32) for n in range(2)]
        end_i = [sb(f"end_i{n}", [P, 16], I32) for n in range(2)]
        shared_base = base[0]

        Wqkv = sb("Wqkv", [P, KC, 3 * C])
        Wproj = sb("Wproj", [P, KC, C])
        qk_bias = sb("qk_bias", [P, 2 * KC])
        v_bias = sb("v_bias", [P, C])
        p_bias = sb("p_bias", [P, C])
        relh_bd = sb("relh_bd", [P, REL, G])
        relw_bd = sb("relw_bd", [P, REL, G])
        rel_t = sb("rel_t", [P, 2, REL])
        qT = sb("qT", [P, KC, T])
        kT = sb("kT", [P, KC, T])
        relhT = sb("relhT", [P, KC, T])
        relwT = sb("relwT", [P, KC, T])
        V = sb("V", [P, NT, C])
        Qa = sb("Qa", [P, 2, G, T])
        Ka = sb("Ka", [P, 2, G, T])
        key_const = Qa[:, 1, 0, :]
        mask_const = Qa[:, 1, 1, :]
        nmax = sb("nmax", [P, KC, G * NT])
        recip = sb("recip", [P, BANK])
        attT = XnT

        base[0] = shared_base
        Wgu, Wd, bgu, bd = [], [], [], []
        for m in moes:
            base[0] = shared_base
            Wgu.append(sb(f"Wgu{m.layer}", [P, 2, KC, 2 * m.I]))
            Wd.append(sb(f"Wd{m.layer}", [P, 2, m.IC, C]))
            if not m.shared:
                bgu.append(sb("bgu", [P, 2, 2 * m.I]))
                bd.append(sb("bd", [P, 2, C]))
            else:
                bgu.append(None)
                bd.append(None)
        base[0] = max(base[0], shared_base + 4 * (2 * KC * 2 * 768 + 2 * 6 * C))
        xb = sb("xb", [P, 2, C])
        xbT = sb("xbT", [P, 2, KC, P])
        gated = sb("gated", [P, 2, 768])
        pre = sb("pre", [P, 2, 768])
        hid = sb("hid", [P, 2, 768])
        hidT = sb("hidT", [P, 2, 6, P])
        yb = sb("yb", [P, 2, C])
        got = sb("got", [P, 2, 3, C])
        zero = sb("zero", [P, C])
        assert top[0] <= nc.sbuf_usable_end, (top[0], nc.sbuf_usable_end)

        PS = ctx.enter_context(nc.psum_tensor("PS", [P, 8, BANK], F32))
        xs = nc.dram_tensor("block_rows_in", [(NT + ROUTED_BLOCKS) * P, C], F32, kind="Internal").ap()
        ys = nc.dram_tensor("block_rows_out", [(NT + ROUTED_BLOCKS) * P, C], F32, kind="Internal").ap()

        key_rows = nc.dram_tensor("key_rows", [P, T], F32, kind="Internal").ap()
        mask_rows = nc.dram_tensor("mask_rows", [P, T], F32, kind="Internal").ap()

        x_in = sem("x_in")
        const_in = sem("const_in")
        pool_const = sem("pool_const")
        rel_in = sem("rel_in")
        rel_ready = sem("rel_ready")
        const_stored = sem("const_stored")
        wqkv_in = [sem("wqkv0_in"), sem("wqkv1_in")]
        dve_step = sem("dve_step")
        pool_step = sem("pool_step")
        var_ready = sem("var_ready")
        std_ready = sem("std_ready")
        xn_ready = sem("xn_ready")
        xT_psum = sem("xT_psum")
        xT_act = sem("xT_act")
        xT_dve = sem("xT_dve")
        job_psum = sem("job_psum")
        job_act = sem("job_act")
        job_dve = sem("job_dve")
        aug_in = [sem("aug_in0"), sem("aug_in1")]
        aug_const_in = sem("aug_const_in")
        max_psum = sem("max_psum")
        max_done = sem("max_done")
        nmax_psum = sem("nmax_psum")
        nmax_act = sem("nmax_act")
        score_psum = sem("score_psum")
        exp_done = sem("exp_done")
        pv_done = sem("pv_done")
        norm_done = sem("norm_done")
        proj_psum = sem("proj_psum")
        proj_dve = sem("proj_dve")
        xs_zeroed = sem("xs_zeroed")
        zero_ready = sem("zero_ready")
        route_psum = sem("route_psum")
        gap_ready = sem("gap_ready")
        exp_gap = sem("exp_gap")
        picked_ready = sem("picked_ready")
        rank_psum = sem("rank_psum")
        rows_ready = sem("rows_ready")
        tables_ready = sem("tables_ready")
        scattered = sem("scattered")
        shared_rows = sem("shared_rows")
        w_in = sem("w_in")
        xb_in = [sem("xb_in0"), sem("xb_in1")]
        bT_psum = sem("bT_psum")
        bT_act = sem("bT_act")
        gu_psum = sem("gu_psum")
        gate_act = sem("gate_act")
        pre_dve = sem("pre_dve")
        hid_done = sem("hid_done")
        hT_psum = sem("hT_psum")
        hT_copied = sem("hT_copied")
        y_psum = sem("y_psum")
        y_dve = sem("y_dve")
        y_stored = [sem("y_stored0"), sem("y_stored1")]
        got_in = [sem("got_in0"), sem("got_in1")]
        added = sem("added")
        out_done = sem("out_done")

        block = ctx.enter_context(nc.Block())

        per_row = 16 * G
        AUG_COUNT = [[4 * per_row, 4 * per_row, 8 * per_row], [10 * per_row, 5 * per_row, 11 * per_row]]
        JOBS = [2 * KC * HALF + NT + 16, (KC + 1) * HALF + NT]

        def jobs(layer):
            q = [("q", c, h) for c in range(KC) for h in range(HALF)]
            k = [("k", c, h) for c in range(KC if layer == 0 else 1) for h in range(HALF)]
            v = [("v", t, 0) for t in range(NT)]
            rel = [("relh", n, 0) for n in range(8)] + [("relw", n, 0) for n in range(8)]
            every = q + k + v + (rel if layer == 0 else [])
            assert len(every) == JOBS[layer]
            return every

        def by_act(kind):
            return kind in ("q", "relh")

        def evacuated(eng, layer, n):
            done = jobs(0) if layer else []
            mine = done + jobs(layer)[:n + 1]
            kind = jobs(layer)[n][0]
            count = sum(by_act(j[0]) == by_act(kind) for j in mine)
            eng.wait_ge(job_act if by_act(kind) else job_dve, count)

        def flat(bank, banks):
            return PS[:, bank:bank + banks, :].rearrange("p b n -> p (b n)")

        @block.sync
        def _(sp):
            x_view = x.rearrange("(t p) c -> p t c", p=P)
            for t in range(NT):
                sp.dma_start(X[:, t, :], x_view[:, t, :]).then_inc(x_in, 16)
            sp.dma_start(router_w[:, 0], Wr0.rearrange("(k p) e -> p k e", p=P)).then_inc(const_in, 16)
            sp.dma_start(router_w[:, 1], Wr1.rearrange("(k p) e -> p k e", p=P)).then_inc(const_in, 16)
            sp.dma_start(router_b[:, 0], br0.partition_broadcast(P)).then_inc(const_in, 16)
            sp.dma_start(router_b[:, 1], br1.partition_broadcast(P)).then_inc(const_in, 16)

            for layer in range(2):
                if layer == 0:
                    sp.dma_start(Wqkv[:, :, :], qkv_w.rearrange("(k p) n -> p k n", p=P)).then_inc(wqkv_in[0], 16)
                    sp.dma_start(qk_bias[:, :], qk_b).then_inc(wqkv_in[0], 16)
                    sp.dma_start(v_bias[:, :], v_b.partition_broadcast(P)).then_inc(wqkv_in[0], 16)
                    sp.dma_start(p_bias[:, :], proj_b.partition_broadcast(P)).then_inc(wqkv_in[0], 16)
                    sp.dma_start(Wproj[:, :, :], proj_w.rearrange("(k p) n -> p k n", p=P)).then_inc(wqkv_in[0], 16)
                    for g in range(G):
                        sp.dma_start(rel_t[D * g:D * g + D], rel_both).then_inc(rel_in, 16)
                else:
                    sp.wait_ge(y_psum, moes[0].blocks)
                    sp.wait_ge(added, 8)
                    sp.dma_start(Wqkv[:, :, 0:C + 2 * P], w_qkv1.rearrange("(k p) n -> p k n", p=P)).then_inc(wqkv_in[1], 16)
                    sp.dma_start(Wproj[:, :, :], w_out1.rearrange("(k p) n -> p k n", p=P)).then_inc(wqkv_in[1], 16)
                if layer == 0:
                    sp.wait_ge(pool_const, 2)
                    sp.dma_start(key_rows[D:P, :], key_const[D:P, :]).then_inc(const_stored, 16)
                    sp.dma_start(mask_rows[D:3 * D, :], mask_const[D:3 * D, :]).then_inc(const_stored, 16)
                    sp.wait_ge(const_stored, 32)
                for s in range(2 if layer == 0 else 1):
                    for g in range(G):
                        sp.dma_start(Ka[D:P, s, g, :], key_rows[D:P, :]).then_inc(aug_const_in, 16)
                if layer == 1:
                    for s in range(2):
                        for g in range(G):
                            sp.dma_start(Qa[D:3 * D, s, g, :], mask_rows[D:3 * D, :]).then_inc(aug_const_in, 16)
                evacuated(sp, layer, len(jobs(layer)) - 1)
                if layer == 0:
                    evacuated(sp, 0, [j[0] for j in jobs(0)].index("relw") - 1)
                else:
                    evacuated(sp, 1, [j[0] for j in jobs(1)].index("k") - 1)
                for c in range(KC):
                    s = c % 2
                    if c >= 2:
                        sp.wait_ge(pv_done, 16 * (KC * layer + c - 1))
                    for g in range(G):
                        rows = slice(D * g, D * g + D)
                        sp.dma_start(Qa[0:D, s, g, :], qT[rows, c, :]).then_inc(aug_in[s], 16)
                        if layer == 0:
                            sp.dma_start(Qa[D:2 * D, s, g, :], relhT[g:P:G, c, :]).then_inc(aug_in[s], 16)
                            sp.dma_start(Qa[2 * D:3 * D, s, g, :], relwT[g:P:G, c, :]).then_inc(aug_in[s], 16)
                            sp.dma_start(Ka[0:D, s, g, :], kT[rows, c, :]).then_inc(aug_in[s], 16)
                        elif c == 0:
                            sp.dma_start(Ka[0:D, 0, g, :], kT[rows, 0, :]).then_inc(aug_in[s], 16)

                if stop_after == 2 * layer + 1:
                    break
                m = moes[layer]
                if layer == 0:
                    sp.wait_ge(zero_ready, 1)
                    sp.dma_start(xs.rearrange("(b p) c -> p b c", p=P),
                                 zero[:, :].rearrange("p (a c) -> p a c", a=1).broadcast_to([P, NT + ROUTED_BLOCKS, C])
                                 ).then_inc(xs_zeroed, 16)
                    sp.wait_ge(xs_zeroed, 16)
                if m.shared:
                    sp.wait_ge(xn_ready, NT * 4)
                    sp.dma_start(xs[0:T, :].rearrange("(t p) c -> p t c", p=P), Xn[:, :, :]).then_inc(shared_rows, 16)
                    sp.wait_ge(shared_rows, 16)

                def load(b):
                    sp.dma_start(xb[:, b % 2, :], xs[bass.ds(b * P, P), :]).then_inc(xb_in[b % 2], 16)

                def load_waiting(b, par):
                    sp.wait_ge(bT_psum, m.blocks_before + b - 1)
                    sp.dma_start(xb[:, par, :], xs[bass.ds(b * P, P), :]).then_inc(xb_in[par], 16)

                def store(b, par):
                    sp.wait_ge(y_dve, m.blocks_before + b + 1)
                    sp.dma_start(ys[bass.ds(b * P, P), :], yb[:, par, :]).then_inc(y_stored[par], 16)

                if not m.shared:
                    sp.wait_ge(scattered, 16 * 2 * NT)
                load(0)
                load(1)
                turns = (m.blocks - 5) // 2
                assert m.blocks % 2 == 1

                def step(b, par, more=True):
                    if more:
                        load_waiting(b + 2, par)
                    store(b, par)

                def steps(lo, hi):
                    for b in range(lo, hi):
                        step(b, b % 2, b + 2 < m.blocks)

                if m.shared:
                    steps(0, 6)
                    sp.wait_ge(scattered, 16 * 2 * NT * 2)
                    first = 6
                else:
                    steps(0, 2)
                    first = 2
                last = m.blocks - 3
                with sp.Fori(0, (last - first) // 2) as i:
                    step(i * 2 + first, 0)
                    step(i * 2 + first + 1, 1)
                steps(last, m.blocks)
                if stop_after == 2 * layer + 2:
                    break
            if stop_after in (1, 3):
                sp.wait_ge(proj_dve, 8 * (1 if stop_after == 1 else 2))
            else:
                sp.wait_ge(added, NT * stop_after // 2)
            sp.dma_start(out.rearrange("(t p) c -> p t c", p=P), X[:, :, :]).then_inc(out_done, 16)
            sp.wait_ge(out_done, 16)

        @block.gpsimd
        def _(pool):
            st = Steps(pool, pool_step)
            st.wait(pool.memset(relh_bd[:, :, :], 0.0))
            st.wait(pool.memset(relw_bd[:, :, :], 0.0))
            st.wait(pool.memset(ident[:, :], 0.0))
            st.wait(pool.affine_select(out=ident[:, :], in_=ident[:, :], compare_op=ALU.not_equal, fill=1.0,
                                       base=0, pattern=[[-1, P]], channel_multiplier=1))
            st.wait(pool.memset(ones[:, :], 1.0))
            st.wait(pool.affine_select(out=before[:, :], in_=ones[:, :], compare_op=ALU.is_gt, fill=0.0,
                                       base=0, pattern=[[1, P]], channel_multiplier=-1))
            st.wait(pool.iota(iota_e[:, :], pattern=[[1, E]], base=0, channel_multiplier=0,
                              allow_small_or_imprecise_dtypes=True))
            st.wait(pool.iota(iota_blk[:, :], pattern=[[1, 32]], base=0, channel_multiplier=0,
                              allow_small_or_imprecise_dtypes=True))
            st.wait(pool.iota(thresholds[:, :], pattern=[[P, 8]], base=0, channel_multiplier=0,
                              allow_small_or_imprecise_dtypes=True))
            st.wait(pool.memset(thresholds[:, 0:1], -1.0))
            pool.sem_inc(pool_const, 1)
            kc = key_const.rearrange("p (h w) -> p h w", w=GRID)
            st.wait(pool.memset(key_const, 0.0))
            st.wait(pool.affine_select(out=kc[D:2 * D], in_=kc[D:2 * D], compare_op=ALU.not_equal, fill=1.0,
                                       base=-(GRID - 1), pattern=[[1, GRID], [0, GRID]], channel_multiplier=1))
            st.wait(pool.affine_select(out=kc[2 * D:3 * D], in_=kc[2 * D:3 * D], compare_op=ALU.not_equal, fill=1.0,
                                       base=-(GRID - 1), pattern=[[0, GRID], [1, GRID]], channel_multiplier=1))
            st.wait(pool.memset(key_const[3 * D:3 * D + 1, :], 1.0))
            st.wait(pool.memset(mask_const, 0.0))
            mc = mask_const.rearrange("p (h w) -> p h w", w=GRID)
            for lo, hi, start, slope in ((0, 3, 0, 0), (3, 28, 0, 1), (28, 32, 25, 0)):
                n = hi - lo
                for rows, by_row in ((slice(D, 2 * D), True), (slice(2 * D, 3 * D), False)):
                    view = mc[rows, lo:hi, :] if by_row else mc[rows, :, lo:hi]
                    pat = (lambda s: [[s, n], [0, GRID]]) if by_row else (lambda s: [[0, GRID], [s, n]])
                    st.wait(pool.affine_select(out=view, in_=view, compare_op=ALU.is_ge, fill=MASKED,
                                               base=GRID - 1 - start, pattern=pat(-slope), channel_multiplier=-1))
                    st.wait(pool.affine_select(out=view, in_=view, compare_op=ALU.is_ge, fill=MASKED,
                                               base=start + WIN - 1 - (GRID - 1), pattern=pat(slope),
                                               channel_multiplier=1))
            pool.sem_inc(pool_const, 1)
            pool.wait_ge(rel_in, 16 * G)
            for g in range(G):
                rows = slice(D * g, D * g + D)
                st.wait(pool.tensor_copy(relh_bd[rows, :, g], rel_t[rows, 0, :]))
                st.wait(pool.tensor_copy(relw_bd[rows, :, g], rel_t[rows, 1, :]))
            pool.sem_inc(rel_ready, 1)

            for layer in range(2):
                if stop_after <= 2 * layer + 1:
                    break
                m = moes[layer]
                pool.wait_ge(proj_psum, NT * (layer + 1))
                if layer == 0:
                    pool.memset(zero[:, :], 0.0).then_inc(zero_ready, 1)

                def load_weights(gate_up, down, slot):
                    for n, src in enumerate(gate_up):
                        width = 2 * m.I // len(gate_up)
                        pool.dma_start(Wgu[layer][:, slot, :, n * width:(n + 1) * width],
                                       src.rearrange("(k p) n -> p k n", p=P)).then_inc(w_in, 16)
                    pool.dma_start(Wd[layer][:, slot], down.rearrange("(k p) n -> p k n", p=P)).then_inc(w_in, 16)

                WIN_LOAD = 16 * (3 if m.shared else 4)
                w_before = 0 if layer == 0 else 16 * 4 * E

                def expert(e, slot):
                    if m.shared:
                        load_weights([Wg_r[bass.ds(e, 1)].rearrange("a k n -> (a k) n"),
                                      Wu_r[bass.ds(e, 1)].rearrange("a k n -> (a k) n")],
                                     Wd_r[bass.ds(e, 1)].rearrange("a k n -> (a k) n"), slot)
                    else:
                        load_weights([Wgu0[bass.ds(e, 1)].rearrange("a k n -> (a k) n")],
                                     Wd0[bass.ds(e, 1)].rearrange("a k n -> (a k) n"), slot)
                        pool.dma_start(bgu[0][:, slot, :], bgu0[bass.ds(e, 1)].rearrange("a n -> (a n)").partition_broadcast(P)).then_inc(w_in, 16)
                        pool.dma_start(bd[0][:, slot, :], bd0[bass.ds(e, 1)].rearrange("a n -> (a n)").partition_broadcast(P)).then_inc(w_in, 16)

                if m.shared:
                    load_weights([Wg_s, Wu_s], Wd_s, 0)
                    pool.wait_ge(w_in, w_before + WIN_LOAD)
                    expert(0, 1)
                else:
                    expert(0, 0)
                    pool.wait_ge(w_in, w_before + WIN_LOAD)
                    expert(1, 1)
                pool.wait_ge(rows_ready, layer + 1)
                if layer == 0:
                    pool.wait_ge(xs_zeroed, 16)
                for k in range(TOP):
                    for t in range(NT):
                        pool.indirect_dma_start(
                            xs[:, :], bass.IndirectOffsetOnAxis(ap=row_i[:, k, t:t + 1], axis=0),
                            Xn[:, t, :], None).then_inc(scattered, 16)
                pool.wait_ge(tables_ready, layer + 1)
                with pool.Fori(2, m.ordinals) as q:
                    done = pool.value_load(end_i[layer][0:1, bass.ds(q, 1)], min_val=1, max_val=m.blocks)
                    pool.wait_ge(w_in, (q * WIN_LOAD + w_before))
                    pool.wait_ge(y_dve, done + m.blocks_before)
                    expert(q - m.shared, q % 2)
                for par in range(2):
                    pool.wait_ge(y_stored[par], 16 * sum((mm.blocks + 1 - par) // 2 for mm in moes[:layer + 1]))
                for t in range(NT):
                    if t >= 2 or layer:
                        pool.wait_ge(added, NT * layer + t - 1 if t >= 2 else NT * layer)
                    for k in range(TOP):
                        pool.indirect_dma_start(
                            got[:, t % 2, k, :], None, ys[0:m.blocks * P, :],
                            bass.IndirectOffsetOnAxis(ap=row_i[:, k, t:t + 1], axis=0)).then_inc(got_in[t % 2], 16)
                    if m.shared:
                        pool.dma_start(got[:, t % 2, TOP, :], ys[t * P:(t + 1) * P, :]).then_inc(got_in[t % 2], 16)

        @block.scalar
        def _(act):
            def ln_and_transposes(n):
                act.wait_ge(var_ready, n + 1)
                act.activation(std[:, :], var_eps[:, :], ACT.Sqrt).then_inc(std_ready, 1)
                for j in range(0, 6, 2):
                    act.wait_ge(xT_psum, 6 * n + j + 1)
                    act.activation(XnT[:, j // 2, (j % 2) * BANK:(j % 2 + 1) * BANK], PS[:, j, :],
                                   ACT.Copy).then_inc(xT_act, 1)

            for layer in range(2):
                ln_and_transposes(2 * layer)
                act.wait_ge(wqkv_in[layer], 16 * (5 if layer == 0 else 2))
                for n, (kind, a, b) in enumerate(jobs(layer)):
                    if not by_act(kind):
                        continue
                    act.wait_ge(job_psum, JOBS[0] * layer + n + 1)
                    bank = n % 8
                    if kind == "q":
                        dst = qT[:, a, b * BANK:(b + 1) * BANK]
                        if layer == 0:
                            act.activation(dst, PS[:, bank, :], ACT.Identity, bias=qk_bias[:, a:a + 1]).then_inc(job_act, 1)
                        else:
                            act.activation(dst, PS[:, bank, :], ACT.Copy).then_inc(job_act, 1)
                    else:
                        for c in range(KC):
                            last = act.activation(
                                relhT[:, c, a * P:(a + 1) * P].rearrange("p (h w) -> p h w", w=GRID),
                                PS[:, bank, 0:4 * KC * GRID].rearrange("p (h c w) -> p h c w", h=4, c=KC)[:, :, c, :],
                                ACT.Copy)
                        last.then_inc(job_act, 1)
                for c in range(KC):
                    n = KC * layer + c
                    act.wait_ge(nmax_psum, n + 1)
                    for g in range(G):
                        last = act.activation(Qa[3 * D:P, c % 2, g, :],
                                              PS[D * g:D * g + D, 6:8, :].rearrange("p b n -> p (b n)"), ACT.Copy)
                    last.then_inc(nmax_act, 1)
                    def exps(i):
                        for j in range(4):
                            u = i * 4 + j
                            act.wait_ge(score_psum, u + (32 * n + 1))
                            if j % 2 == 0 and not (n == 0 and isinstance(i, int)):
                                act.wait_ge(pv_done, i * 2 + (16 * n + j // 2 - 1))
                            slot = (u + (64 * n + 32)) % 3
                            act.activation(expS[:, j, :].rearrange("p (b n) -> p b n", b=2),
                                           PS[:, bass.ds(slot * 2, 2), :], ACT.Exp).then_inc(exp_done, 1)

                    if n == 0:
                        exps(0)
                    with act.Fori(1 if n == 0 else 0, 8) as i:
                        exps(i)
                if stop_after == 2 * layer + 1:
                    return
                m = moes[layer]
                ln_and_transposes(2 * layer + 1)
                act.wait_ge(gap_ready, layer + 1)
                act.activation(weight[:, 1, :], gap[:, :], ACT.Exp).then_inc(exp_gap, 1)
                o = m.blocks_before

                def copy_xT(b, par):
                    act.wait_ge(bT_psum, b + (o + 1))
                    if not (isinstance(b, int) and b < 2):
                        act.wait_ge(gu_psum, b + (o - 1))
                    act.activation(xbT[:, par].rearrange("p k n -> p (k n)"), PS[:, 6, 0:C], ACT.Copy).then_inc(bT_act, 1)

                def gate(b, par):
                    if m.shared:
                        act.wait_ge(gu_psum, b + (o + 1))
                        if not (isinstance(b, int) and b < 2):
                            act.wait_ge(hid_done, b + (o - 1))
                        act.activation(gated[:, par, 0:m.I], flat(3 * par, 3)[:, 0:m.I], ACT.Silu).then_inc(gate_act, 1)
                    else:
                        act.wait_ge(pre_dve, b + 1)
                        if not (isinstance(b, int) and b < 2):
                            act.wait_ge(hid_done, b - 1)
                        act.activation(gated[:, par, 0:m.I], pre[:, par, 0:m.I], ACT.Sigmoid, scale=ALPHA).then_inc(gate_act, 1)

                def copy_hT(b, par):
                    act.wait_ge(hT_psum, b + (o + 1))
                    if not (isinstance(b, int) and b < 2):
                        act.wait_ge(y_psum, b + (o - 1))
                    act.activation(hidT[:, par, 0:3].rearrange("p k n -> p (k n)"),
                                   PS[:, 3 * par, 0:3 * P], ACT.Copy).then_inc(hT_copied, 1)

                def step(b, par, more):
                    copy_hT(b, par)
                    if more >= 2:
                        copy_xT(b + 2, par)
                    if more >= 1:
                        gate(b + 1, 1 - par)

                copy_xT(0, 0)
                copy_xT(1, 1)
                gate(0, 0)
                for b in range(2):
                    step(b, b, 2)
                with act.Fori(0, (m.blocks - 5) // 2) as i:
                    step(i * 2 + 2, 0, 2)
                    step(i * 2 + 3, 1, 2)
                for b in range(m.blocks - 3, m.blocks):
                    step(b, b % 2, m.blocks - 1 - b)
                if stop_after == 2 * layer + 2:
                    return

        @block.vector
        def _(dve):
            st = Steps(dve, dve_step)

            def layernorm(n, eps):
                if n == 0:
                    dve.wait_ge(x_in, 16 * NT)
                for t in range(NT):
                    last = dve.bn_stats(stats[:, t, :], X[:, t, :])
                st.wait(last)
                for t in range(NT):
                    last = dve.bn_aggr(mv[:, t, :], stats[:, t, :])
                st.wait(last)
                dve.tensor_scalar(var_eps[:, :], mv[:, :, 1], eps, None, ALU.add).then_inc(var_ready, 1)
                dve.wait_ge(std_ready, n + 1)
                st.wait(dve.reciprocal(rstd[:, :], std[:, :]))
                for t in range(NT):
                    dve.tensor_scalar(Xn[:, t, :], X[:, t, :], mv[:, t, 0:1], rstd[:, t:t + 1],
                                      ALU.subtract, ALU.mult).then_inc(xn_ready, 1)
                for j in range(1, 6, 2):
                    dve.wait_ge(xT_psum, 6 * n + j + 1)
                    dve.tensor_copy(XnT[:, j // 2, (j % 2) * BANK:(j % 2 + 1) * BANK], PS[:, j, :]).then_inc(xT_dve, 1)

            for layer in range(2):
                layernorm(2 * layer, 1e-6)
                dve.wait_ge(wqkv_in[layer], 16 * (5 if layer == 0 else 2))
                if layer == 0:
                    st.wait(dve.tensor_tensor(X[:, :, :], X[:, :, :],
                                              p_bias[:, :].rearrange("p (a c) -> p a c", a=1).broadcast_to([P, NT, C]),
                                              ALU.add))
                for n, (kind, a, b) in enumerate(jobs(layer)):
                    if by_act(kind):
                        continue
                    dve.wait_ge(job_psum, JOBS[0] * layer + n + 1)
                    bank = n % 8
                    if kind == "k":
                        bias = qk_bias[:, KC + a:KC + a + 1] if layer == 0 else 0.0
                        dve.tensor_scalar(kT[:, a, b * BANK:(b + 1) * BANK], PS[:, bank, :], bias, QK_SCALE,
                                          ALU.add, ALU.mult).then_inc(job_dve, 1)
                    elif kind == "v":
                        if layer == 0:
                            dve.tensor_tensor(V[:, a, :], PS[:, bank, 0:C], v_bias[:, :], ALU.add).then_inc(job_dve, 1)
                        else:
                            dve.tensor_copy(V[:, a, 0:P], PS[:, bank, 0:P]).then_inc(job_dve, 1)
                    else:
                        for c in range(KC):
                            last = dve.tensor_copy(
                                relwT[:, c, :].rearrange("p (h w) -> p w h", w=GRID)[:, 4 * a:4 * a + 4, :],
                                PS[:, bank, 0:4 * KC * GRID].rearrange("p (w c h) -> p w c h", w=4, c=KC)[:, :, c, :])
                        last.then_inc(job_dve, 1)
                for c in range(KC):
                    n = KC * layer + c
                    with dve.Fori(0, 8) as i:
                        for j in range(4):
                            u = i * 4 + j
                            dve.wait_ge(max_psum, u + (32 * n + 1))
                            ring = (u + 64 * n) % 3
                            dve.tensor_reduce(nmax[:, c, bass.ds(u, 1)], PS[:, bass.ds(ring * 2, 2), :],
                                              axis=AX.XY, op=ALU.max, negate=True).then_inc(max_done, 1)
                    for half in range(HALF):
                        dve.wait_ge(pv_done, 16 * n + 8 * (half + 1))
                        st.wait(dve.reciprocal(recip[:, :], PS[:, 7, :]))
                        dve.tensor_tensor(attT[:, c, half * BANK:(half + 1) * BANK], PS[:, 6, :], recip[:, :],
                                          ALU.mult).then_inc(norm_done, 1)
                for t in range(NT):
                    dve.wait_ge(proj_psum, NT * layer + t + 1)
                    ins = dve.tensor_tensor(X[:, t, :], X[:, t, :], PS[:, t % 6, 0:C], ALU.add).then_inc(proj_dve, 1)
                dve.wait_ge(proj_dve, NT * (layer + 1))
                if stop_after == 2 * layer + 1:
                    return

                m = moes[layer]
                layernorm(2 * layer + 1, 1e-5)
                dve.wait_ge(const_in, 16 * 4)
                dve.wait_ge(pool_const, 2)
                dve.wait_ge(route_psum, layer + 1)
                st.wait(dve.tensor_tensor(logits[:, :, :], PS[:, 6, 0:NT * E].rearrange("p (t e) -> p t e", e=E),
                                          router_b[:, layer, :].rearrange("p (a e) -> p a e", a=1).broadcast_to([P, NT, E]), ALU.add))
                for t in range(NT):
                    last = dve.max(top8[:, t, :], logits[:, t, :])
                st.wait(last)
                for t in range(NT):
                    last = dve.max_index(top8i[:, t, :], top8[:, t, :], logits[:, t, :])
                st.wait(last)
                dve.tensor_tensor(gap[:, :], top8[:, :, 1], top8[:, :, 0], ALU.subtract).then_inc(gap_ready, 1)
                st.wait(dve.tensor_copy(top_f[:, :, :], top8i[:, :, 0:2]))
                for k in range(TOP):
                    last = dve.tensor_tensor(chosen[:, k],
                                             iota_e[:, :].rearrange("p (a e) -> p a e", a=1).broadcast_to([P, NT, E]),
                                             top_f[:, :, k:k + 1].broadcast_to([P, NT, E]), ALU.is_equal)
                st.wait(last)
                dve.tensor_tensor(picked[:, :, :], chosen[:, 0], chosen[:, 1], ALU.add).then_inc(picked_ready, 1)
                dve.wait_ge(exp_gap, layer + 1)
                st.wait(dve.tensor_scalar(weight[:, 0, :], weight[:, 1, :], 1.0, None, ALU.add))
                st.wait(dve.reciprocal(weight[:, 0, :], weight[:, 0, :]))
                st.wait(dve.tensor_tensor(weight[:, 1, :], weight[:, 1, :], weight[:, 0, :], ALU.mult))
                dve.wait_ge(rank_psum, layer + 1)
                rank = PS[:, 7, 0:NT * E].rearrange("p (t e) -> p t e", e=E)
                count = PS[:, 7, NT * E:2 * NT * E].rearrange("p (t e) -> p t e", e=E)
                st.wait(dve.tensor_copy(tile_cum[0][:, :, :], count))
                for r, shift in enumerate((1, 2, 4)):
                    src, dst = tile_cum[r], tile_cum[r + 1]
                    dve.tensor_copy(dst[:, 0:shift], src[:, 0:shift])
                    st.wait(dve.tensor_tensor(dst[:, shift:], src[:, shift:], src[:, :NT - shift], ALU.add))
                st.wait(dve.tensor_tensor(over[:, :, :], tile_cum[3][:, NT - 1, :].rearrange("p (e a) -> p e a", a=1).broadcast_to([P, E, 8]),
                                          thresholds[:, :].rearrange("p (a k) -> p a k", a=1).broadcast_to([P, E, 8]), ALU.is_gt))
                st.wait(dve.tensor_reduce(blk_cum[0][:, :], over[:, :, :], axis=AX.X, op=ALU.add))
                for r, shift in enumerate((1, 2, 4)):
                    src, dst = blk_cum[r], blk_cum[r + 1]
                    dve.tensor_copy(dst[:, 0:shift], src[:, 0:shift])
                    st.wait(dve.tensor_tensor(dst[:, shift:], src[:, shift:], src[:, :E - shift], ALU.add))
                st.wait(dve.tensor_tensor(start_row[:, :], blk_cum[3][:, :], blk_cum[0][:, :], ALU.subtract))
                st.wait(dve.tensor_scalar(start_row[:, :], start_row[:, :], float(m.first_routed), float(P), ALU.add, ALU.mult))
                st.wait(dve.tensor_tensor(place[:, :, :], tile_cum[3][:, :, :], tile_cum[0][:, :, :], ALU.subtract))
                st.wait(dve.tensor_tensor(place[:, :, :], place[:, :, :], rank, ALU.add))
                st.wait(dve.tensor_tensor(place[:, :, :], place[:, :, :],
                                          start_row[:, :].rearrange("p (a e) -> p a e", a=1).broadcast_to([P, NT, E]), ALU.add))
                for k in range(TOP):
                    last = dve.tensor_tensor(place_k[:, k], place[:, :, :], chosen[:, k], ALU.mult)
                st.wait(last)
                st.wait(dve.tensor_reduce(row_f[:, :, :], place_k[:, :, :, :], axis=AX.X, op=ALU.add))
                dve.tensor_copy(row_i[:, :, :], row_f[:, :, :]).then_inc(rows_ready, 1)
                nr = ROUTED_BLOCKS
                st.wait(dve.tensor_tensor(blk_ge[:, 0:nr], iota_blk[:, 0:nr].rearrange("p (b a) -> p b a", a=1).broadcast_to([P, nr, E]),
                                          blk_cum[3][:, :].rearrange("p (a e) -> p a e", a=1).broadcast_to([P, nr, E]), ALU.is_ge))
                if m.shared:
                    st.wait(dve.memset(ord_f[:, 0:NT], 0.0))
                    st.wait(dve.memset(end_f[:, 2:3], float(NT)))
                fr = m.first_routed
                st.wait(dve.tensor_reduce(ord_f[:, fr:fr + nr], blk_ge[:, 0:nr], axis=AX.X, op=ALU.add))
                st.wait(dve.tensor_scalar(ord_f[:, fr:fr + nr], ord_f[:, fr:fr + nr], float(E - 1), float(m.shared), ALU.min, ALU.add))
                st.wait(dve.tensor_scalar(end_f[:, 2 + m.shared:m.ordinals], blk_cum[3][:, 0:m.ordinals - 2 - m.shared], float(fr), None, ALU.add))
                st.wait(dve.tensor_copy(ord_i[layer][:, 0:m.blocks], ord_f[:, 0:m.blocks]))
                dve.tensor_copy(end_i[layer][:, 2:m.ordinals], end_f[:, 2:m.ordinals]).then_inc(tables_ready, 1)
                dve.wait_ge(tables_ready, layer + 1)

                o = m.blocks_before

                def copy_hT(b, par):
                    if not m.shared:
                        return
                    dve.wait_ge(hT_psum, b + (o + 1))
                    if not (isinstance(b, int) and b < 2):
                        dve.wait_ge(y_psum, b + (o - 1))
                    dve.tensor_copy(hidT[:, par, 3:6].rearrange("p k n -> p (k n)"),
                                    PS[:, 3 * par + 1, 0:3 * P]).then_inc(hT_copied, 1)

                def hidden(b, par):
                    I = m.I
                    if m.shared:
                        dve.wait_ge(gate_act, moes[0].blocks + b + 1)
                        if not (isinstance(b, int) and b < 2):
                            dve.wait_ge(hT_psum, b + (o - 1))
                        dve.tensor_tensor(hid[:, par, 0:I], gated[:, par, 0:I], flat(3 * par, 3)[:, I:2 * I],
                                          ALU.mult).then_inc(hid_done, 1)
                        return
                    q = dve.value_load(ord_i[layer][0:1, bass.ds(b, 1)], min_val=0, max_val=m.ordinals - 1)
                    dve.wait_ge(gu_psum, b + 1)
                    s = q % 2
                    dve.wait_ge(w_in, (q + 1) * 64)
                    st.wait(dve.tensor_tensor(pre[:, par, :], flat(3 * par, 2)[:, 0:2 * I],
                                              bgu[0][:, bass.ds(s, 1), :].rearrange("p a n -> p (a n)"), ALU.add))
                    st.wait(dve.tensor_scalar(pre[:, par, 0:I], pre[:, par, 0:I], LIMIT, None, ALU.min))
                    dve.tensor_scalar(pre[:, par, I:2 * I], pre[:, par, I:2 * I], LIMIT, -LIMIT, ALU.min, ALU.max).then_inc(pre_dve, 1)
                    dve.wait_ge(gate_act, b + 1)
                    if not (isinstance(b, int) and b < 2):
                        dve.wait_ge(hT_psum, b - 1)
                    st.wait(dve.tensor_tensor(gated[:, par, I:2 * I], gated[:, par, 0:I], pre[:, par, 0:I], ALU.mult))
                    dve.scalar_tensor_tensor(hid[:, par, 0:I], pre[:, par, I:2 * I], 1.0, gated[:, par, I:2 * I],
                                             ALU.add, ALU.mult).then_inc(hid_done, 1)

                def copy_y(b, par):
                    if not m.shared:
                        q = dve.value_load(ord_i[layer][0:1, bass.ds(b, 1)], min_val=0, max_val=m.ordinals - 1)
                    dve.wait_ge(y_psum, b + (o + 1))
                    if m.shared:
                        dve.wait_ge(y_stored[par], stored_before(b, par))
                        dve.tensor_copy(yb[:, par, :], PS[:, 7, 0:C]).then_inc(y_dve, 1)
                        return
                    if not (isinstance(b, int) and b < 2):
                        dve.wait_ge(y_stored[par], stored_before(b, par))
                    dve.tensor_tensor(yb[:, par, :], PS[:, 7, 0:C],
                                      bd[0][:, bass.ds(q % 2, 1), :].rearrange("p a n -> p (a n)"), ALU.add).then_inc(y_dve, 1)

                def stored_before(b, par):
                    before = 0 if layer == 0 else 16 * ((moes[0].blocks + 1 - par) // 2)
                    if isinstance(b, int):
                        return before + 8 * (b - par)
                    return b * 8 + (before - 8 * par)

                def step(b, par, more):
                    copy_hT(b, par)
                    if more >= 1:
                        hidden(b + 1, 1 - par)
                    copy_y(b, par)

                hidden(0, 0)
                for b in range(2):
                    step(b, b, 2)
                turns = (m.blocks - 5) // 2
                with dve.Fori(0, turns) as i:
                    if not m.shared:
                        st.enter(i, 6)
                    step(i * 2 + 2, 0, 2)
                    step(i * 2 + 3, 1, 2)
                if not m.shared:
                    st.leave(turns)
                for b in range(m.blocks - 3, m.blocks):
                    step(b, b % 2, m.blocks - 1 - b)
                for t in range(NT):
                    per = 32 + 16 * m.shared
                    dve.wait_ge(got_in[t % 2], (NT // 2) * 32 * layer + per * (t // 2 + 1))
                    if m.shared:
                        st.wait(dve.tensor_tensor(X[:, t, :], X[:, t, :], got[:, t % 2, TOP, :], ALU.add))
                    st.wait(dve.scalar_tensor_tensor(X[:, t, :], got[:, t % 2, 0, :], weight[:, 0, t:t + 1], X[:, t, :],
                                                     ALU.mult, ALU.add))
                    dve.scalar_tensor_tensor(X[:, t, :], got[:, t % 2, 1, :], weight[:, 1, t:t + 1], X[:, t, :],
                                             ALU.mult, ALU.add).then_inc(added, 1)
                dve.wait_ge(added, NT * (layer + 1))
                if stop_after == 2 * layer + 2:
                    return

        @block.tensor
        def _(pe):
            pe.wait_ge(pool_const, 2)

            def transposes(n):
                for j in range(6):
                    kc, half = j // 2, j % 2
                    for t in range(4 * half, 4 * half + 4):
                        pe.wait_ge(xn_ready, NT * n + t + 1)
                        last = pe.transpose(PS[:, j, (t % 4) * P:(t % 4 + 1) * P], Xn[:, t, kc * P:(kc + 1) * P], ident[:, :])
                    last.then_inc(xT_psum, 1)
                pe.wait_ge(xT_act, 3 * (n + 1))
                pe.wait_ge(xT_dve, 3 * (n + 1))

            for layer in range(2):
                transposes(2 * layer)
                pe.wait_ge(wqkv_in[layer], 16 * (5 if layer == 0 else 2))
                k_col, v_col, v_width = (C, 2 * C, C) if layer == 0 else (C, C + P, P)
                for n, (kind, a, b) in enumerate(jobs(layer)):
                    bank = n % 8
                    if n >= 8:
                        evacuated(pe, layer, n - 8)
                    if kind in ("q", "k"):
                        col = (0 if kind == "q" else k_col) + a * P
                        for kc in range(KC):
                            last = pe.matmul(PS[:, bank, :], Wqkv[:, kc, col:col + P], XnT[:, kc, b * BANK:(b + 1) * BANK],
                                             start=kc == 0, stop=kc == KC - 1)
                    elif kind == "v":
                        for kc in range(KC):
                            last = pe.matmul(PS[:, bank, 0:v_width], XnT[:, kc, a * P:(a + 1) * P],
                                             Wqkv[:, kc, v_col:v_col + v_width], start=kc == 0, stop=kc == KC - 1)
                    else:
                        if a == 0 and kind == "relh":
                            evacuated(pe, layer, HALF * KC - 1)
                            pe.wait_ge(rel_ready, 1)
                        table = relh_bd if kind == "relh" else relw_bd
                        for r in range(4):
                            i = 4 * a + r
                            rhs = (qT[:, :, i * GRID:(i + 1) * GRID] if kind == "relh" else
                                   qT[:, :, :].rearrange("p c (h w) -> p c h w", w=GRID)[:, :, :, i])
                            last = pe.matmul(PS[:, bank, r * KC * GRID:(r + 1) * KC * GRID].rearrange("p (c n) -> p c n", c=KC),
                                             table[:, i:i + GRID, :].rearrange("p j g -> p (j g)"), rhs, start=r == 0, stop=r == 3, skip_group_check=True)
                    last.then_inc(job_psum, 1)
                njobs = len(jobs(layer))
                for n in range(njobs - 8, njobs):
                    evacuated(pe, layer, n)

                pe.wait_ge(aug_const_in, 16 * (8 if layer == 0 else 8 + 12))
                for c in range(KC):
                    n = KC * layer + c
                    s = c % 2
                    ks = s if layer == 0 else 0
                    pe.wait_ge(aug_in[s], AUG_COUNT[layer][c])
                    def wait_slot(u):
                        prev = 64 * n + u - 3
                        if prev < 0:
                            return
                        pn, pu = prev // 64, prev % 64
                        if pu < 32:
                            pe.wait_ge(max_done, 32 * pn + pu + 1)
                        else:
                            pe.wait_ge(exp_done, 32 * pn + pu - 32 + 1)

                    for g in range(G):
                        for qt in range(NT):
                            u = NT * g + qt
                            wait_slot(u)
                            slot = (64 * n + u) % 3
                            for half in range(HALF):
                                last = pe.matmul(PS[:, 2 * slot + half, :], Qa[0:3 * D, s, g, qt * P:(qt + 1) * P],
                                                 Ka[0:3 * D, ks, g, half * BANK:(half + 1) * BANK], start=True, stop=True)
                            last.then_inc(max_psum, 1)
                    if n > 0:
                        pe.wait_ge(norm_done, 2 * n)
                    for qt in range(NT):
                        pe.wait_ge(max_done, 32 * n + 32)
                        for g in range(G):
                            col = NT * g + qt
                            last = pe.matmul(PS[D * g:D * g + D, 6 + qt // 4, (qt % 4) * P:(qt % 4 + 1) * P],
                                             nmax[:, c, col:col + 1].broadcast_to([P, D]), ident[:, :],
                                             start=qt % 4 == 0, stop=qt % 4 == 3, skip_group_check=True)
                    last.then_inc(nmax_psum, 1)
                    pe.wait_ge(nmax_act, n + 1)

                    def scores(unit):
                        half, kt = unit // NT, unit % NT
                        for pair in range(2):
                            u = 32 + 2 * unit + pair
                            wait_slot(u)
                            slot = (64 * n + u) % 3
                            for j in range(2):
                                g = 2 * pair + j
                                last = pe.matmul(PS[:, 2 * slot + j, :], Ka[:, ks, g, kt * P:(kt + 1) * P],
                                                 Qa[:, s, g, half * BANK:(half + 1) * BANK], start=True, stop=True)
                            last.then_inc(score_psum, 1)

                    def weighted(unit):
                        half, kt = unit // NT, unit % NT
                        pe.wait_ge(exp_done, 32 * n + 2 * unit + 2)
                        if kt == 0 and half > 0:
                            pe.wait_ge(norm_done, 2 * n + half)
                        probs = [expS[:, 2 * (unit % 2) + g // 2, (g % 2) * BANK:(g % 2 + 1) * BANK] for g in range(G)]
                        for g in range(G):
                            vcol = P * c + D * g if layer == 0 else D * g
                            pe.matmul(PS[D * g:D * g + D, 6, :], V[:, kt, vcol:vcol + D], probs[g],
                                      start=kt == 0, stop=kt == NT - 1)
                        for g in range(G):
                            last = pe.matmul(PS[D * g:D * g + D, 7, :], ones[:, 0:D], probs[g],
                                             start=kt == 0, stop=kt == NT - 1)
                        last.then_inc(pv_done, 1)

                    units = HALF * NT
                    scores(0)
                    for unit in range(units):
                        if unit + 1 < units:
                            scores(unit + 1)
                        weighted(unit)
                pe.wait_ge(norm_done, 2 * KC * (layer + 1))
                pe.wait_ge(exp_done, 32 * KC * (layer + 1))
                for t in range(NT):
                    if t >= 6:
                        pe.wait_ge(proj_dve, NT * layer + t - 5)
                    for kc in range(KC):
                        last = pe.matmul(PS[:, t % 6, 0:C], attT[:, kc, t * P:(t + 1) * P], Wproj[:, kc, :],
                                         start=kc == 0, stop=kc == KC - 1)
                    last.then_inc(proj_psum, 1)
                if stop_after == 2 * layer + 1:
                    return
                pe.wait_ge(proj_dve, NT * (layer + 1))

                m = moes[layer]
                transposes(2 * layer + 1)
                pe.wait_ge(const_in, 16 * 4)
                for t in range(NT):
                    for kc in range(KC):
                        last = pe.matmul(PS[:, 6, t * E:(t + 1) * E], XnT[:, kc, t * P:(t + 1) * P], router_w[:, layer, kc, :],
                                         start=kc == 0, stop=kc == KC - 1)
                last.then_inc(route_psum, 1)
                pe.wait_ge(picked_ready, layer + 1)
                pk = picked[:, :, :].rearrange("p t e -> p (t e)")
                pe.matmul(PS[:, 7, 0:NT * E], before[:, :], pk, start=True, stop=True)
                pe.matmul(PS[:, 7, NT * E:2 * NT * E], ones[:, :], pk, start=True, stop=True).then_inc(rank_psum, 1)
                pe.wait_ge(tables_ready, layer + 1)

                o = m.blocks_before
                WIN_LOAD = 16 * (3 if m.shared else 4)
                w_before = 0 if layer == 0 else 64 * E
                xb_before = 16 * o

                def transpose_x(b, par):
                    pe.wait_ge(xb_in[par], b * 8 + (16 + 16 * ((o + 1 - par) // 2) - 8 * par))
                    if not (isinstance(b, int) and b == 0):
                        pe.wait_ge(bT_act, b + o)
                    for kc in range(KC):
                        last = pe.transpose(PS[:, 6, kc * P:(kc + 1) * P], xb[:, par, kc * P:(kc + 1) * P], ident[:, :])
                    last.then_inc(bT_psum, 1)

                def gate_up(b, par):
                    q = pe.value_load(ord_i[layer][0:1, bass.ds(b, 1)], min_val=0, max_val=m.ordinals - 1)
                    pe.wait_ge(bT_act, b + (o + 1))
                    pe.wait_ge(w_in, (q + 1) * WIN_LOAD + w_before)
                    s = q % 2
                    width = 2 * m.I
                    for lo in range(0, width, BANK):
                        n = min(BANK, width - lo)
                        for kc in range(KC):
                            last = pe.matmul(PS[:, 3 * par + lo // BANK, 0:n], xbT[:, par, kc, :],
                                             Wgu[layer][:, bass.ds(s, 1), kc, lo:lo + n],
                                             start=kc == 0, stop=kc == KC - 1)
                    last.then_inc(gu_psum, 1)

                def transpose_h(b, par):
                    pe.wait_ge(hid_done, b + (o + 1))
                    for i in range(m.IC):
                        last = pe.transpose(PS[:, 3 * par + i // 3, (i % 3) * P:(i % 3 + 1) * P],
                                            hid[:, par, i * P:(i + 1) * P], ident[:, :])
                    last.then_inc(hT_psum, 1)

                def down(b, par):
                    per = 2 if m.shared else 1
                    q = pe.value_load(ord_i[layer][0:1, bass.ds(b, 1)], min_val=0, max_val=m.ordinals - 1)
                    pe.wait_ge(hT_copied, b * per + (per + (moes[0].blocks if m.shared else 0)))
                    if not (isinstance(b, int) and b == 0):
                        pe.wait_ge(y_dve, b + o)
                    s = q % 2
                    for i in range(m.IC):
                        last = pe.matmul(PS[:, 7, 0:C], hidT[:, par, i, :], Wd[layer][:, bass.ds(s, 1), i, :],
                                         start=i == 0, stop=i == m.IC - 1)
                    last.then_inc(y_psum, 1)

                def step(b, par, more):
                    if more >= 1:
                        gate_up(b + 1, 1 - par)
                    transpose_h(b, par)
                    if more >= 2:
                        transpose_x(b + 2, par)
                    down(b, par)

                transpose_x(0, 0)
                gate_up(0, 0)
                transpose_x(1, 1)
                for b in range(2):
                    step(b, b, 2)
                with pe.Fori(0, (m.blocks - 5) // 2) as i:
                    step(i * 2 + 2, 0, 2)
                    step(i * 2 + 3, 1, 2)
                for b in range(m.blocks - 3, m.blocks):
                    step(b, b % 2, m.blocks - 1 - b)
                if stop_after == 2 * layer + 2:
                    return


_OUT = ((1, 32, 32, 384), "float32")


def kernel(**inputs):
    import numpy as np
    import concourse.bacc as bacc
    from concourse.bass_utils import run_bass_kernel_spmd as run

    a = {k: np.ascontiguousarray(v) for k, v in inputs.items()}
    arrays = {
        "x": a["x"].reshape(T, C),
        "qkv_w": a["L0_conv_qkv_w"], 
        "qk_b": np.ascontiguousarray(a["L0_conv_qkv_b"][:2 * C].reshape(2 * KC, P).T),
        "v_b": np.ascontiguousarray(a["L0_conv_qkv_b"][2 * C:]),
        "proj_w": a["L0_conv_proj_w"], "proj_b": a["L0_conv_proj_b"],
        "rel_both": np.ascontiguousarray(np.stack([a["L0_conv_rel_pos_h"].T, a["L0_conv_rel_pos_w"].T], 1)),
        "Wr0": a["L0_ffn_Wr"], "br0": a["L0_ffn_br"], "Wgu0": a["L0_ffn_Wgu"], "bgu0": a["L0_ffn_bgu"],
        "Wd0": a["L0_ffn_Wd"], "bd0": a["L0_ffn_bd"],
        "w_qkv1": np.ascontiguousarray(a["L1_conv_w_qkv"].T),
        "w_out1": np.ascontiguousarray(a["L1_conv_w_out"].T),
        "Wg_s": a["L1_ffn_Wg_s"][0], "Wu_s": a["L1_ffn_Wu_s"][0], "Wd_s": a["L1_ffn_Wd_s"][0],
        "Wg_r": a["L1_ffn_Wg_r"], "Wu_r": a["L1_ffn_Wu_r"], "Wd_r": a["L1_ffn_Wd_r"],
        "Wr1": a["L1_ffn_W_router"], "br1": a["L1_ffn_expert_bias"],
    }
    nc = bacc.Bacc("TRN2", target_bir_lowering=False, num_devices=1)
    args = {k: nc.dram_tensor(f"in_{k}", v.shape, mybir.dt.from_np(v.dtype), kind="ExternalInput").ap()
            for k, v in arrays.items()}
    out = nc.dram_tensor("out_0", (T, C), mybir.dt.from_np(np.dtype(_OUT[1])), kind="ExternalOutput").ap()
    build(nc, out=out, **args)
    r = run(nc, [{f"in_{k}": v for k, v in arrays.items()}], core_ids=[0])
    return r.results[0]["out_0"].reshape(_OUT[0])
```

```python
from contextlib import ExitStack

import concourse.bass as bass
from concourse import mybir

F32 = mybir.dt.float32
F32R = mybir.dt.float32r
I32 = mybir.dt.int32
U32 = mybir.dt.uint32
ACT = mybir.ActivationFunctionType
ALU = mybir.AluOpType
AX = mybir.AxisListType

P = 128
GRID = 32
T = GRID * GRID
NT = T // P
C = 384
KC = C // P
D = 32
G = P // D
QK_SCALE = D ** -0.5
REL_SCALE = D ** 0.5
BANK = 512
HALF = T // BANK
WIN = 7
MASKED = -float(2 ** 100)
E = 8
TOP = 2
ALPHA, LIMIT = 1.702, 7.0
ROUTED_BLOCKS = (TOP * T + E * (P - 1)) // P
REL = 2 * GRID - 1


class Steps:

    def __init__(self, eng, sem):
        self.eng, self.sem, self.n, self.off = eng, sem, 0, None

    def value(self):
        return self.n if self.off is None else self.off + self.n

    def wait(self, ins):
        self.n += 1
        ins.then_inc(self.sem, 1)
        self.eng.wait_ge(self.sem, self.value())

    def enter(self, turn, per_turn):
        self.first, self.per = self.n, per_turn
        self.off = turn * per_turn

    def leave(self, turns):
        assert self.n - self.first == self.per
        self.off = None
        self.n = self.first + self.per * turns


class Moe:

    def __init__(self, layer, inner, shared):
        self.layer, self.I, self.shared = layer, inner, shared
        self.IC = inner // P
        self.ordinals = E + shared
        self.first_routed = NT * shared
        self.blocks = self.first_routed + ROUTED_BLOCKS
        self.loads = 2 if shared else 4
        self.blocks_before = 0
        self.loads_before = 0


def build(nc, x, qkv_w, qk_b, v_b, proj_w, proj_b, rel_both, Wr0, br0, Wgu0, bgu0, Wd0, bd0,
          w_qkv1, w_out1, Wg_s, Wu_s, Wd_s, Wg_r, Wu_r, Wd_r, Wr1, br1, out, stop_after=4):
    ctx = ExitStack()
    base = [nc.sbuf_base + (-nc.sbuf_base) % 64]
    top = [0]

    def sb(name, shape, dt=F32):
        size = 2 if dt == mybir.dt.bfloat16 else 4
        for n in shape[1:]:
            size *= n
        t = nc.alloc_sbuf_tensor_at(name, shape, dt, offset=base[0])
        base[0] += size + (-size) % 64
        top[0] = max(top[0], base[0])
        return t

    moes = [Moe(0, 384, 0), Moe(1, 768, 1)]
    moes[1].blocks_before = moes[0].blocks
    moes[1].loads_before = moes[0].loads * moes[0].ordinals

    with ctx:
        def sem(name):
            return ctx.enter_context(nc.semaphore(name))

        X = sb("X", [P, NT, C])
        Xn = sb("Xn", [P, NT, C])
        expS = nc.alloc_sbuf_tensor_at("expS", [P, 4, 2 * BANK], F32, offset=base[0] - 4 * NT * C)
        xn_end = base[0]
        base[0] += 4 * (4 * 2 * BANK - NT * C)
        XnT = sb("XnT", [P, KC, T])
        ident = sb("ident", [P, P])
        before = sb("before", [P, P])
        ones = sb("ones", [P, P])
        stats = sb("stats", [P, NT, 6])
        mv = sb("mv", [P, NT, 2])
        var_eps = sb("var_eps", [P, NT])
        std = sb("std", [P, NT])
        rstd = sb("rstd", [P, NT])
        router_w = sb("router_w", [P, 2, KC, E])
        router_b = sb("router_b", [P, 2, E])
        iota_e = sb("iota_e", [P, E])
        iota_blk = sb("iota_blk", [P, 32])
        thresholds = sb("thresholds", [P, 8])
        logits = sb("logits", [P, NT, E])
        top8 = sb("top8", [P, NT, 8])
        top8i = sb("top8i", [P, NT, 8], U32)
        top_f = sb("top_f", [P, NT, 2])
        gap = sb("gap", [P, NT])
        weight = sb("weight", [P, 2, NT])
        chosen = sb("chosen", [P, 2, NT, E])
        picked = sb("picked", [P, NT, E])
        tile_cum = [sb(f"tile_cum{i}", [P, NT, E]) for i in range(4)]
        blk_cum = [sb(f"blk_cum{i}", [P, E]) for i in range(4)]
        over = sb("over", [P, E, 8])
        n_blk = sb("n_blk", [P, E])
        start_row = sb("start_row", [P, E])
        place = sb("place", [P, NT, E])
        place_k = sb("place_k", [P, 2, NT, E])
        row_f = sb("row_f", [P, 2, NT])
        row_i = sb("row_i", [P, 2, NT], I32)
        blk_ge = sb("blk_ge", [P, 32, E])
        ord_f = sb("ord_f", [P, 32])
        end_f = sb("end_f", [P, 16])
        ord_i = [sb(f"ord_i{n}", [P, 32], I32) for n in range(2)]
        end_i = [sb(f"end_i{n}", [P, 16], I32) for n in range(2)]
        shared_base = base[0]

        Wproj = sb("Wproj", [P, KC, C])
        qk_bias = sb("qk_bias", [P, 2 * KC])
        v_bias = sb("v_bias", [P, C])
        p_bias = sb("p_bias", [P, C])
        relh_bd = sb("relh_bd", [P, REL, G])
        relw_bd = sb("relw_bd", [P, REL, G])
        rel_t = sb("rel_t", [P, 2, REL])
        V = sb("V", [P, NT, C])
        nmax = sb("nmax", [P, KC, G * NT])
        recip = sb("recip", [P, BANK])
        attT = XnT
        parts_base = base[0]
        QA = sb("QA", [P, 2, G, T], F32R)
        KA = sb("KA", [P, 2, G, T], F32R)
        QKB = sb("QKB", [P, 2, 2, G, T], F32R)
        assert base[0] <= nc.sbuf_usable_end, base[0]
        part = {}
        for n, name in enumerate(("q_hi", "q_lo", "k_hi", "k_lo", "rh_hi", "rh_lo", "rw_hi", "rw_lo")):
            part[name] = nc.alloc_sbuf_tensor_at(f"part_{name}", [P, KC, T], F32R, offset=parts_base + n * 4 * KC * T)
        spare = parts_base + 4 * (2 * 2 * G * T + 2 * G * T)
        q32 = nc.alloc_sbuf_tensor_at("q32", [P, KC, T], F32, offset=spare)
        key_const = nc.alloc_sbuf_tensor_at("key_const", [P, T], F32, offset=spare + 4 * KC * T)
        Wqkv = nc.alloc_sbuf_tensor_at("Wqkv", [P, KC, 3 * C], F32, offset=spare + 4 * G * T)
        mask_const = nc.alloc_sbuf_tensor_at("mask_const", [P, T], F32, offset=xn_end)

        base[0] = shared_base
        Wgu, Wd, bgu, bd = [], [], [], []
        for m in moes:
            base[0] = shared_base
            Wgu.append(sb(f"Wgu{m.layer}", [P, 2, KC, 2 * m.I]))
            Wd.append(sb(f"Wd{m.layer}", [P, 2, m.IC, C]))
            if not m.shared:
                bgu.append(sb("bgu", [P, 2, 2 * m.I]))
                bd.append(sb("bd", [P, 2, C]))
            else:
                bgu.append(None)
                bd.append(None)
        base[0] = max(base[0], shared_base + 4 * (2 * KC * 2 * 768 + 2 * 6 * C))
        xb = sb("xb", [P, 2, C])
        xbT = sb("xbT", [P, 2, KC, P])
        gated = sb("gated", [P, 2, 768])
        pre = sb("pre", [P, 2, 768])
        hid = sb("hid", [P, 2, 768])
        hidT = sb("hidT", [P, 2, 6, P])
        yb = sb("yb", [P, 2, C])
        got = sb("got", [P, 2, 3, C])
        zero = sb("zero", [P, C])
        assert top[0] <= nc.sbuf_usable_end, (top[0], nc.sbuf_usable_end)

        PS = ctx.enter_context(nc.psum_tensor("PS", [P, 8, BANK], F32))
        xs = nc.dram_tensor("block_rows_in", [(NT + ROUTED_BLOCKS) * P, C], F32, kind="Internal").ap()
        ys = nc.dram_tensor("block_rows_out", [(NT + ROUTED_BLOCKS) * P, C], F32, kind="Internal").ap()

        key_rows = nc.dram_tensor("key_rows", [P, T], F32, kind="Internal").ap()
        zero_rows = nc.dram_tensor("zero_rows", [2 * D, T], F32, kind="Internal").ap()
        mask_rows = nc.dram_tensor("mask_rows", [P, T], F32, kind="Internal").ap()

        part_rows = {name: nc.dram_tensor(f"rows_{name}", [KC, P, T], F32, kind="Internal").ap() for name in part}

        x_in = sem("x_in")
        const_in = sem("const_in")
        pool_const = sem("pool_const")
        rel_in = sem("rel_in")
        rel_ready = sem("rel_ready")
        const_stored = sem("const_stored")
        wqkv_in = [sem("wqkv0_in"), sem("wqkv1_in")]
        dve_step = sem("dve_step")
        pool_step = sem("pool_step")
        var_ready = sem("var_ready")
        std_ready = sem("std_ready")
        xn_ready = sem("xn_ready")
        xT_psum = sem("xT_psum")
        xT_act = sem("xT_act")
        xT_dve = sem("xT_dve")
        job_psum = sem("job_psum")
        job_act = sem("job_act")
        job_dve = sem("job_dve")
        hi_act = sem("hi_act")
        q_split = sem("q_split")
        parts_stored = sem("parts_stored")
        a_in = [sem("a_in0"), sem("a_in1")]
        b_in = [sem("b_in0"), sem("b_in1")]
        max_psum = sem("max_psum")
        max_done = sem("max_done")
        nmax_psum = sem("nmax_psum")
        nmax_act = sem("nmax_act")
        score_psum = sem("score_psum")
        exp_done = sem("exp_done")
        pv_done = sem("pv_done")
        norm_done = sem("norm_done")
        proj_psum = sem("proj_psum")
        proj_dve = sem("proj_dve")
        xs_zeroed = sem("xs_zeroed")
        zero_ready = sem("zero_ready")
        route_psum = sem("route_psum")
        gap_ready = sem("gap_ready")
        exp_gap = sem("exp_gap")
        picked_ready = sem("picked_ready")
        rank_psum = sem("rank_psum")
        rows_ready = sem("rows_ready")
        tables_ready = sem("tables_ready")
        scattered = sem("scattered")
        shared_rows = sem("shared_rows")
        w_in = sem("w_in")
        xb_in = [sem("xb_in0"), sem("xb_in1")]
        bT_psum = sem("bT_psum")
        bT_act = sem("bT_act")
        gu_psum = sem("gu_psum")
        gate_act = sem("gate_act")
        pre_dve = sem("pre_dve")
        hid_done = sem("hid_done")
        hT_psum = sem("hT_psum")
        hT_copied = sem("hT_copied")
        y_psum = sem("y_psum")
        y_dve = sem("y_dve")
        y_stored = [sem("y_stored0"), sem("y_stored1")]
        got_in = [sem("got_in0"), sem("got_in1")]
        added = sem("added")
        out_done = sem("out_done")

        block = ctx.enter_context(nc.Block())

        A_DMAS = [[28, 28, 24], [24, 12, 8]]
        B_DMAS = [[20, 20, 16], [16, 8, 4]]

        def placed(dmas, layer, c):
            return 16 * sum(dmas[la][ch] for la in range(2) for ch in range(KC)
                            if (la, ch) <= (layer, c) and ch % 2 == c % 2)

        HI_JOBS = 16 + KC * HALF
        JOBS = [2 * KC * HALF + NT + 16, (KC + 1) * HALF + NT]

        def jobs(layer):
            q = [("q", c, h) for c in range(KC) for h in range(HALF)]
            k = [("k", c, h) for c in range(KC if layer == 0 else 1) for h in range(HALF)]
            v = [("v", t, 0) for t in range(NT)]
            rel = [("relh", n, 0) for n in range(8)] + [("relw", n, 0) for n in range(8)]
            every = q + (rel if layer == 0 else []) + k + v
            assert len(every) == JOBS[layer]
            return every

        def by_act(kind):
            return kind == "q"

        def units(layer):
            out = []
            for half in range(HALF):
                for kt in range(NT):
                    lo, hi = (0, NT - 1) if layer == 0 else (kt - 1, kt + 1)
                    lo, hi = max(lo, 4 * half), min(hi, 4 * half + 3)
                    if lo <= hi:
                        out.append((half, kt, (lo - 4 * half) * P, (hi + 1 - 4 * half) * P))
            return out

        def rel_views(kind, half, a, bank):
            src = PS[:, bank, 0:4 * KC * GRID].rearrange("p (r c n) -> p c r n", r=4, c=KC)
            if kind == "relh":
                return part[f"rh_{half}"][:, :, a * P:(a + 1) * P].rearrange("p c (r n) -> p c r n", r=4), src
            return part[f"rw_{half}"][:, :, :].rearrange("p c (n r) -> p c r n", r=GRID)[:, :, 4 * a:4 * a + 4, :], src

        U = [len(units(0)), len(units(1))]
        PV_BEFORE = [0, KC * U[0]]
        TILES = G * NT

        def keys_of(layer, qt):
            return (0, T) if layer == 0 else (max(qt - 1, 0) * P, min(qt + 2, NT) * P)

        def tiles_at(layer, u):
            return range(TILES * u // U[layer], TILES * (u + 1) // U[layer])

        for layer in range(2):
            assert tiles_at(layer, U[layer] // 2)[0] == TILES // 2

        def evacuated(eng, layer, n):
            done = jobs(0) if layer else []
            mine = done + jobs(layer)[:n + 1]
            kind = jobs(layer)[n][0]
            count = sum(by_act(j[0]) == by_act(kind) for j in mine)
            eng.wait_ge(job_act if by_act(kind) else job_dve, count)

        def flat(bank, banks):
            return PS[:, bank:bank + banks, :].rearrange("p b n -> p (b n)")

        @block.sync
        def _(sp):
            x_view = x.rearrange("(t p) c -> p t c", p=P)
            for t in range(NT):
                sp.dma_start(X[:, t, :], x_view[:, t, :]).then_inc(x_in, 16)
            sp.dma_start(router_w[:, 0], Wr0.rearrange("(k p) e -> p k e", p=P)).then_inc(const_in, 16)
            sp.dma_start(router_w[:, 1], Wr1.rearrange("(k p) e -> p k e", p=P)).then_inc(const_in, 16)
            sp.dma_start(router_b[:, 0], br0.partition_broadcast(P)).then_inc(const_in, 16)
            sp.dma_start(router_b[:, 1], br1.partition_broadcast(P)).then_inc(const_in, 16)

            for layer in range(2):
                if layer == 0:
                    sp.dma_start(Wqkv[:, :, :], qkv_w.rearrange("(k p) n -> p k n", p=P)).then_inc(wqkv_in[0], 16)
                    sp.dma_start(qk_bias[:, :], qk_b).then_inc(wqkv_in[0], 16)
                    sp.dma_start(v_bias[:, :], v_b.partition_broadcast(P)).then_inc(wqkv_in[0], 16)
                    sp.dma_start(p_bias[:, :], proj_b.partition_broadcast(P)).then_inc(wqkv_in[0], 16)
                    sp.dma_start(Wproj[:, :, :], proj_w.rearrange("(k p) n -> p k n", p=P)).then_inc(wqkv_in[0], 16)
                    for g in range(G):
                        sp.dma_start(rel_t[D * g:D * g + D], rel_both).then_inc(rel_in, 16)
                else:
                    sp.wait_ge(y_psum, moes[0].blocks)
                    sp.wait_ge(added, 8)
                    sp.dma_start(Wqkv[:, :, 0:C + 2 * P], w_qkv1.rearrange("(k p) n -> p k n", p=P)).then_inc(wqkv_in[1], 16)
                    sp.dma_start(Wproj[:, :, :], w_out1.rearrange("(k p) n -> p k n", p=P)).then_inc(wqkv_in[1], 16)
                if layer == 0:
                    sp.wait_ge(pool_const, 2)
                    sp.dma_start(key_rows[D:P, :], key_const[D:P, :]).then_inc(const_stored, 16)
                    sp.dma_start(mask_rows[D:3 * D, :], mask_const[D:3 * D, :]).then_inc(const_stored, 16)
                    for n in range(2):
                        sp.dma_start(zero_rows[D * n:D * n + D, :], mask_const[0:D, :]).then_inc(const_stored, 16)
                    sp.wait_ge(const_stored, 16 * 4)
                chunks = {"q": KC, "rh": KC, "rw": KC, "k": KC if layer == 0 else 1}
                sp.wait_ge(q_split, KC * (layer + 1))
                kinds = [j[0] for j in jobs(layer)]
                for name, kind in (("q", None), ("rh", "relh"), ("rw", "relw"), ("k", "k")):
                    if kind and kind not in kinds:
                        continue
                    if kind:
                        evacuated(sp, layer, len(kinds) - 1 - kinds[::-1].index(kind))
                    n = chunks[name]
                    for half in ("hi", "lo"):
                        sp.dma_start(part_rows[f"{name}_{half}"][0:n].rearrange("c p t -> p c t"),
                                     part[f"{name}_{half}"][:, 0:n, :].bitcast(F32)).then_inc(parts_stored, 16)
                sp.wait_ge(parts_stored, 16 * (8 if layer == 0 else 12))

                def place(dst, src, done):
                    sp.dma_start(dst.bitcast(F32), src).then_inc(done, 16)

                def head(name, c, g):
                    rows = slice(D * g, D * g + D) if name[0] in "qk" else slice(g, P, G)
                    return part_rows[name][c, rows, :]

                def place_a(c):
                    s, done, n = c % 2, a_in[c % 2], 0
                    for g in range(G):
                        todo = [(QA[0:D, s, g, :], head("q_hi", c, g)), (QA[3 * D:P, s, g, :], head("q_lo", c, g))]
                        if layer == 0:
                            todo += [(QA[D:2 * D, s, g, :], head("rh_hi", c, g)), (QA[2 * D:3 * D, s, g, :], head("rw_hi", c, g))]
                        elif c < 2:
                            todo += [(QA[D:3 * D, s, g, :], mask_rows[D:3 * D, :])]
                        if layer == 0 or c == 0:
                            todo += [(KA[0:D, s, g, :], head("k_hi", c, g)), (KA[3 * D:P, s, g, :], head("k_hi", c, g))]
                            if c < 2:
                                todo += [(KA[D:3 * D, s, g, :], key_rows[D:3 * D, :])]
                        for dst, src in todo:
                            place(dst, src, done)
                        n += len(todo)
                    assert n == A_DMAS[layer][c], n

                def place_b(c):
                    s, done, n = c % 2, b_in[c % 2], 0
                    for g in range(G):
                        todo = [(QKB[0:D, s, 0, g, :], head("q_hi", c, g))]
                        if layer == 0:
                            todo += [(QKB[D:2 * D, s, 0, g, :], head("rh_lo", c, g)), (QKB[2 * D:3 * D, s, 0, g, :], head("rw_lo", c, g))]
                        if layer == 0 or c == 0:
                            todo += [(QKB[0:D, s, 1, g, :], head("k_lo", c, g))]
                            if c < 2:
                                todo += [(QKB[D:P, s, 1, g, :], key_rows[D:P, :])]
                        if layer == 1 and c < 2:
                            todo += [(QKB[D:3 * D, s, 0, g, :], zero_rows)]
                        for dst, src in todo:
                            place(dst, src, done)
                        n += len(todo)
                    assert n == B_DMAS[layer][c], n

                place_a(0)
                place_b(0)
                place_a(1)
                sp.wait_ge(job_psum, JOBS[0] if layer == 0 else JOBS[0] + JOBS[1])
                place_b(1)
                sp.wait_ge(pv_done, PV_BEFORE[layer] + U[layer])
                place_a(2)
                place_b(2)

                if stop_after == 2 * layer + 1:
                    break
                m = moes[layer]
                if layer == 0:
                    sp.wait_ge(zero_ready, 1)
                    sp.dma_start(xs.rearrange("(b p) c -> p b c", p=P),
                                 zero[:, :].rearrange("p (a c) -> p a c", a=1).broadcast_to([P, NT + ROUTED_BLOCKS, C])
                                 ).then_inc(xs_zeroed, 16)
                    sp.wait_ge(xs_zeroed, 16)
                if m.shared:
                    sp.wait_ge(xn_ready, NT * 4)
                    sp.dma_start(xs[0:T, :].rearrange("(t p) c -> p t c", p=P), Xn[:, :, :]).then_inc(shared_rows, 16)
                    sp.wait_ge(shared_rows, 16)

                def load(b):
                    sp.dma_start(xb[:, b % 2, :], xs[bass.ds(b * P, P), :]).then_inc(xb_in[b % 2], 16)

                def load_waiting(b, par):
                    sp.wait_ge(bT_psum, m.blocks_before + b - 1)
                    sp.dma_start(xb[:, par, :], xs[bass.ds(b * P, P), :]).then_inc(xb_in[par], 16)

                def store(b, par):
                    sp.wait_ge(y_dve, m.blocks_before + b + 1)
                    sp.dma_start(ys[bass.ds(b * P, P), :], yb[:, par, :]).then_inc(y_stored[par], 16)

                if not m.shared:
                    sp.wait_ge(scattered, 16 * 2 * NT)
                load(0)
                load(1)
                turns = (m.blocks - 5) // 2
                assert m.blocks % 2 == 1

                def step(b, par, more=True):
                    if more:
                        load_waiting(b + 2, par)
                    store(b, par)

                def steps(lo, hi):
                    for b in range(lo, hi):
                        step(b, b % 2, b + 2 < m.blocks)

                if m.shared:
                    steps(0, 6)
                    sp.wait_ge(scattered, 16 * 2 * NT * 2)
                    first = 6
                else:
                    steps(0, 2)
                    first = 2
                last = m.blocks - 3
                with sp.Fori(0, (last - first) // 2) as i:
                    step(i * 2 + first, 0)
                    step(i * 2 + first + 1, 1)
                steps(last, m.blocks)
                if stop_after == 2 * layer + 2:
                    break
            if stop_after in (1, 3):
                sp.wait_ge(proj_dve, 8 * (1 if stop_after == 1 else 2))
            else:
                sp.wait_ge(added, NT * stop_after // 2)
            sp.dma_start(out.rearrange("(t p) c -> p t c", p=P), X[:, :, :]).then_inc(out_done, 16)
            sp.wait_ge(out_done, 16)

        @block.gpsimd
        def _(pool):
            st = Steps(pool, pool_step)
            st.wait(pool.memset(relh_bd[:, :, :], 0.0))
            st.wait(pool.memset(relw_bd[:, :, :], 0.0))
            st.wait(pool.memset(ident[:, :], 0.0))
            st.wait(pool.affine_select(out=ident[:, :], in_=ident[:, :], compare_op=ALU.not_equal, fill=1.0,
                                       base=0, pattern=[[-1, P]], channel_multiplier=1))
            st.wait(pool.memset(ones[:, :], 1.0))
            st.wait(pool.affine_select(out=before[:, :], in_=ones[:, :], compare_op=ALU.is_gt, fill=0.0,
                                       base=0, pattern=[[1, P]], channel_multiplier=-1))
            st.wait(pool.iota(iota_e[:, :], pattern=[[1, E]], base=0, channel_multiplier=0,
                              allow_small_or_imprecise_dtypes=True))
            st.wait(pool.iota(iota_blk[:, :], pattern=[[1, 32]], base=0, channel_multiplier=0,
                              allow_small_or_imprecise_dtypes=True))
            st.wait(pool.iota(thresholds[:, :], pattern=[[P, 8]], base=0, channel_multiplier=0,
                              allow_small_or_imprecise_dtypes=True))
            st.wait(pool.memset(thresholds[:, 0:1], -1.0))
            pool.sem_inc(pool_const, 1)
            kc = key_const[:, :].rearrange("p (h w) -> p h w", w=GRID)
            st.wait(pool.memset(key_const[:, :], 0.0))
            st.wait(pool.affine_select(out=kc[D:2 * D], in_=kc[D:2 * D], compare_op=ALU.not_equal, fill=1.0,
                                       base=-(GRID - 1), pattern=[[1, GRID], [0, GRID]], channel_multiplier=1))
            st.wait(pool.affine_select(out=kc[2 * D:3 * D], in_=kc[2 * D:3 * D], compare_op=ALU.not_equal, fill=1.0,
                                       base=-(GRID - 1), pattern=[[0, GRID], [1, GRID]], channel_multiplier=1))
            st.wait(pool.memset(key_const[3 * D:3 * D + 1, :], 1.0))
            st.wait(pool.memset(mask_const[:, :], 0.0))
            mc = mask_const[:, :].rearrange("p (h w) -> p h w", w=GRID)
            for lo, hi, start, slope in ((0, 3, 0, 0), (3, 28, 0, 1), (28, 32, 25, 0)):
                n = hi - lo
                for rows, by_row in ((slice(D, 2 * D), True), (slice(2 * D, 3 * D), False)):
                    view = mc[rows, lo:hi, :] if by_row else mc[rows, :, lo:hi]
                    pat = (lambda s: [[s, n], [0, GRID]]) if by_row else (lambda s: [[0, GRID], [s, n]])
                    st.wait(pool.affine_select(out=view, in_=view, compare_op=ALU.is_ge, fill=MASKED,
                                               base=GRID - 1 - start, pattern=pat(-slope), channel_multiplier=-1))
                    st.wait(pool.affine_select(out=view, in_=view, compare_op=ALU.is_ge, fill=MASKED,
                                               base=start + WIN - 1 - (GRID - 1), pattern=pat(slope),
                                               channel_multiplier=1))
            pool.sem_inc(pool_const, 1)
            pool.wait_ge(rel_in, 16 * G)
            for g in range(G):
                rows = slice(D * g, D * g + D)
                st.wait(pool.tensor_scalar(relh_bd[rows, :, g], rel_t[rows, 0, :], REL_SCALE, None, ALU.mult))
                st.wait(pool.tensor_scalar(relw_bd[rows, :, g], rel_t[rows, 1, :], REL_SCALE, None, ALU.mult))
            pool.sem_inc(rel_ready, 1)

            for layer in range(2):
                if stop_after <= 2 * layer + 1:
                    break
                m = moes[layer]
                pool.wait_ge(proj_psum, NT * (layer + 1))
                if layer == 0:
                    pool.memset(zero[:, :], 0.0).then_inc(zero_ready, 1)

                def load_weights(gate_up, down, slot):
                    for n, src in enumerate(gate_up):
                        width = 2 * m.I // len(gate_up)
                        pool.dma_start(Wgu[layer][:, slot, :, n * width:(n + 1) * width],
                                       src.rearrange("(k p) n -> p k n", p=P)).then_inc(w_in, 16)
                    pool.dma_start(Wd[layer][:, slot], down.rearrange("(k p) n -> p k n", p=P)).then_inc(w_in, 16)

                WIN_LOAD = 16 * (3 if m.shared else 4)
                w_before = 0 if layer == 0 else 16 * 4 * E

                def expert(e, slot):
                    if m.shared:
                        load_weights([Wg_r[bass.ds(e, 1)].rearrange("a k n -> (a k) n"),
                                      Wu_r[bass.ds(e, 1)].rearrange("a k n -> (a k) n")],
                                     Wd_r[bass.ds(e, 1)].rearrange("a k n -> (a k) n"), slot)
                    else:
                        load_weights([Wgu0[bass.ds(e, 1)].rearrange("a k n -> (a k) n")],
                                     Wd0[bass.ds(e, 1)].rearrange("a k n -> (a k) n"), slot)
                        pool.dma_start(bgu[0][:, slot, :], bgu0[bass.ds(e, 1)].rearrange("a n -> (a n)").partition_broadcast(P)).then_inc(w_in, 16)
                        pool.dma_start(bd[0][:, slot, :], bd0[bass.ds(e, 1)].rearrange("a n -> (a n)").partition_broadcast(P)).then_inc(w_in, 16)

                if m.shared:
                    load_weights([Wg_s, Wu_s], Wd_s, 0)
                    pool.wait_ge(w_in, w_before + WIN_LOAD)
                    expert(0, 1)
                else:
                    expert(0, 0)
                    pool.wait_ge(w_in, w_before + WIN_LOAD)
                    expert(1, 1)
                pool.wait_ge(rows_ready, layer + 1)
                if layer == 0:
                    pool.wait_ge(xs_zeroed, 16)
                for k in range(TOP):
                    for t in range(NT):
                        pool.indirect_dma_start(
                            xs[:, :], bass.IndirectOffsetOnAxis(ap=row_i[:, k, t:t + 1], axis=0),
                            Xn[:, t, :], None).then_inc(scattered, 16)
                pool.wait_ge(tables_ready, layer + 1)
                with pool.Fori(2, m.ordinals) as q:
                    done = pool.value_load(end_i[layer][0:1, bass.ds(q, 1)], min_val=1, max_val=m.blocks)
                    pool.wait_ge(w_in, (q * WIN_LOAD + w_before))
                    pool.wait_ge(y_dve, done + m.blocks_before)
                    expert(q - m.shared, q % 2)
                for par in range(2):
                    pool.wait_ge(y_stored[par], 16 * sum((mm.blocks + 1 - par) // 2 for mm in moes[:layer + 1]))
                for t in range(NT):
                    if t >= 2 or layer:
                        pool.wait_ge(added, NT * layer + t - 1 if t >= 2 else NT * layer)
                    for k in range(TOP):
                        pool.indirect_dma_start(
                            got[:, t % 2, k, :], None, ys[0:m.blocks * P, :],
                            bass.IndirectOffsetOnAxis(ap=row_i[:, k, t:t + 1], axis=0)).then_inc(got_in[t % 2], 16)
                    if m.shared:
                        pool.dma_start(got[:, t % 2, TOP, :], ys[t * P:(t + 1) * P, :]).then_inc(got_in[t % 2], 16)

        @block.scalar
        def _(act):
            def ln_and_transposes(n):
                act.wait_ge(var_ready, n + 1)
                act.activation(std[:, :], var_eps[:, :], ACT.Sqrt).then_inc(std_ready, 1)
                for j in range(0, 6, 2):
                    act.wait_ge(xT_psum, 6 * n + j + 1)
                    act.activation(XnT[:, j // 2, (j % 2) * BANK:(j % 2 + 1) * BANK], PS[:, j, :],
                                   ACT.Copy).then_inc(xT_act, 1)

            for layer in range(2):
                ln_and_transposes(2 * layer)
                act.wait_ge(wqkv_in[layer], 16 * (5 if layer == 0 else 2))
                for n, (kind, a, b) in enumerate(jobs(layer)):
                    if kind == "v":
                        continue
                    act.wait_ge(job_psum, JOBS[0] * layer + n + 1)
                    bank = n % 8
                    cols = slice(b * BANK, (b + 1) * BANK)
                    if kind == "q":
                        if layer == 0:
                            act.activation(q32[:, a, cols], PS[:, bank, :], ACT.Identity, bias=qk_bias[:, a:a + 1]).then_inc(job_act, 1)
                        else:
                            act.activation(q32[:, a, cols], PS[:, bank, :], ACT.Copy).then_inc(job_act, 1)
                        continue
                    if kind == "k":
                        if layer == 0:
                            act.activation(part["k_hi"][:, a, cols], PS[:, bank, :], ACT.Identity,
                                           bias=qk_bias[:, KC + a:KC + a + 1]).then_inc(hi_act, 1)
                        else:
                            act.activation(part["k_hi"][:, a, cols], PS[:, bank, :], ACT.Copy).then_inc(hi_act, 1)
                        continue
                    dst, src = rel_views(kind, "hi", a, bank)
                    act.activation(dst, src, ACT.Copy).then_inc(hi_act, 1)
                base = PV_BEFORE[layer]

                def chunk_exps(c, first):
                    n = c + KC * layer
                    act.wait_ge(nmax_psum, n + 1)
                    for g in range(G):
                        last = act.activation(QKB[3 * D:P, bass.ds(c % 2, 1), 0, g, :].rearrange("p a n -> p (a n)"),
                                              PS[D * g:D * g + D, 4:6, :].rearrange("p b n -> p (b n)"), ACT.Copy)
                    last.then_inc(nmax_act, 1)

                    def unit_exps(unit, par, lo, hi, skip):
                        for pair in range(2):
                            done = c * (2 * U[layer]) + unit * 2 + (2 * base + pair + 1)
                            act.wait_ge(score_psum, done)
                            if pair == 0 and not skip:
                                act.wait_ge(pv_done, c * U[layer] + unit + (base - 1))
                            act.activation(expS[:, 2 * par + pair, :].rearrange("p (b n) -> p b n", b=2)[:, :, lo:hi],
                                           PS[:, 2 * pair:2 * pair + 2, lo:hi], ACT.Exp, scale=QK_SCALE).then_inc(exp_done, 1)

                    if layer == 0:
                        if first:
                            unit_exps(0, 0, 0, BANK, True)
                            unit_exps(1, 1, 0, BANK, True)
                        with act.Fori(1 if first else 0, U[0] // 2) as i:
                            unit_exps(i * 2, 0, 0, BANK, False)
                            unit_exps(i * 2 + 1, 1, 0, BANK, False)
                    else:
                        for unit, (half, kt, lo, hi) in enumerate(units(1)):
                            unit_exps(unit, unit % 2, lo, hi, False)

                if layer == 0:
                    chunk_exps(0, True)
                with act.Fori(1 if layer == 0 else 0, KC) as c:
                    chunk_exps(c, False)
                if stop_after == 2 * layer + 1:
                    return
                m = moes[layer]
                ln_and_transposes(2 * layer + 1)
                act.wait_ge(gap_ready, layer + 1)
                act.activation(weight[:, 1, :], gap[:, :], ACT.Exp).then_inc(exp_gap, 1)
                o = m.blocks_before

                def copy_xT(b, par):
                    act.wait_ge(bT_psum, b + (o + 1))
                    if not (isinstance(b, int) and b < 2):
                        act.wait_ge(gu_psum, b + (o - 1))
                    act.activation(xbT[:, par].rearrange("p k n -> p (k n)"), PS[:, 6, 0:C], ACT.Copy).then_inc(bT_act, 1)

                def gate(b, par):
                    if m.shared:
                        act.wait_ge(gu_psum, b + (o + 1))
                        if not (isinstance(b, int) and b < 2):
                            act.wait_ge(hid_done, b + (o - 1))
                        act.activation(gated[:, par, 0:m.I], flat(3 * par, 3)[:, 0:m.I], ACT.Silu).then_inc(gate_act, 1)
                    else:
                        act.wait_ge(pre_dve, b + 1)
                        if not (isinstance(b, int) and b < 2):
                            act.wait_ge(hid_done, b - 1)
                        act.activation(gated[:, par, 0:m.I], pre[:, par, 0:m.I], ACT.Sigmoid, scale=ALPHA).then_inc(gate_act, 1)

                def copy_hT(b, par):
                    act.wait_ge(hT_psum, b + (o + 1))
                    if not (isinstance(b, int) and b < 2):
                        act.wait_ge(y_psum, b + (o - 1))
                    act.activation(hidT[:, par, 0:3].rearrange("p k n -> p (k n)"),
                                   PS[:, 3 * par, 0:3 * P], ACT.Copy).then_inc(hT_copied, 1)

                def step(b, par, more):
                    copy_hT(b, par)
                    if more >= 2:
                        copy_xT(b + 2, par)
                    if more >= 1:
                        gate(b + 1, 1 - par)

                copy_xT(0, 0)
                copy_xT(1, 1)
                gate(0, 0)
                for b in range(2):
                    step(b, b, 2)
                with act.Fori(0, (m.blocks - 5) // 2) as i:
                    step(i * 2 + 2, 0, 2)
                    step(i * 2 + 3, 1, 2)
                for b in range(m.blocks - 3, m.blocks):
                    step(b, b % 2, m.blocks - 1 - b)
                if stop_after == 2 * layer + 2:
                    return

        @block.vector
        def _(dve):
            st = Steps(dve, dve_step)

            def layernorm(n, eps):
                if n == 0:
                    dve.wait_ge(x_in, 16 * NT)
                for t in range(NT):
                    last = dve.bn_stats(stats[:, t, :], X[:, t, :])
                st.wait(last)
                for t in range(NT):
                    last = dve.bn_aggr(mv[:, t, :], stats[:, t, :])
                st.wait(last)
                dve.tensor_scalar(var_eps[:, :], mv[:, :, 1], eps, None, ALU.add).then_inc(var_ready, 1)
                dve.wait_ge(std_ready, n + 1)
                st.wait(dve.reciprocal(rstd[:, :], std[:, :]))
                for t in range(NT):
                    dve.tensor_scalar(Xn[:, t, :], X[:, t, :], mv[:, t, 0:1], rstd[:, t:t + 1],
                                      ALU.subtract, ALU.mult).then_inc(xn_ready, 1)
                for j in range(1, 6, 2):
                    dve.wait_ge(xT_psum, 6 * n + j + 1)
                    dve.tensor_copy(XnT[:, j // 2, (j % 2) * BANK:(j % 2 + 1) * BANK], PS[:, j, :]).then_inc(xT_dve, 1)

            for layer in range(2):
                layernorm(2 * layer, 1e-6)
                dve.wait_ge(wqkv_in[layer], 16 * (5 if layer == 0 else 2))
                if layer == 0:
                    st.wait(dve.tensor_tensor(X[:, :, :], X[:, :, :],
                                              p_bias[:, :].rearrange("p (a c) -> p a c", a=1).broadcast_to([P, NT, C]),
                                              ALU.add))
                rounded = 0
                for n, (kind, a, b) in enumerate(jobs(layer)):
                    bank = n % 8
                    cols = slice(b * BANK, (b + 1) * BANK)
                    if kind == "q":
                        if b == HALF - 1:
                            dve.wait_ge(job_act, HALF * (KC * layer + a + 1))
                            st.wait(dve.tensor_copy(part["q_hi"][:, a, :], q32[:, a, :]))
                            dve.tensor_tensor(part["q_lo"][:, a, :], q32[:, a, :], part["q_hi"][:, a, :].bitcast(F32),
                                              ALU.subtract).then_inc(q_split, 1)
                        continue
                    if kind == "v":
                        dve.wait_ge(job_psum, JOBS[0] * layer + n + 1)
                        if layer == 0:
                            dve.tensor_tensor(V[:, a, :], PS[:, bank, 0:C], v_bias[:, :], ALU.add).then_inc(job_dve, 1)
                        else:
                            dve.tensor_copy(V[:, a, 0:P], PS[:, bank, 0:P]).then_inc(job_dve, 1)
                        continue
                    rounded += 1
                    dve.wait_ge(hi_act, HI_JOBS * layer + rounded)
                    if kind == "k":
                        bias = qk_bias[:, KC + a:KC + a + 1] if layer == 0 else 0.0
                        dve.scalar_tensor_tensor(part["k_lo"][:, a, cols], PS[:, bank, :], bias,
                                                 part["k_hi"][:, a, cols].bitcast(F32), ALU.add,
                                                 ALU.subtract).then_inc(job_dve, 1)
                    else:
                        dst, src = rel_views(kind, "lo", a, bank)
                        hi, _ = rel_views(kind, "hi", a, bank)
                        dve.tensor_tensor(dst, src, hi.bitcast(F32), ALU.subtract).then_inc(job_dve, 1)
                def maxima(c, part):
                    with dve.Fori(0, TILES // 2 // NT) as i:
                        for qt in range(NT):
                            t = i * NT + (part * TILES // 2 + qt)
                            dve.wait_ge(max_psum, t + (TILES * (KC * layer + c) + 1))
                            lo, hi = keys_of(layer, qt)
                            if c == 0:
                                pair = (i * NT + (part * TILES // 2 + qt)) % 3
                                src = PS[:, bass.ds(pair * 2, 2), :] if layer == 0 else PS[:, bass.ds(pair * 2, 1), 0:hi - lo]
                            else:
                                src = PS[:, 4:6, :] if layer == 0 else PS[:, 4 + qt % 2, 0:hi - lo]
                            dve.tensor_reduce(nmax[:, c, bass.ds(t, 1)], src, axis=AX.X if layer and c else AX.XY,
                                              op=ALU.max, negate=True).then_inc(max_done, 1)

                maxima(0, 0)
                maxima(0, 1)
                for c in range(KC):
                    for half in range(HALF):
                        if c + 1 < KC:
                            maxima(c + 1, half)
                        dve.wait_ge(pv_done, PV_BEFORE[layer] + U[layer] * c + U[layer] // 2 * (half + 1))
                        st.wait(dve.reciprocal(recip[:, :], PS[:, 7, :]))
                        dve.tensor_tensor(attT[:, c, half * BANK:(half + 1) * BANK], PS[:, 6, :], recip[:, :],
                                          ALU.mult).then_inc(norm_done, 1)
                for t in range(NT):
                    dve.wait_ge(proj_psum, NT * layer + t + 1)
                    ins = dve.tensor_tensor(X[:, t, :], X[:, t, :], PS[:, t % 6, 0:C], ALU.add).then_inc(proj_dve, 1)
                dve.wait_ge(proj_dve, NT * (layer + 1))
                if stop_after == 2 * layer + 1:
                    return

                m = moes[layer]
                layernorm(2 * layer + 1, 1e-5)
                dve.wait_ge(const_in, 16 * 4)
                dve.wait_ge(pool_const, 2)
                dve.wait_ge(route_psum, layer + 1)
                st.wait(dve.tensor_tensor(logits[:, :, :], PS[:, 6, 0:NT * E].rearrange("p (t e) -> p t e", e=E),
                                          router_b[:, layer, :].rearrange("p (a e) -> p a e", a=1).broadcast_to([P, NT, E]), ALU.add))
                for t in range(NT):
                    last = dve.max(top8[:, t, :], logits[:, t, :])
                st.wait(last)
                for t in range(NT):
                    last = dve.max_index(top8i[:, t, :], top8[:, t, :], logits[:, t, :])
                st.wait(last)
                dve.tensor_tensor(gap[:, :], top8[:, :, 1], top8[:, :, 0], ALU.subtract).then_inc(gap_ready, 1)
                st.wait(dve.tensor_copy(top_f[:, :, :], top8i[:, :, 0:2]))
                for k in range(TOP):
                    last = dve.tensor_tensor(chosen[:, k],
                                             iota_e[:, :].rearrange("p (a e) -> p a e", a=1).broadcast_to([P, NT, E]),
                                             top_f[:, :, k:k + 1].broadcast_to([P, NT, E]), ALU.is_equal)
                st.wait(last)
                dve.tensor_tensor(picked[:, :, :], chosen[:, 0], chosen[:, 1], ALU.add).then_inc(picked_ready, 1)
                dve.wait_ge(exp_gap, layer + 1)
                st.wait(dve.tensor_scalar(weight[:, 0, :], weight[:, 1, :], 1.0, None, ALU.add))
                st.wait(dve.reciprocal(weight[:, 0, :], weight[:, 0, :]))
                st.wait(dve.tensor_tensor(weight[:, 1, :], weight[:, 1, :], weight[:, 0, :], ALU.mult))
                dve.wait_ge(rank_psum, layer + 1)
                rank = PS[:, 7, 0:NT * E].rearrange("p (t e) -> p t e", e=E)
                count = PS[:, 7, NT * E:2 * NT * E].rearrange("p (t e) -> p t e", e=E)
                st.wait(dve.tensor_copy(tile_cum[0][:, :, :], count))
                for r, shift in enumerate((1, 2, 4)):
                    src, dst = tile_cum[r], tile_cum[r + 1]
                    dve.tensor_copy(dst[:, 0:shift], src[:, 0:shift])
                    st.wait(dve.tensor_tensor(dst[:, shift:], src[:, shift:], src[:, :NT - shift], ALU.add))
                st.wait(dve.tensor_tensor(over[:, :, :], tile_cum[3][:, NT - 1, :].rearrange("p (e a) -> p e a", a=1).broadcast_to([P, E, 8]),
                                          thresholds[:, :].rearrange("p (a k) -> p a k", a=1).broadcast_to([P, E, 8]), ALU.is_gt))
                st.wait(dve.tensor_reduce(blk_cum[0][:, :], over[:, :, :], axis=AX.X, op=ALU.add))
                for r, shift in enumerate((1, 2, 4)):
                    src, dst = blk_cum[r], blk_cum[r + 1]
                    dve.tensor_copy(dst[:, 0:shift], src[:, 0:shift])
                    st.wait(dve.tensor_tensor(dst[:, shift:], src[:, shift:], src[:, :E - shift], ALU.add))
                st.wait(dve.tensor_tensor(start_row[:, :], blk_cum[3][:, :], blk_cum[0][:, :], ALU.subtract))
                st.wait(dve.tensor_scalar(start_row[:, :], start_row[:, :], float(m.first_routed), float(P), ALU.add, ALU.mult))
                st.wait(dve.tensor_tensor(place[:, :, :], tile_cum[3][:, :, :], tile_cum[0][:, :, :], ALU.subtract))
                st.wait(dve.tensor_tensor(place[:, :, :], place[:, :, :], rank, ALU.add))
                st.wait(dve.tensor_tensor(place[:, :, :], place[:, :, :],
                                          start_row[:, :].rearrange("p (a e) -> p a e", a=1).broadcast_to([P, NT, E]), ALU.add))
                for k in range(TOP):
                    last = dve.tensor_tensor(place_k[:, k], place[:, :, :], chosen[:, k], ALU.mult)
                st.wait(last)
                st.wait(dve.tensor_reduce(row_f[:, :, :], place_k[:, :, :, :], axis=AX.X, op=ALU.add))
                dve.tensor_copy(row_i[:, :, :], row_f[:, :, :]).then_inc(rows_ready, 1)
                nr = ROUTED_BLOCKS
                st.wait(dve.tensor_tensor(blk_ge[:, 0:nr], iota_blk[:, 0:nr].rearrange("p (b a) -> p b a", a=1).broadcast_to([P, nr, E]),
                                          blk_cum[3][:, :].rearrange("p (a e) -> p a e", a=1).broadcast_to([P, nr, E]), ALU.is_ge))
                if m.shared:
                    st.wait(dve.memset(ord_f[:, 0:NT], 0.0))
                    st.wait(dve.memset(end_f[:, 2:3], float(NT)))
                fr = m.first_routed
                st.wait(dve.tensor_reduce(ord_f[:, fr:fr + nr], blk_ge[:, 0:nr], axis=AX.X, op=ALU.add))
                st.wait(dve.tensor_scalar(ord_f[:, fr:fr + nr], ord_f[:, fr:fr + nr], float(E - 1), float(m.shared), ALU.min, ALU.add))
                st.wait(dve.tensor_scalar(end_f[:, 2 + m.shared:m.ordinals], blk_cum[3][:, 0:m.ordinals - 2 - m.shared], float(fr), None, ALU.add))
                st.wait(dve.tensor_copy(ord_i[layer][:, 0:m.blocks], ord_f[:, 0:m.blocks]))
                dve.tensor_copy(end_i[layer][:, 2:m.ordinals], end_f[:, 2:m.ordinals]).then_inc(tables_ready, 1)
                dve.wait_ge(tables_ready, layer + 1)

                o = m.blocks_before

                def copy_hT(b, par):
                    if not m.shared:
                        return
                    dve.wait_ge(hT_psum, b + (o + 1))
                    if not (isinstance(b, int) and b < 2):
                        dve.wait_ge(y_psum, b + (o - 1))
                    dve.tensor_copy(hidT[:, par, 3:6].rearrange("p k n -> p (k n)"),
                                    PS[:, 3 * par + 1, 0:3 * P]).then_inc(hT_copied, 1)

                def hidden(b, par):
                    I = m.I
                    if m.shared:
                        dve.wait_ge(gate_act, moes[0].blocks + b + 1)
                        if not (isinstance(b, int) and b < 2):
                            dve.wait_ge(hT_psum, b + (o - 1))
                        dve.tensor_tensor(hid[:, par, 0:I], gated[:, par, 0:I], flat(3 * par, 3)[:, I:2 * I],
                                          ALU.mult).then_inc(hid_done, 1)
                        return
                    q = dve.value_load(ord_i[layer][0:1, bass.ds(b, 1)], min_val=0, max_val=m.ordinals - 1)
                    dve.wait_ge(gu_psum, b + 1)
                    s = q % 2
                    dve.wait_ge(w_in, (q + 1) * 64)
                    st.wait(dve.tensor_tensor(pre[:, par, :], flat(3 * par, 2)[:, 0:2 * I],
                                              bgu[0][:, bass.ds(s, 1), :].rearrange("p a n -> p (a n)"), ALU.add))
                    st.wait(dve.tensor_scalar(pre[:, par, 0:I], pre[:, par, 0:I], LIMIT, None, ALU.min))
                    dve.tensor_scalar(pre[:, par, I:2 * I], pre[:, par, I:2 * I], LIMIT, -LIMIT, ALU.min, ALU.max).then_inc(pre_dve, 1)
                    dve.wait_ge(gate_act, b + 1)
                    if not (isinstance(b, int) and b < 2):
                        dve.wait_ge(hT_psum, b - 1)
                    st.wait(dve.tensor_tensor(gated[:, par, I:2 * I], gated[:, par, 0:I], pre[:, par, 0:I], ALU.mult))
                    dve.scalar_tensor_tensor(hid[:, par, 0:I], pre[:, par, I:2 * I], 1.0, gated[:, par, I:2 * I],
                                             ALU.add, ALU.mult).then_inc(hid_done, 1)

                def copy_y(b, par):
                    if not m.shared:
                        q = dve.value_load(ord_i[layer][0:1, bass.ds(b, 1)], min_val=0, max_val=m.ordinals - 1)
                    dve.wait_ge(y_psum, b + (o + 1))
                    if m.shared:
                        dve.wait_ge(y_stored[par], stored_before(b, par))
                        dve.tensor_copy(yb[:, par, :], PS[:, 7, 0:C]).then_inc(y_dve, 1)
                        return
                    if not (isinstance(b, int) and b < 2):
                        dve.wait_ge(y_stored[par], stored_before(b, par))
                    dve.tensor_tensor(yb[:, par, :], PS[:, 7, 0:C],
                                      bd[0][:, bass.ds(q % 2, 1), :].rearrange("p a n -> p (a n)"), ALU.add).then_inc(y_dve, 1)

                def stored_before(b, par):
                    before = 0 if layer == 0 else 16 * ((moes[0].blocks + 1 - par) // 2)
                    if isinstance(b, int):
                        return before + 8 * (b - par)
                    return b * 8 + (before - 8 * par)

                def step(b, par, more):
                    copy_hT(b, par)
                    if more >= 1:
                        hidden(b + 1, 1 - par)
                    copy_y(b, par)

                hidden(0, 0)
                for b in range(2):
                    step(b, b, 2)
                turns = (m.blocks - 5) // 2
                with dve.Fori(0, turns) as i:
                    if not m.shared:
                        st.enter(i, 6)
                    step(i * 2 + 2, 0, 2)
                    step(i * 2 + 3, 1, 2)
                if not m.shared:
                    st.leave(turns)
                for b in range(m.blocks - 3, m.blocks):
                    step(b, b % 2, m.blocks - 1 - b)
                for t in range(NT):
                    per = 32 + 16 * m.shared
                    dve.wait_ge(got_in[t % 2], (NT // 2) * 32 * layer + per * (t // 2 + 1))
                    if m.shared:
                        st.wait(dve.tensor_tensor(X[:, t, :], X[:, t, :], got[:, t % 2, TOP, :], ALU.add))
                    st.wait(dve.scalar_tensor_tensor(X[:, t, :], got[:, t % 2, 0, :], weight[:, 0, t:t + 1], X[:, t, :],
                                                     ALU.mult, ALU.add))
                    dve.scalar_tensor_tensor(X[:, t, :], got[:, t % 2, 1, :], weight[:, 1, t:t + 1], X[:, t, :],
                                             ALU.mult, ALU.add).then_inc(added, 1)
                dve.wait_ge(added, NT * (layer + 1))
                if stop_after == 2 * layer + 2:
                    return

        @block.tensor
        def _(pe):
            pe.wait_ge(pool_const, 2)

            def transposes(n):
                for j in range(6):
                    kc, half = j // 2, j % 2
                    for t in range(4 * half, 4 * half + 4):
                        pe.wait_ge(xn_ready, NT * n + t + 1)
                        last = pe.transpose(PS[:, j, (t % 4) * P:(t % 4 + 1) * P], Xn[:, t, kc * P:(kc + 1) * P], ident[:, :])
                    last.then_inc(xT_psum, 1)
                pe.wait_ge(xT_act, 3 * (n + 1))
                pe.wait_ge(xT_dve, 3 * (n + 1))

            for layer in range(2):
                transposes(2 * layer)
                pe.wait_ge(wqkv_in[layer], 16 * (5 if layer == 0 else 2))
                k_col, v_col, v_width = (C, 2 * C, C) if layer == 0 else (C, C + P, P)
                for n, (kind, a, b) in enumerate(jobs(layer)):
                    bank = n % 8
                    if n >= 8:
                        evacuated(pe, layer, n - 8)
                    if kind in ("q", "k"):
                        col = (0 if kind == "q" else k_col) + a * P
                        for kc in range(KC):
                            last = pe.matmul(PS[:, bank, :], Wqkv[:, kc, col:col + P], XnT[:, kc, b * BANK:(b + 1) * BANK],
                                             start=kc == 0, stop=kc == KC - 1)
                    elif kind == "v":
                        for kc in range(KC):
                            last = pe.matmul(PS[:, bank, 0:v_width], XnT[:, kc, a * P:(a + 1) * P],
                                             Wqkv[:, kc, v_col:v_col + v_width], start=kc == 0, stop=kc == KC - 1)
                    else:
                        if a == 0 and kind == "relh":
                            evacuated(pe, layer, HALF * KC - 1)
                            pe.wait_ge(rel_ready, 1)
                        table = relh_bd if kind == "relh" else relw_bd
                        for r in range(4):
                            i = 4 * a + r
                            rhs = (q32[:, :, i * GRID:(i + 1) * GRID] if kind == "relh" else
                                   q32[:, :, :].rearrange("p c (h w) -> p c h w", w=GRID)[:, :, :, i])
                            last = pe.matmul(PS[:, bank, r * KC * GRID:(r + 1) * KC * GRID].rearrange("p (c n) -> p c n", c=KC),
                                             table[:, i:i + GRID, :].rearrange("p j g -> p (j g)"), rhs, start=r == 0, stop=r == 3, skip_group_check=True)
                    last.then_inc(job_psum, 1)
                njobs = len(jobs(layer))
                for n in range(njobs - 8, njobs):
                    evacuated(pe, layer, n)

                def max_tile(c, t):
                    g, qt = t // NT, t % NT
                    number = TILES * (KC * layer + c) + t
                    lo, hi = keys_of(layer, qt)
                    if c == 0:
                        bank = 2 * (t % 3)
                        if t >= 3:
                            pe.wait_ge(max_done, number - 2)
                    else:
                        bank = 4 if layer == 0 else 4 + qt % 2
                        pe.wait_ge(max_done, number if layer == 0 or t == 0 else number - 1)
                    for k0 in range(lo, hi, BANK):
                        k1 = min(k0 + BANK, hi)
                        last = pe.matmul(PS[:, bank + (k0 - lo) // BANK, 0:k1 - k0], QA[:, c % 2, g, qt * P:(qt + 1) * P],
                                         KA[:, c % 2 if layer == 0 else 0, g, k0:k1], start=True, stop=True)
                    last.then_inc(max_psum, 1)

                def maxima_rows(c):
                    pe.wait_ge(max_done, TILES * (KC * layer + c + 1))
                    for qt in range(NT):
                        for g in range(G):
                            col = NT * g + qt
                            last = pe.matmul(PS[D * g:D * g + D, 4 + qt // 4, (qt % 4) * P:(qt % 4 + 1) * P],
                                             nmax[:, c, col:col + 1].broadcast_to([P, D]), ident[:, :],
                                             start=qt % 4 == 0, stop=qt % 4 == 3, skip_group_check=True)
                    last.then_inc(nmax_psum, 1)
                    pe.wait_ge(nmax_act, KC * layer + c + 1)

                def scores(c, u, pair):
                    half, kt, lo, hi = units(layer)[u]
                    use = 2 * (PV_BEFORE[layer] + U[layer] * c + u) + pair
                    if use >= 2:
                        pe.wait_ge(exp_done, use - 1)
                    for j in range(2):
                        g = 2 * pair + j
                        ks, keys = c % 2 if layer == 0 else 0, slice(kt * P, (kt + 1) * P)
                        queries = slice(half * BANK + lo, half * BANK + hi)
                        pe.matmul(PS[:, 2 * pair + j, lo:hi], KA[:, ks, g, keys], QA[:, c % 2, g, queries],
                                  start=True, stop=False)
                        last = pe.matmul(PS[:, 2 * pair + j, lo:hi], QKB[:, ks, 1, g, keys], QKB[:, c % 2, 0, g, queries],
                                         start=False, stop=True)
                    last.then_inc(score_psum, 1)

                def weighted(c, u):
                    half, kt, lo, hi = units(layer)[u]
                    first, last_one = u % (U[layer] // 2) == 0, (u + 1) % (U[layer] // 2) == 0
                    pe.wait_ge(exp_done, 2 * (PV_BEFORE[layer] + U[layer] * c + u + 1))
                    if first and (layer or c or half):
                        pe.wait_ge(norm_done, 2 * (KC * layer + c) + half)
                    probs = [expS[:, 2 * (u % 2) + g // 2, (g % 2) * BANK + lo:(g % 2) * BANK + hi] for g in range(G)]
                    for g in range(G):
                        vcol = P * c + D * g if layer == 0 else D * g
                        pe.matmul(PS[D * g:D * g + D, 6, lo:hi], V[:, kt, vcol:vcol + D], probs[g],
                                  start=first, stop=last_one, skip_group_check=True)
                    for g in range(G):
                        last = pe.matmul(PS[D * g:D * g + D, 7, lo:hi], ones[:, 0:D], probs[g],
                                         start=first, stop=last_one, skip_group_check=True)
                    last.then_inc(pv_done, 1)

                pe.wait_ge(a_in[0], placed(A_DMAS, layer, 0))
                for t in range(TILES):
                    max_tile(0, t)
                for c in range(KC):
                    maxima_rows(c)
                    pe.wait_ge(b_in[c % 2], placed(B_DMAS, layer, c))
                    scores(c, 0, 0)
                    scores(c, 0, 1)
                    for u in range(U[layer]):
                        tiles = list(tiles_at(layer, u)) if c + 1 < KC else []
                        if c + 1 < KC and u == 0:
                            pe.wait_ge(a_in[(c + 1) % 2], placed(A_DMAS, layer, c + 1))
                        more = u + 1 < U[layer]
                        for n, t in enumerate(tiles[:2]):
                            if more:
                                scores(c, u + 1, n)
                            max_tile(c + 1, t)
                        for pair in range(len(tiles[:2]), 2):
                            if more:
                                scores(c, u + 1, pair)
                        weighted(c, u)
                        for t in tiles[2:]:
                            max_tile(c + 1, t)
                pe.wait_ge(norm_done, 2 * KC * (layer + 1))
                for t in range(NT):
                    if t >= 6:
                        pe.wait_ge(proj_dve, NT * layer + t - 5)
                    for kc in range(KC):
                        last = pe.matmul(PS[:, t % 6, 0:C], attT[:, kc, t * P:(t + 1) * P], Wproj[:, kc, :],
                                         start=kc == 0, stop=kc == KC - 1)
                    last.then_inc(proj_psum, 1)
                if stop_after == 2 * layer + 1:
                    return
                pe.wait_ge(proj_dve, NT * (layer + 1))

                m = moes[layer]
                transposes(2 * layer + 1)
                pe.wait_ge(const_in, 16 * 4)
                for t in range(NT):
                    for kc in range(KC):
                        last = pe.matmul(PS[:, 6, t * E:(t + 1) * E], XnT[:, kc, t * P:(t + 1) * P], router_w[:, layer, kc, :],
                                         start=kc == 0, stop=kc == KC - 1)
                last.then_inc(route_psum, 1)
                pe.wait_ge(picked_ready, layer + 1)
                pk = picked[:, :, :].rearrange("p t e -> p (t e)")
                pe.matmul(PS[:, 7, 0:NT * E], before[:, :], pk, start=True, stop=True)
                pe.matmul(PS[:, 7, NT * E:2 * NT * E], ones[:, :], pk, start=True, stop=True).then_inc(rank_psum, 1)
                pe.wait_ge(tables_ready, layer + 1)

                o = m.blocks_before
                WIN_LOAD = 16 * (3 if m.shared else 4)
                w_before = 0 if layer == 0 else 64 * E
                xb_before = 16 * o

                def transpose_x(b, par):
                    pe.wait_ge(xb_in[par], b * 8 + (16 + 16 * ((o + 1 - par) // 2) - 8 * par))
                    if not (isinstance(b, int) and b == 0):
                        pe.wait_ge(bT_act, b + o)
                    for kc in range(KC):
                        last = pe.transpose(PS[:, 6, kc * P:(kc + 1) * P], xb[:, par, kc * P:(kc + 1) * P], ident[:, :])
                    last.then_inc(bT_psum, 1)

                def gate_up(b, par):
                    q = pe.value_load(ord_i[layer][0:1, bass.ds(b, 1)], min_val=0, max_val=m.ordinals - 1)
                    pe.wait_ge(bT_act, b + (o + 1))
                    pe.wait_ge(w_in, (q + 1) * WIN_LOAD + w_before)
                    s = q % 2
                    width = 2 * m.I
                    for lo in range(0, width, BANK):
                        n = min(BANK, width - lo)
                        for kc in range(KC):
                            last = pe.matmul(PS[:, 3 * par + lo // BANK, 0:n], xbT[:, par, kc, :],
                                             Wgu[layer][:, bass.ds(s, 1), kc, lo:lo + n],
                                             start=kc == 0, stop=kc == KC - 1)
                    last.then_inc(gu_psum, 1)

                def transpose_h(b, par):
                    pe.wait_ge(hid_done, b + (o + 1))
                    for i in range(m.IC):
                        last = pe.transpose(PS[:, 3 * par + i // 3, (i % 3) * P:(i % 3 + 1) * P],
                                            hid[:, par, i * P:(i + 1) * P], ident[:, :])
                    last.then_inc(hT_psum, 1)

                def down(b, par):
                    per = 2 if m.shared else 1
                    q = pe.value_load(ord_i[layer][0:1, bass.ds(b, 1)], min_val=0, max_val=m.ordinals - 1)
                    pe.wait_ge(hT_copied, b * per + (per + (moes[0].blocks if m.shared else 0)))
                    if not (isinstance(b, int) and b == 0):
                        pe.wait_ge(y_dve, b + o)
                    s = q % 2
                    for i in range(m.IC):
                        last = pe.matmul(PS[:, 7, 0:C], hidT[:, par, i, :], Wd[layer][:, bass.ds(s, 1), i, :],
                                         start=i == 0, stop=i == m.IC - 1)
                    last.then_inc(y_psum, 1)

                def step(b, par, more):
                    if more >= 1:
                        gate_up(b + 1, 1 - par)
                    transpose_h(b, par)
                    if more >= 2:
                        transpose_x(b + 2, par)
                    down(b, par)

                transpose_x(0, 0)
                gate_up(0, 0)
                transpose_x(1, 1)
                for b in range(2):
                    step(b, b, 2)
                with pe.Fori(0, (m.blocks - 5) // 2) as i:
                    step(i * 2 + 2, 0, 2)
                    step(i * 2 + 3, 1, 2)
                for b in range(m.blocks - 3, m.blocks):
                    step(b, b % 2, m.blocks - 1 - b)
                if stop_after == 2 * layer + 2:
                    return


_OUT = ((1, 32, 32, 384), "float32")


def kernel(**inputs):
    import numpy as np
    import concourse.bacc as bacc
    from concourse.bass_utils import run_bass_kernel_spmd as run

    a = {k: np.ascontiguousarray(v) for k, v in inputs.items()}
    arrays = {
        "x": a["x"].reshape(T, C),
        "qkv_w": a["L0_conv_qkv_w"], 
        "qk_b": np.ascontiguousarray(a["L0_conv_qkv_b"][:2 * C].reshape(2 * KC, P).T),
        "v_b": np.ascontiguousarray(a["L0_conv_qkv_b"][2 * C:]),
        "proj_w": a["L0_conv_proj_w"], "proj_b": a["L0_conv_proj_b"],
        "rel_both": np.ascontiguousarray(np.stack([a["L0_conv_rel_pos_h"].T, a["L0_conv_rel_pos_w"].T], 1)),
        "Wr0": a["L0_ffn_Wr"], "br0": a["L0_ffn_br"], "Wgu0": a["L0_ffn_Wgu"], "bgu0": a["L0_ffn_bgu"],
        "Wd0": a["L0_ffn_Wd"], "bd0": a["L0_ffn_bd"],
        "w_qkv1": np.ascontiguousarray(a["L1_conv_w_qkv"].T),
        "w_out1": np.ascontiguousarray(a["L1_conv_w_out"].T),
        "Wg_s": a["L1_ffn_Wg_s"][0], "Wu_s": a["L1_ffn_Wu_s"][0], "Wd_s": a["L1_ffn_Wd_s"][0],
        "Wg_r": a["L1_ffn_Wg_r"], "Wu_r": a["L1_ffn_Wu_r"], "Wd_r": a["L1_ffn_Wd_r"],
        "Wr1": a["L1_ffn_W_router"], "br1": a["L1_ffn_expert_bias"],
    }
    nc = bacc.Bacc("TRN2", target_bir_lowering=False, num_devices=1)
    args = {k: nc.dram_tensor(f"in_{k}", v.shape, mybir.dt.from_np(v.dtype), kind="ExternalInput").ap()
            for k, v in arrays.items()}
    out = nc.dram_tensor("out_0", (T, C), mybir.dt.from_np(np.dtype(_OUT[1])), kind="ExternalOutput").ap()
    build(nc, out=out, **args)
    r = run(nc, [{f"in_{k}": v for k, v in arrays.items()}], core_ids=[0])
    return r.results[0]["out_0"].reshape(_OUT[0])
```

```python
from contextlib import ExitStack

import concourse.bass as bass
from concourse import mybir

F32 = mybir.dt.float32
F32R = mybir.dt.float32r
I32 = mybir.dt.int32
U32 = mybir.dt.uint32
ACT = mybir.ActivationFunctionType
ALU = mybir.AluOpType
AX = mybir.AxisListType

P = 128
GRID = 32
T = GRID * GRID
NT = T // P
C = 384
KC = C // P
D = 32
G = P // D
QK_SCALE = D ** -0.5
REL_SCALE = D ** 0.5
BANK = 512
HALF = T // BANK
WIN = 7
MASKED = -float(2 ** 100)
E = 8
TOP = 2
ALPHA, LIMIT = 1.702, 7.0
ROUTED_BLOCKS = (TOP * T + E * (P - 1)) // P
REL = 2 * GRID - 1


class Steps:

    def __init__(self, eng, sem):
        self.eng, self.sem, self.n, self.off = eng, sem, 0, None

    def value(self):
        return self.n if self.off is None else self.off + self.n

    def wait(self, ins):
        self.n += 1
        ins.then_inc(self.sem, 1)
        self.eng.wait_ge(self.sem, self.value())

    def enter(self, turn, per_turn):
        self.first, self.per = self.n, per_turn
        self.off = turn * per_turn

    def leave(self, turns):
        assert self.n - self.first == self.per
        self.off = None
        self.n = self.first + self.per * turns


class Moe:

    def __init__(self, layer, inner, slots):
        self.layer, self.I, self.slots = layer, inner, slots
        self.IC = inner // P
        self.blocks = ROUTED_BLOCKS
        self.blocks_before = layer * ROUTED_BLOCKS


def build(nc, x, qkv_w, qk_b, v_b, proj_w, proj_b, rel_both, Wr0, br0, Wgu0, bgu0, Wd0, bd0,
          w_qkv1, w_out1, Wg_s, Wu_s, Wd_s, Wg_r, Wu_r, Wd_r, Wr1, br1, out):
    ctx = ExitStack()
    base = [nc.sbuf_base + (-nc.sbuf_base) % 64]
    top = [0]

    def sb(name, shape, dt=F32):
        size = 2 if dt == mybir.dt.bfloat16 else 4
        for n in shape[1:]:
            size *= n
        t = nc.alloc_sbuf_tensor_at(name, shape, dt, offset=base[0])
        base[0] += size + (-size) % 64
        top[0] = max(top[0], base[0])
        return t

    moes = [Moe(0, 384, 4), Moe(1, 768, 2)]

    with ctx:
        def sem(name):
            return ctx.enter_context(nc.semaphore(name))

        X = sb("X", [P, NT, C])
        Xn = sb("Xn", [P, NT, C])
        expS = nc.alloc_sbuf_tensor_at("expS", [P, 4, 2 * BANK], F32, offset=base[0] - 4 * NT * C)
        xn_end = base[0]
        base[0] += 4 * (4 * 2 * BANK - NT * C)
        XnT = sb("XnT", [P, KC, T])
        ident = sb("ident", [P, P])
        before = sb("before", [P, P])
        ones = sb("ones", [P, P])
        stats = sb("stats", [P, NT, 6])
        mv = sb("mv", [P, NT, 2])
        var_eps = sb("var_eps", [P, NT])
        std = sb("std", [P, NT])
        rstd = sb("rstd", [P, NT])
        router_w = sb("router_w", [P, 2, KC, E])
        router_b = sb("router_b", [P, 2])
        logits_t = sb("logits_t", [P, T])
        iota_e = sb("iota_e", [P, E])
        iota_blk = sb("iota_blk", [P, 32])
        thresholds = sb("thresholds", [P, 8])
        warm = sb("warm", [P, 1])
        logits = sb("logits", [P, NT, E])
        top8 = sb("top8", [P, NT, 8])
        top8i = sb("top8i", [P, NT, 8], U32)
        top_f = sb("top_f", [P, NT, 2])
        gap = sb("gap", [P, NT])
        weight = sb("weight", [P, 2, NT])
        chosen = sb("chosen", [P, 2, NT, E])
        picked = sb("picked", [P, NT, E])
        tile_cum = [sb(f"tile_cum{i}", [P, NT, E]) for i in range(4)]
        blk_cum = [sb(f"blk_cum{i}", [P, E]) for i in range(4)]
        over = sb("over", [P, E, 8])
        start_row = sb("start_row", [P, E])
        place = sb("place", [P, NT, E])
        place_k = sb("place_k", [P, 2, NT, E])
        row_f = sb("row_f", [P, 2, NT])
        row_i = sb("row_i", [P, 2, NT], I32)
        blk_ge = sb("blk_ge", [P, 32, E])
        ord_f = sb("ord_f", [P, 32])
        ord_i = [sb(f"ord_i{n}", [P, 32], I32) for n in range(2)]
        end_i = [sb(f"end_i{n}", [P, 16], I32) for n in range(2)]
        shared_base = base[0]

        Wproj = sb("Wproj", [P, KC, C])
        qk_bias = sb("qk_bias", [P, 2 * KC])
        v_bias = sb("v_bias", [P, C])
        p_bias = sb("p_bias", [P, C])
        relh_bd = sb("relh_bd", [P, REL, G])
        relw_bd = sb("relw_bd", [P, REL, G])
        rel_t = sb("rel_t", [P, 2, REL])
        V = sb("V", [P, NT, C])
        nmax = sb("nmax", [P, KC, G * NT])
        sum_exp = sb("sum_exp", [P, BANK])
        weighted_exp = sb("weighted_exp", [P, BANK])
        attT = XnT
        parts_base = base[0]
        QKA = sb("QKA", [P, 2, 2, G, T], F32R)
        QA, KA = QKA[:, :, 0], QKA[:, :, 1]
        QKB = sb("QKB", [P, 2, 2, G, T], F32R)
        assert base[0] <= nc.sbuf_usable_end, base[0]
        part = {}
        for n, name in enumerate(("q_hi", "q_lo", "rh_hi", "rh_lo", "rw_hi", "rw_lo", "k_hi", "k_lo")):
            part[name] = nc.alloc_sbuf_tensor_at(f"part_{name}", [P, KC, T], F32R, offset=parts_base + n * 4 * KC * T)
        part1 = dict(part, q_hi=part["rh_lo"], q_lo=part["rw_hi"])
        spare = parts_base + 4 * (2 * 2 * G * T + 2 * G * T)
        q32 = nc.alloc_sbuf_tensor_at("q32", [P, KC, T], F32, offset=spare)
        key_const = nc.alloc_sbuf_tensor_at("key_const", [P, T], F32, offset=spare + 4 * KC * T)
        Wqkv = nc.alloc_sbuf_tensor_at("Wqkv", [P, KC, 3 * C], F32, offset=spare + 4 * G * T)
        mask_const = nc.alloc_sbuf_tensor_at("mask_const", [P, T], F32, offset=xn_end)

        base[0] = parts_base
        Wgu, Wd = [], []
        for m in moes:
            base[0] = parts_base
            Wgu.append(sb(f"Wgu{m.layer}", [P, m.slots, KC, 2 * m.I]))
            Wd.append(sb(f"Wd{m.layer}", [P, m.slots, m.IC, C]))
            if m.layer == 0:
                bgu = sb("bgu", [P, m.slots, 2 * m.I])
                bd = sb("bd", [P, m.slots, C])
        I1 = moes[1].I
        shared_gu = sb("shared_gu", [P, KC, 2 * I1])
        shared_d = sb("shared_d", [P, moes[1].IC, C])
        hidden_base = base[0]
        gated = sb("gated", [P, 2, I1])
        pre = sb("pre", [P, 2, I1])
        hid = sb("hid", [P, 2, I1])
        hidT = sb("hidT", [P, 2, I1 // P, P])
        shared_hidT = nc.alloc_sbuf_tensor_at("shared_hidT", [P, I1 // P, T], F32, offset=hidden_base)
        assert hidden_base + 4 * (I1 // P) * T <= base[0]
        shared_gate = sb("shared_gate", [P, 2, BANK])
        assert base[0] <= spare + 4 * G * T
        slot_gu, slot_d = 4 * KC * 2 * I1, 4 * (I1 // P) * C
        gu_hi = nc.alloc_sbuf_tensor_at("gu_hi", [P, KC, 2 * I1], F32R, offset=parts_base + slot_gu)
        gu_lo = nc.alloc_sbuf_tensor_at("gu_lo", [P, KC, 2 * I1], F32R, offset=parts_base + 2 * (slot_gu + slot_d))
        xn_hi = sb("xn_hi", [P, KC, T], F32R)
        assert 2 * 4 * T <= slot_d
        xn_lo = [nc.alloc_sbuf_tensor_at(f"xn_lo{kc}", [P, T], F32R, offset=parts_base + 2 * slot_gu + slot_d + 4 * T * kc)
                 for kc in range(2)] + [sb("xn_lo2", [P, T], F32R)]
        base[0] = shared_base
        xb = sb("xb", [P, 4, C])
        xbT = sb("xbT", [P, 2, KC, P])
        yb = sb("yb", [P, 2, C])
        got = sb("got", [P, 4, TOP, C])
        assert base[0] <= parts_base, (base[0], parts_base)
        assert top[0] <= nc.sbuf_usable_end, (top[0], nc.sbuf_usable_end)

        PS = ctx.enter_context(nc.psum_tensor("PS", [P, 8, BANK], F32))
        xs = nc.dram_tensor("block_rows_in", [ROUTED_BLOCKS * P, C], F32, kind="Internal").ap()
        ys = nc.dram_tensor("block_rows_out", [ROUTED_BLOCKS * P, C], F32, kind="Internal").ap()

        key_rows = nc.dram_tensor("key_rows", [P, T], F32, kind="Internal").ap()
        zero_rows = nc.dram_tensor("zero_rows", [2 * D, T], F32, kind="Internal").ap()
        mask_rows = nc.dram_tensor("mask_rows", [P, T], F32, kind="Internal").ap()

        part_rows = {name: nc.dram_tensor(f"rows_{name}", [KC, P, T], F32, kind="Internal").ap() for name in part}

        x_in = [sem(f"x_in{n}") for n in range(4)]
        const_in = sem("const_in")
        ident_ready = sem("ident_ready")
        pool_const = sem("pool_const")
        rel_in = sem("rel_in")
        rel_ready = sem("rel_ready")
        const_stored = sem("const_stored")
        bias_in = sem("bias_in")
        wproj_in = sem("wproj_in")
        x_biased = sem("x_biased")
        wqkv_in = [sem("wqkv0_in"), sem("wqkv1_in")]
        dve_step = sem("dve_step")
        pool_step = sem("pool_step")
        var_ready = sem("var_ready")
        std_ready = sem("std_ready")
        xn_ready = sem("xn_ready")
        xT_psum = sem("xT_psum")
        xT_act = sem("xT_act")
        xT_dve = sem("xT_dve")
        job_psum = sem("job_psum")
        job_act = sem("job_act")
        job_dve = sem("job_dve")
        hi_act = sem("hi_act")
        q_split = sem("q_split")
        parts_stored = sem("parts_stored")
        a_in = [sem("a_in0"), sem("a_in1")]
        b_in = [sem("b_in0"), sem("b_in1")]
        v_psum = sem("v_psum")
        v_copied = sem("v_copied")
        v_biased = sem("v_biased")
        max_psum = sem("max_psum")
        max_done = sem("max_done")
        nmax_psum = sem("nmax_psum")
        nmax_act = sem("nmax_act")
        score_psum = sem("score_psum")
        exp_done = sem("exp_done")
        pv_done = sem("pv_done")
        pv_copied = sem("pv_copied")
        inverted = sem("inverted")
        normalised = sem("normalised")
        proj_psum = sem("proj_psum")
        proj_dve = sem("proj_dve")
        xs_zeroed = sem("xs_zeroed")
        zero_ready = sem("zero_ready")
        logits_psum = sem("logits_psum")
        logits_act = sem("logits_act")
        route_psum = sem("route_psum")
        gap_ready = sem("gap_ready")
        exp_gap = sem("exp_gap")
        picked_ready = sem("picked_ready")
        rank_psum = sem("rank_psum")
        rows_ready = sem("rows_ready")
        tables_ready = sem("tables_ready")
        scattered = sem("scattered")
        shared_in = sem("shared_in")
        xn_hi_ready = sem("xn_hi_ready")
        xn_lo_ready = sem("xn_lo_ready")
        gu_hi_ready = sem("gu_hi_ready")
        gu_lo_ready = sem("gu_lo_ready")
        shared_psum = sem("shared_psum")
        shared_silu = sem("shared_silu")
        shared_hid = sem("shared_hid")
        shared_y = sem("shared_y")
        shared_added = sem("shared_added")
        w_in = sem("w_in")
        xb_in = [sem(f"xb_in{n}") for n in range(4)]
        bT_psum = sem("bT_psum")
        bT_act = sem("bT_act")
        gu_psum = sem("gu_psum")
        gate_act = sem("gate_act")
        pre_dve = sem("pre_dve")
        hid_done = sem("hid_done")
        hT_psum = sem("hT_psum")
        hT_copied = sem("hT_copied")
        y_psum = sem("y_psum")
        y_dve = sem("y_dve")
        y_stored = [sem("y_stored0"), sem("y_stored1")]
        got_in = [sem(f"got_in{n}") for n in range(4)]
        added = sem("added")
        out_done = sem("out_done")

        block = ctx.enter_context(nc.Block())

        A_DMAS = [[16, 7, 6], [18, 3, 2]]
        B_DMAS = [[5, 5, 4], [4, 2, 1]]

        W_LOAD = [16 * 4, 16 * 3]
        W_BEFORE = [0, E * W_LOAD[0]]
        PARTS_STORED = [8, 11]

        def placed(dmas, layer, c):
            return 16 * sum(dmas[la][ch] for la in range(2) for ch in range(KC)
                            if (la, ch) <= (layer, c) and ch % 2 == c % 2)

        HI_JOBS = 16 + KC * HALF
        JOBS = [2 * KC * HALF + 16, (KC + 1) * HALF]

        def jobs(layer):
            def q(half):
                return [("q", c, half) for c in range(KC)]

            def k(c):
                return [("k", c, half) for half in range(HALF)]

            rel = [("relh", n, 0) for n in range(8)] + [("relw", n, 0) for n in range(8)]
            if layer == 0:
                every = q(0) + q(1) + k(0) + rel + k(1) + k(2)
            else:
                every = k(0)[:1] + q(0) + k(0)[1:] + q(1)
            assert len(every) == JOBS[layer]
            return every

        EARLY_JOBS = [KC, KC + 1]

        def job_bank(n):
            return (n + 6) % 8

        def by_act(kind):
            return kind == "q"

        def units(layer):
            out = []
            for half in range(HALF):
                for kt in range(NT):
                    lo, hi = (0, NT - 1) if layer == 0 else (kt - 1, kt + 1)
                    lo, hi = max(lo, 4 * half), min(hi, 4 * half + 3)
                    if lo <= hi:
                        out.append((half, kt, (lo - 4 * half) * P, (hi + 1 - 4 * half) * P))
            return out

        def rel_views(kind, half, a, bank):
            src = PS[:, bank, 0:4 * KC * GRID].rearrange("p (r c n) -> p c r n", r=4, c=KC)
            if kind == "relh":
                return part[f"rh_{half}"][:, :, a * P:(a + 1) * P].rearrange("p c (r n) -> p c r n", r=4), src
            return part[f"rw_{half}"][:, :, :].rearrange("p c (n r) -> p c r n", r=GRID)[:, :, 4 * a:4 * a + 4, :], src

        U = [len(units(0)), len(units(1))]
        PV_BEFORE = [0, KC * U[0]]
        TILES = G * NT

        def keys_of(layer, qt):
            return (0, T) if layer == 0 else (max(qt - 1, 0) * P, min(qt + 2, NT) * P)

        def tiles_at(layer, u):
            units_half = U[layer] // 2
            half, v = u // units_half, u % units_half
            first, end = (layer, units_half) if half == 0 else (0, units_half - 1)
            if not first <= v < end:
                return range(0)
            lo, count, n = TILES // 2 * half, TILES // 2, end - first
            return range(lo + count * (v - first) // n, lo + count * (v - first + 1) // n)

        def rows_at(layer, u):
            return {U[layer] // 2: 0, U[layer] - 1: 1}.get(u)

        for layer in range(2):
            assert sorted(t for u in range(U[layer]) for t in tiles_at(layer, u)) == list(range(TILES))

        FIRST, TURNS = 2, (ROUTED_BLOCKS - 2 - 3) // 4
        LAST = FIRST + 4 * TURNS

        def all_blocks(eng, step):
            for b in range(FIRST):
                step(b, b % 4, 4)
            with eng.Fori(0, TURNS) as i:
                for n in range(4):
                    step(i * 4 + (FIRST + n), (FIRST + n) % 4, 4)
            for b in range(LAST, ROUTED_BLOCKS):
                step(b, b % 4, ROUTED_BLOCKS - 1 - b)

        def evacuated(eng, layer, n):
            done = jobs(0) if layer else []
            mine = done + jobs(layer)[:n + 1]
            kind = jobs(layer)[n][0]
            count = sum(by_act(j[0]) == by_act(kind) for j in mine)
            eng.wait_ge(job_act if by_act(kind) else job_dve, count)

        def chunk_of(w, f):
            return w[:, :, :].rearrange("p k (u n) -> p k u n", u=2)[:, :, :, f * P:(f + 1) * P]

        def flat(bank, banks):
            return PS[:, bank:bank + banks, :].rearrange("p b n -> p (b n)")

        @block.sync
        def _(sp):
            x_view = x.rearrange("(t p) c -> p t c", p=P)
            for n in range(4):
                sp.dma_start(X[:, 2 * n:2 * n + 2, :], x_view[:, 2 * n:2 * n + 2, :]).then_inc(x_in[n], 16)
            for layer in range(2):
                if layer == 0:
                    sp.dma_start(Wqkv[:, :, :], qkv_w.rearrange("(k p) n -> p k n", p=P)).then_inc(wqkv_in[0], 16)
                    sp.dma_start(qk_bias[:, :], qk_b).then_inc(bias_in, 16)
                    for g in range(G):
                        sp.dma_start(rel_t[D * g:D * g + D], rel_both).then_inc(rel_in, 16)
                    sp.dma_start(v_bias[:, :], v_b.partition_broadcast(P)).then_inc(bias_in, 16)
                    sp.dma_start(p_bias[:, :], proj_b.partition_broadcast(P)).then_inc(bias_in, 16)
                    sp.dma_start(Wproj[:, :, :], proj_w.rearrange("(k p) n -> p k n", p=P)).then_inc(wproj_in, 16)
                    for la, (w, b) in enumerate(((Wr0, br0), (Wr1, br1))):
                        sp.dma_start(router_w[:, la], w.rearrange("(k p) e -> p k e", p=P)).then_inc(const_in, 16)
                        sp.dma_start(router_b[0:E, la:la + 1], b.rearrange("(e a) -> e a", a=1)).then_inc(const_in, 16)
                    sp.wait_ge(zero_ready, 1)
                    sp.dma_start(xs.rearrange("(b p) c -> p b c", p=P),
                                 V[:, 0:1, :].broadcast_to([P, ROUTED_BLOCKS, C])).then_inc(xs_zeroed, 16)
                else:
                    sp.wait_ge(y_psum, moes[0].blocks)
                    sp.wait_ge(added, NT)
                    sp.dma_start(Wproj[:, :, :], w_out1.rearrange("(k p) n -> p k n", p=P)).then_inc(wproj_in, 16)
                if layer == 0:
                    sp.wait_ge(pool_const, 2)
                    sp.dma_start(key_rows[D:P, :], key_const[D:P, :]).then_inc(const_stored, 16)
                    sp.dma_start(mask_rows[D:3 * D, :], mask_const[D:3 * D, :]).then_inc(const_stored, 16)
                    for n in range(2):
                        sp.dma_start(zero_rows[D * n:D * n + D, :], mask_const[0:D, :]).then_inc(const_stored, 16)
                    sp.wait_ge(const_stored, 16 * 4)
                parts = part if layer == 0 else part1
                stored = [PARTS_STORED[0] if layer else 0]

                def store(name, lo, hi):
                    sp.dma_start(part_rows[name][lo:hi].rearrange("c p t -> p c t"),
                                 parts[name][:, lo:hi, :].bitcast(F32)).then_inc(parts_stored, 16)
                    stored[0] += 1

                def last_job(kind, a):
                    evacuated(sp, layer, max(n for n, j in enumerate(jobs(layer)) if j[0] == kind and j[1] <= a))

                placing = {}

                def place(dst, src, done):
                    sp.dma_start(dst.bitcast(F32), src).then_inc(done, 16)
                    placing[done.name] = placing.get(done.name, 0) + 1

                def place_heads(dst, name, c, done):
                    order = "(g p) t -> p g t" if name[0] in "qk" else "(p g) t -> p g t"
                    place(dst, part_rows[name][c].rearrange(order, g=G), done)

                def place_direct(dst, name, done):
                    for g in range(G):
                        rows = slice(D * g, D * g + D) if name[0] in "qk" else slice(g, P, G)
                        place(dst[:, g, :], parts[name][rows, 0, :].bitcast(F32), done)

                def place_same(dst, rows, done):
                    place(dst, rows.rearrange("p (a t) -> p a t", a=1).broadcast_to([rows.shape[0], G, T]), done)

                def check(done, dmas):
                    assert placing.pop(done.name) == dmas

                def place_a(c):
                    s, done = c % 2, a_in[c % 2]
                    place_heads(QA[0:D, s], "q_hi", c, done)
                    place_heads(QA[3 * D:P, s], "q_lo", c, done)
                    if layer == 0:
                        place_heads(QA[D:2 * D, s], "rh_hi", c, done)
                        place_heads(QA[2 * D:3 * D, s], "rw_hi", c, done)
                        place_heads(KA[0:D, s], "k_hi", c, done)
                        place_heads(KA[3 * D:P, s], "k_hi", c, done)
                        if c == 1:
                            place_same(KA[D:3 * D, s], key_rows[D:3 * D, :], done)
                    elif c == 1:
                        place_same(QA[D:3 * D, s], mask_rows[D:3 * D, :], done)
                    check(done, A_DMAS[layer][c])

                def place_b(c):
                    s, done = c % 2, b_in[c % 2]
                    place_heads(QKB[0:D, s, 0], "q_hi", c, done)
                    if layer == 0:
                        place_heads(QKB[D:2 * D, s, 0], "rh_lo", c, done)
                        place_heads(QKB[2 * D:3 * D, s, 0], "rw_lo", c, done)
                    elif c < 2:
                        place_same(QKB[D:3 * D, s, 0], zero_rows, done)
                    if layer == 0 or c == 0:
                        place_heads(QKB[0:D, s, 1], "k_lo", c, done)
                        if c < 2:
                            place_same(QKB[D:P, s, 1], key_rows[D:P, :], done)
                    check(done, B_DMAS[layer][c])

                done = a_in[0]
                if layer == 0:
                    sp.wait_ge(q_split, KC)
                    store("q_hi", 0, KC)
                    store("q_lo", 0, KC)
                    last_job("relh", 7)
                    store("rh_hi", 0, KC)
                    sp.wait_ge(parts_stored, 16 * stored[0])
                    for dst, name in ((QA[0:D, 0], "q_hi"), (QA[3 * D:P, 0], "q_lo"), (QA[D:2 * D, 0], "rh_hi")):
                        place_heads(dst, name, 0, done)
                    place_same(KA[D:3 * D, 0], key_rows[D:3 * D, :], done)
                    last_job("k", 0)
                    place_direct(KA[0:D, 0], "k_hi", done)
                    place_direct(KA[3 * D:P, 0], "k_hi", done)
                    last_job("relw", 7)
                    place_direct(QA[2 * D:3 * D, 0], "rw_hi", done)
                    for name in ("rh_lo", "rw_hi", "rw_lo"):
                        store(name, 0, KC)
                    last_job("k", KC - 1)
                    store("k_hi", 0, KC)
                    store("k_lo", 0, KC)
                else:
                    place_same(QA[D:3 * D, 0], mask_rows[D:3 * D, :], done)
                    place_same(KA[D:3 * D, 0], key_rows[D:3 * D, :], done)
                    last_job("k", 0)
                    place_direct(KA[0:D, 0], "k_hi", done)
                    place_direct(KA[3 * D:P, 0], "k_hi", done)
                    sp.wait_ge(q_split, KC + 1)
                    place_direct(QA[0:D, 0], "q_hi", done)
                    place_direct(QA[3 * D:P, 0], "q_lo", done)
                    sp.wait_ge(q_split, 2 * KC)
                    store("q_hi", 0, KC)
                    store("q_lo", 0, KC)
                    store("k_lo", 0, 1)
                check(done, A_DMAS[layer][0])
                assert stored[0] == PARTS_STORED[layer]
                sp.wait_ge(a_in[0], placed(A_DMAS, layer, 0))
                sp.wait_ge(parts_stored, 16 * stored[0])
                place_b(0)
                place_a(1)
                sp.wait_ge(v_psum, NT * (layer + 1))
                place_b(1)
                sp.wait_ge(score_psum, 2 * (PV_BEFORE[layer] + U[layer]))
                place_a(2)
                place_b(2)

                m = moes[layer]
                if layer == 0:
                    sp.wait_ge(pv_done, PV_BEFORE[0] + KC * U[0])
                    sp.dma_start(Wqkv[:, :, 0:C + 2 * P], w_qkv1.rearrange("(k p) n -> p k n", p=P)).then_inc(wqkv_in[1], 16)

                def load(b, place):
                    sp.dma_start(xb[:, place, :], xs[bass.ds(b * P, P), :]).then_inc(xb_in[place], 16)

                def step(b, place, more):
                    if more >= 4:
                        sp.wait_ge(bT_psum, b + (m.blocks_before + 1))
                        load(b + 4, place)
                    sp.wait_ge(y_dve, b + (m.blocks_before + 1))
                    sp.dma_start(ys[bass.ds(b * P, P), :], yb[:, place % 2, :]).then_inc(y_stored[place % 2], 16)

                sp.wait_ge(scattered, 16 * TOP * NT * (layer + 1))
                for b in range(4):
                    load(b, b)
                all_blocks(sp, step)
            out_view = out.rearrange("(t p) c -> p t c", p=P)
            for t in range(NT):
                sp.wait_ge(added, NT + t + 1)
                sp.dma_start(out_view[:, t, :], X[:, t, :]).then_inc(out_done, 16)
            sp.wait_ge(out_done, 16 * NT)

        @block.gpsimd
        def _(pool):
            st = Steps(pool, pool_step)
            st.wait(pool.memset(ident[:, :], 0.0))
            st.wait(pool.affine_select(out=ident[:, :], in_=ident[:, :], compare_op=ALU.not_equal, fill=1.0,
                                       base=0, pattern=[[-1, P]], channel_multiplier=1))
            pool.sem_inc(ident_ready, 1)
            pool.memset(V[:, 0, :], 0.0).then_inc(zero_ready, 1)
            st.wait(pool.memset(relh_bd[:, :, :], 0.0))
            st.wait(pool.memset(relw_bd[:, :, :], 0.0))
            pool.wait_ge(rel_in, 16 * G)
            for g in range(G):
                rows = slice(D * g, D * g + D)
                st.wait(pool.tensor_scalar(relh_bd[rows, :, g], rel_t[rows, 0, :], REL_SCALE, None, ALU.mult))
                st.wait(pool.tensor_scalar(relw_bd[rows, :, g], rel_t[rows, 1, :], REL_SCALE, None, ALU.mult))
            pool.sem_inc(rel_ready, 1)
            st.wait(pool.memset(ones[:, :], 1.0))
            st.wait(pool.affine_select(out=before[:, :], in_=ones[:, :], compare_op=ALU.is_gt, fill=0.0,
                                       base=0, pattern=[[1, P]], channel_multiplier=-1))
            st.wait(pool.iota(iota_e[:, :], pattern=[[1, E]], base=0, channel_multiplier=0,
                              allow_small_or_imprecise_dtypes=True))
            st.wait(pool.iota(iota_blk[:, :], pattern=[[1, 32]], base=0, channel_multiplier=0,
                              allow_small_or_imprecise_dtypes=True))
            st.wait(pool.iota(thresholds[:, :], pattern=[[P, 8]], base=0, channel_multiplier=0,
                              allow_small_or_imprecise_dtypes=True))
            st.wait(pool.memset(thresholds[:, 0:1], -1.0))
            pool.sem_inc(pool_const, 1)
            kc = key_const[:, :].rearrange("p (h w) -> p h w", w=GRID)
            st.wait(pool.memset(key_const[:, :], 0.0))
            st.wait(pool.affine_select(out=kc[D:2 * D], in_=kc[D:2 * D], compare_op=ALU.not_equal, fill=1.0,
                                       base=-(GRID - 1), pattern=[[1, GRID], [0, GRID]], channel_multiplier=1))
            st.wait(pool.affine_select(out=kc[2 * D:3 * D], in_=kc[2 * D:3 * D], compare_op=ALU.not_equal, fill=1.0,
                                       base=-(GRID - 1), pattern=[[0, GRID], [1, GRID]], channel_multiplier=1))
            st.wait(pool.memset(key_const[3 * D:3 * D + 1, :], 1.0))
            st.wait(pool.memset(mask_const[:, :], 0.0))
            mc = mask_const[:, :].rearrange("p (h w) -> p h w", w=GRID)
            for lo, hi, start, slope in ((0, 3, 0, 0), (3, 28, 0, 1), (28, 32, 25, 0)):
                n = hi - lo
                for rows, by_row in ((slice(D, 2 * D), True), (slice(2 * D, 3 * D), False)):
                    view = mc[rows, lo:hi, :] if by_row else mc[rows, :, lo:hi]
                    pat = (lambda s: [[s, n], [0, GRID]]) if by_row else (lambda s: [[0, GRID], [s, n]])
                    st.wait(pool.affine_select(out=view, in_=view, compare_op=ALU.is_ge, fill=MASKED,
                                               base=GRID - 1 - start, pattern=pat(-slope), channel_multiplier=-1))
                    st.wait(pool.affine_select(out=view, in_=view, compare_op=ALU.is_ge, fill=MASKED,
                                               base=start + WIN - 1 - (GRID - 1), pattern=pat(slope),
                                               channel_multiplier=1))
            pool.sem_inc(pool_const, 1)

            for layer in range(2):
                if layer == 0:
                    pool.wait_ge(bias_in, 16 * 3)
                    pool.wait_ge(xn_ready, NT)
                    pool.tensor_tensor(X[:, :, :], X[:, :, :],
                                       p_bias[:, :].rearrange("p (a c) -> p a c", a=1).broadcast_to([P, NT, C]),
                                       ALU.add).then_inc(x_biased, 1)
                    for t in range(NT):
                        pool.wait_ge(v_copied, t + 1)
                        pool.tensor_tensor(V[:, t, :], V[:, t, :], v_bias[:, :], ALU.add).then_inc(v_biased, 1)
                for c in range(KC):
                    for half in range(HALF):
                        pool.wait_ge(inverted, HALF * (KC * layer + c) + half + 1)
                        pool.tensor_tensor(attT[:, c, half * BANK:(half + 1) * BANK], weighted_exp[:, :], sum_exp[:, :],
                                           ALU.mult).then_inc(normalised, 1)
                m = moes[layer]
                pool.wait_ge(pv_done, PV_BEFORE[layer] + KC * U[layer])

                def load_weights(gate_up, down, dst_gu, dst_d, done):
                    for n, src in enumerate(gate_up):
                        width = 2 * m.I // len(gate_up)
                        pool.dma_start(dst_gu[:, :, n * width:(n + 1) * width],
                                       src.rearrange("(k p) n -> p k n", p=P)).then_inc(done, 16)
                    pool.dma_start(dst_d, down.rearrange("(k p) n -> p k n", p=P)).then_inc(done, 16)

                def expert(e, slot):
                    one = lambda w: w[bass.ds(e, 1)].rearrange("a k n -> (a k) n")
                    gate_up, down = ([Wg_r, Wu_r], Wd_r) if layer else ([Wgu0], Wd0)
                    load_weights([one(w) for w in gate_up], one(down), Wgu[layer][:, slot], Wd[layer][:, slot], w_in)
                    if layer == 0:
                        pool.dma_start(bgu[:, slot, :], bgu0[bass.ds(e, 1)].rearrange("a n -> (a n)").partition_broadcast(P)).then_inc(w_in, 16)
                        pool.dma_start(bd[:, slot, :], bd0[bass.ds(e, 1)].rearrange("a n -> (a n)").partition_broadcast(P)).then_inc(w_in, 16)

                if layer:
                    load_weights([Wg_s, Wu_s], Wd_s, shared_gu[:, :, :], shared_d[:, :, :], shared_in)
                early = 1 if layer else m.slots
                for q in range(early):
                    if q:
                        pool.wait_ge(w_in, W_BEFORE[layer] + q * W_LOAD[layer])
                    expert(q, q)
                if layer:
                    for f in range(m.IC):
                        pool.wait_ge(gu_hi_ready, f + 1)
                        pool.tensor_tensor(chunk_of(gu_lo, f), chunk_of(shared_gu, f), chunk_of(gu_hi, f).bitcast(F32),
                                           ALU.subtract).then_inc(gu_lo_ready, 1)
                pool.wait_ge(rows_ready, layer + 1)
                if layer == 0:
                    pool.wait_ge(xs_zeroed, 16)
                for k in range(TOP):
                    for t in range(NT):
                        pool.indirect_dma_start(
                            xs[:, :], bass.IndirectOffsetOnAxis(ap=row_i[:, k, t:t + 1], axis=0),
                            Xn[:, t, :], None).then_inc(scattered, 16)
                for q in range(early, m.slots):
                    pool.wait_ge(w_in, W_BEFORE[layer] + q * W_LOAD[layer])
                    pool.wait_ge(shared_psum, HALF * m.IC)
                    expert(q, q)
                pool.wait_ge(tables_ready, layer + 1)
                with pool.Fori(m.slots, E) as q:
                    done = pool.value_load(end_i[layer][0:1, bass.ds(q, 1)], min_val=1, max_val=m.blocks)
                    pool.wait_ge(w_in, (q * W_LOAD[layer] + W_BEFORE[layer]))
                    pool.wait_ge(y_dve, done + m.blocks_before)
                    expert(q, q % m.slots)
                for par in range(2):
                    pool.wait_ge(y_stored[par], 16 * (layer + 1) * ((m.blocks + 1 - par) // 2))
                for t in range(NT):
                    if t >= 4 or layer:
                        pool.wait_ge(added, NT * layer + max(t - 3, 0))
                    for k in range(TOP):
                        pool.indirect_dma_start(
                            got[:, t % 4, k, :], None, ys[:, :],
                            bass.IndirectOffsetOnAxis(ap=row_i[:, k, t:t + 1], axis=0)).then_inc(got_in[t % 4], 16)

        @block.scalar
        def _(act):
            def ln_and_transposes(n):
                def root(half):
                    act.wait_ge(var_ready, 2 * n + half + 1)
                    tiles = slice(NT // 2 * half, NT // 2 * (half + 1))
                    act.activation(std[:, tiles], var_eps[:, tiles], ACT.Sqrt).then_inc(std_ready, 1)

                def copy(half, kc):
                    act.wait_ge(xT_psum, 6 * n + 3 * half + kc + 1)
                    act.activation(XnT[:, kc, half * BANK:(half + 1) * BANK], PS[:, 3 * half + kc, :],
                                   ACT.Copy).then_inc(xT_act, 1)

                root(0)
                if n % 2:
                    root(1)
                for kc in range(KC):
                    copy(0, kc)
                if n % 2 == 0:
                    root(1)
                copy(1, 0)

            for layer in range(2):
                ln_and_transposes(2 * layer)
                act.wait_ge(bias_in, 16 * 3)
                for n, (kind, a, b) in enumerate(jobs(layer)):
                    act.wait_ge(job_psum, JOBS[0] * layer + n + 1)
                    bank = job_bank(n)
                    cols = slice(b * BANK, (b + 1) * BANK)
                    if kind == "q":
                        if layer == 0:
                            act.activation(q32[:, a, cols], PS[:, bank, :], ACT.Identity, bias=qk_bias[:, a:a + 1]).then_inc(job_act, 1)
                        else:
                            act.activation(q32[:, a, cols], PS[:, bank, :], ACT.Copy).then_inc(job_act, 1)
                        continue
                    if kind == "k":
                        if layer == 0:
                            act.activation(part["k_hi"][:, a, cols], PS[:, bank, :], ACT.Identity,
                                           bias=qk_bias[:, KC + a:KC + a + 1]).then_inc(hi_act, 1)
                        else:
                            act.activation(part["k_hi"][:, a, cols], PS[:, bank, :], ACT.Copy).then_inc(hi_act, 1)
                        continue
                    dst, src = rel_views(kind, "hi", a, bank)
                    act.activation(dst, src, ACT.Copy).then_inc(hi_act, 1)
                base = PV_BEFORE[layer]

                def copy_rows(c, part):
                    act.wait_ge(nmax_psum, 2 * (KC * layer + c) + part + 1)
                    for g in (2 * part, 2 * part + 1):
                        last = act.activation(QKB[3 * D:P, c % 2, 0, g, :],
                                              PS[D * g:D * g + D, 4:6, :].rearrange("p b n -> p (b n)"), ACT.Copy)
                    last.then_inc(nmax_act, 1)

                def unit_exps(c, unit, par, lo, hi):
                    for pair in range(2):
                        act.wait_ge(score_psum, unit * 2 + (2 * base + c * (2 * U[layer]) + pair + 1))
                        if pair == 0 and not (layer == 0 and c == 0 and isinstance(unit, int) and unit < 2):
                            act.wait_ge(pv_done, unit + (c * U[layer] + base - 1))
                        act.activation(expS[:, 2 * par + pair, :].rearrange("p (b n) -> p b n", b=2)[:, :, lo:hi],
                                       PS[:, 2 * pair:2 * pair + 2, lo:hi], ACT.Exp, scale=QK_SCALE).then_inc(exp_done, 1)

                if layer == 0:
                    act.wait_ge(xs_zeroed, 16)
                v_width = C if layer == 0 else P
                for t in range(NT):
                    act.wait_ge(v_psum, NT * layer + t + 1)
                    act.activation(V[:, t, 0:v_width], PS[:, 6 + t % 2, 0:v_width], ACT.Copy).then_inc(v_copied, 1)
                def copy_sums(c, half):
                    act.wait_ge(pv_done, PV_BEFORE[layer] + U[layer] * c + U[layer] // 2 * (half + 1))
                    if layer or c or half:
                        act.wait_ge(normalised, HALF * (KC * layer + c) + half)
                    act.activation(sum_exp[:, :], PS[:, 7, :], ACT.Copy).then_inc(pv_copied, 1)
                    act.activation(weighted_exp[:, :], PS[:, 6, :], ACT.Copy).then_inc(pv_copied, 1)

                def beside(c, unit):
                    if unit == 0 and c:
                        copy_sums(c - 1, 1)
                    if unit == U[layer] // 2:
                        copy_sums(c, 0)
                    if rows_at(layer, unit) is not None and c + 1 < KC:
                        copy_rows(c + 1, rows_at(layer, unit))

                act.activation(warm[:, :], ones[:, 0:1], ACT.Exp)
                act.wait_ge(parts_stored, 16 * PARTS_STORED[layer])
                copy_rows(0, 0)
                copy_rows(0, 1)
                for c in range(KC):
                    if layer == 0:
                        for first, last_unit in ((0, 2), (8, 10), (14, 16)):
                            for unit in range(first, last_unit):
                                unit_exps(c, unit, unit % 2, 0, BANK)
                                beside(c, unit)
                            if last_unit < 16:
                                with act.Fori(0, 3 if first == 0 else 2) as i:
                                    unit_exps(c, i * 2 + last_unit, 0, 0, BANK)
                                    unit_exps(c, i * 2 + (last_unit + 1), 1, 0, BANK)
                    else:
                        for unit, (half, kt, lo, hi) in enumerate(units(1)):
                            unit_exps(c, unit, unit % 2, lo, hi)
                            beside(c, unit)
                copy_sums(KC - 1, 1)
                m = moes[layer]
                ln_and_transposes(2 * layer + 1)
                def round_weights(chunks):
                    act.wait_ge(shared_in, 16 * 3)
                    for f in chunks:
                        act.activation(chunk_of(gu_hi, f), chunk_of(shared_gu, f), ACT.Copy).then_inc(gu_hi_ready, 1)

                if layer:
                    round_weights(range(1))
                for half in range(HALF):
                    cols = slice(half * BANK, (half + 1) * BANK)
                    if layer:
                        if half:
                            act.wait_ge(xT_dve, 2 * (2 * layer + 2))
                        for kc in range(KC):
                            act.wait_ge(xT_act, 4 * (2 * layer + 1) + 3 + half)
                            act.activation(xn_hi[:, kc, cols], XnT[:, kc, cols], ACT.Copy).then_inc(xn_hi_ready, 1)
                    act.wait_ge(logits_psum, 2 * layer + half + 1)
                    act.activation(logits_t[0:E, cols], PS[0:E, 6 + half, :], ACT.Identity,
                                   bias=router_b[0:E, layer:layer + 1]).then_inc(logits_act, 1)
                if layer:
                    round_weights(range(1, 3))
                act.wait_ge(gap_ready, layer + 1)
                act.activation(weight[:, 1, :], gap[:, :], ACT.Exp).then_inc(exp_gap, 1)
                if layer:
                    round_weights(range(3, m.IC))
                o = m.blocks_before

                if layer:
                    for n in range(HALF * m.IC):
                        act.wait_ge(shared_psum, n + 1)
                        if n >= 2:
                            act.wait_ge(shared_hid, n - 1)
                        act.activation(shared_gate[:, n % 2, :], PS[:, 2 * (n % 3), :], ACT.Silu).then_inc(shared_silu, 1)

                act.activation(warm[:, :], ones[:, 0:1], ACT.Silu if layer else ACT.Sigmoid)

                def copy_xT(b, par):
                    act.wait_ge(bT_psum, b + (o + 1))
                    if not (isinstance(b, int) and b < 2):
                        act.wait_ge(gu_psum, b + (o - 1))
                    act.activation(xbT[:, par].rearrange("p k n -> p (k n)"), PS[:, 6, 0:C], ACT.Copy).then_inc(bT_act, 1)

                def gate(b, par):
                    if layer:
                        act.wait_ge(gu_psum, b + (o + 1))
                    else:
                        act.wait_ge(pre_dve, b + 1)
                    if not (isinstance(b, int) and b < 2):
                        act.wait_ge(hid_done, b + (o - 1))
                    if layer:
                        act.activation(gated[:, par, 0:m.I], flat(3 * par, 3)[:, 0:m.I], ACT.Silu).then_inc(gate_act, 1)
                    else:
                        act.activation(gated[:, par, 0:m.I], pre[:, par, 0:m.I], ACT.Sigmoid, scale=ALPHA).then_inc(gate_act, 1)

                def copy_hT(b, par):
                    act.wait_ge(hT_psum, b + (o + 1))
                    if not (isinstance(b, int) and b < 2):
                        act.wait_ge(y_psum, b + (o - 1))
                    act.activation(hidT[:, par, 0:3].rearrange("p k n -> p (k n)"),
                                   PS[:, 3 * par, 0:3 * P], ACT.Copy).then_inc(hT_copied, 1)

                def step(b, place, more):
                    par = place % 2
                    copy_hT(b, par)
                    if more >= 2:
                        copy_xT(b + 2, par)
                    if more >= 1:
                        gate(b + 1, 1 - par)

                copy_xT(0, 0)
                copy_xT(1, 1)
                gate(0, 0)
                all_blocks(act, step)

        @block.vector
        def _(dve):
            st = Steps(dve, dve_step)

            def normalise(n, half, eps):
                tiles = range(NT // 2 * half, NT // 2 * (half + 1))
                ts = slice(tiles[0], tiles[-1] + 1)
                for t in tiles:
                    last = dve.bn_aggr(mv[:, t, :], stats[:, t, :])
                st.wait(last)
                dve.tensor_scalar(var_eps[:, ts], mv[:, ts, 1], eps, None, ALU.add).then_inc(var_ready, 1)
                dve.wait_ge(std_ready, 2 * n + half + 1)
                st.wait(dve.reciprocal(rstd[:, ts], std[:, ts]))
                for t in tiles:
                    dve.tensor_scalar(Xn[:, t, :], X[:, t, :], mv[:, t, 0:1], rstd[:, t:t + 1],
                                      ALU.subtract, ALU.mult).then_inc(xn_ready, 1)

            def copy_transposes(n):
                for kc in (1, 2):
                    dve.wait_ge(xT_psum, 6 * n + 3 + kc + 1)
                    dve.tensor_copy(XnT[:, kc, BANK:2 * BANK], PS[:, 3 + kc, :]).then_inc(xT_dve, 1)

            def statistics(t, sem, count):
                dve.wait_ge(sem, count)
                last = dve.bn_stats(stats[:, t, :], X[:, t, :])
                if t % (NT // 2) == NT // 2 - 1:
                    st.wait(last)

            for layer in range(2):
                if layer == 0:
                    for t in range(NT):
                        statistics(t, x_in[t // 2], 16)
                        if t % (NT // 2) == NT // 2 - 1:
                            normalise(0, t // (NT // 2), 1e-6)
                copy_transposes(2 * layer)
                dve.wait_ge(bias_in, 16 * 3)
                rounded = 0
                parts = part if layer == 0 else part1
                for n, (kind, a, b) in enumerate(jobs(layer)):
                    bank = job_bank(n)
                    cols = slice(b * BANK, (b + 1) * BANK)
                    if kind == "q":
                        if b == HALF - 1:
                            evacuated(dve, layer, n)
                            st.wait(dve.tensor_copy(parts["q_hi"][:, a, :], q32[:, a, :]))
                            dve.tensor_tensor(parts["q_lo"][:, a, :], q32[:, a, :], parts["q_hi"][:, a, :].bitcast(F32),
                                              ALU.subtract).then_inc(q_split, 1)
                        continue
                    rounded += 1
                    dve.wait_ge(hi_act, HI_JOBS * layer + rounded)
                    if kind == "k":
                        bias = qk_bias[:, KC + a:KC + a + 1] if layer == 0 else 0.0
                        dve.scalar_tensor_tensor(part["k_lo"][:, a, cols], PS[:, bank, :], bias,
                                                 part["k_hi"][:, a, cols].bitcast(F32), ALU.add,
                                                 ALU.subtract).then_inc(job_dve, 1)
                    else:
                        dst, src = rel_views(kind, "lo", a, bank)
                        hi, _ = rel_views(kind, "hi", a, bank)
                        dve.tensor_tensor(dst, src, hi.bitcast(F32), ALU.subtract).then_inc(job_dve, 1)

                def maxima(c, part):
                    with dve.Fori(0, TILES // 2 // NT) as i:
                        for qt in range(NT):
                            t = i * NT + (part * TILES // 2 + qt)
                            dve.wait_ge(max_psum, t + (TILES * (KC * layer + c) + 1))
                            lo, hi = keys_of(layer, qt)
                            if c == 0:
                                pair = (i * NT + (part * TILES // 2 + qt)) % 3
                                src = PS[:, bass.ds(pair * 2, 2), :] if layer == 0 else PS[:, bass.ds(pair * 2, 1), 0:hi - lo]
                            else:
                                src = PS[:, 4:6, :] if layer == 0 else PS[:, 4 + qt % 2, 0:hi - lo]
                            dve.tensor_reduce(nmax[:, c, bass.ds(t, 1)], src, axis=AX.X if layer and c else AX.XY,
                                              op=ALU.max, negate=True).then_inc(max_done, 1)

                maxima(0, 0)
                maxima(0, 1)
                for c in range(KC):
                    for half in range(HALF):
                        if c + 1 < KC:
                            maxima(c + 1, half)
                        dve.wait_ge(pv_copied, 2 * (HALF * (KC * layer + c) + half + 1))
                        dve.reciprocal(sum_exp[:, :], sum_exp[:, :]).then_inc(inverted, 1)
                m = moes[layer]
                for t in range(NT):
                    dve.wait_ge(proj_psum, NT * layer + t + 1)
                    if layer == 0:
                        dve.wait_ge(x_biased, 1)
                    dve.tensor_tensor(X[:, t, :], X[:, t, :], PS[:, t, 0:C], ALU.add).then_inc(proj_dve, 1)
                    statistics(t, proj_dve, NT * layer + t + 1)
                    if t % (NT // 2) == NT // 2 - 1:
                        normalise(2 * layer + 1, t // (NT // 2), 1e-5)
                copy_transposes(2 * layer + 1)
                if layer:
                    for half in range(HALF):
                        cols = slice(half * BANK, (half + 1) * BANK)
                        for kc in range(KC):
                            dve.wait_ge(xn_hi_ready, KC * half + kc + 1)
                            dve.tensor_tensor(xn_lo[kc][:, cols], XnT[:, kc, cols], xn_hi[:, kc, cols].bitcast(F32),
                                              ALU.subtract).then_inc(xn_lo_ready, 1)

                dve.wait_ge(pool_const, 2)
                dve.wait_ge(route_psum, layer + 1)
                st.wait(dve.tensor_copy(logits[:, :, :], PS[:, 6, 0:NT * E].rearrange("p (t e) -> p t e", e=E)))
                for t in range(NT):
                    last = dve.max(top8[:, t, :], logits[:, t, :])
                st.wait(last)
                for t in range(NT):
                    last = dve.max_index(top8i[:, t, :], top8[:, t, :], logits[:, t, :])
                st.wait(last)
                dve.tensor_tensor(gap[:, :], top8[:, :, 1], top8[:, :, 0], ALU.subtract).then_inc(gap_ready, 1)
                st.wait(dve.tensor_copy(top_f[:, :, :], top8i[:, :, 0:2]))
                for k in range(TOP):
                    last = dve.tensor_tensor(chosen[:, k],
                                             iota_e[:, :].rearrange("p (a e) -> p a e", a=1).broadcast_to([P, NT, E]),
                                             top_f[:, :, k:k + 1].broadcast_to([P, NT, E]), ALU.is_equal)
                st.wait(last)
                dve.tensor_tensor(picked[:, :, :], chosen[:, 0], chosen[:, 1], ALU.add).then_inc(picked_ready, 1)
                dve.wait_ge(exp_gap, layer + 1)
                st.wait(dve.tensor_scalar(weight[:, 0, :], weight[:, 1, :], 1.0, None, ALU.add))
                st.wait(dve.reciprocal(weight[:, 0, :], weight[:, 0, :]))
                st.wait(dve.tensor_tensor(weight[:, 1, :], weight[:, 1, :], weight[:, 0, :], ALU.mult))
                dve.wait_ge(rank_psum, layer + 1)
                rank = PS[:, 7, 0:NT * E].rearrange("p (t e) -> p t e", e=E)
                count = PS[:, 7, NT * E:2 * NT * E].rearrange("p (t e) -> p t e", e=E)
                st.wait(dve.tensor_copy(tile_cum[0][:, :, :], count))
                for r, shift in enumerate((1, 2, 4)):
                    src, dst = tile_cum[r], tile_cum[r + 1]
                    dve.tensor_copy(dst[:, 0:shift], src[:, 0:shift])
                    st.wait(dve.tensor_tensor(dst[:, shift:], src[:, shift:], src[:, :NT - shift], ALU.add))
                st.wait(dve.tensor_tensor(over[:, :, :], tile_cum[3][:, NT - 1, :].rearrange("p (e a) -> p e a", a=1).broadcast_to([P, E, 8]),
                                          thresholds[:, :].rearrange("p (a k) -> p a k", a=1).broadcast_to([P, E, 8]), ALU.is_gt))
                st.wait(dve.tensor_reduce(blk_cum[0][:, :], over[:, :, :], axis=AX.X, op=ALU.add))
                for r, shift in enumerate((1, 2, 4)):
                    src, dst = blk_cum[r], blk_cum[r + 1]
                    dve.tensor_copy(dst[:, 0:shift], src[:, 0:shift])
                    st.wait(dve.tensor_tensor(dst[:, shift:], src[:, shift:], src[:, :E - shift], ALU.add))
                st.wait(dve.tensor_tensor(start_row[:, :], blk_cum[3][:, :], blk_cum[0][:, :], ALU.subtract))
                st.wait(dve.tensor_scalar(start_row[:, :], start_row[:, :], float(P), None, ALU.mult))
                st.wait(dve.tensor_tensor(place[:, :, :], tile_cum[3][:, :, :], tile_cum[0][:, :, :], ALU.subtract))
                st.wait(dve.tensor_tensor(place[:, :, :], place[:, :, :], rank, ALU.add))
                st.wait(dve.tensor_tensor(place[:, :, :], place[:, :, :],
                                          start_row[:, :].rearrange("p (a e) -> p a e", a=1).broadcast_to([P, NT, E]), ALU.add))
                for k in range(TOP):
                    last = dve.tensor_tensor(place_k[:, k], place[:, :, :], chosen[:, k], ALU.mult)
                st.wait(last)
                st.wait(dve.tensor_reduce(row_f[:, :, :], place_k[:, :, :, :], axis=AX.X, op=ALU.add))
                dve.tensor_copy(row_i[:, :, :], row_f[:, :, :]).then_inc(rows_ready, 1)
                nr = ROUTED_BLOCKS
                st.wait(dve.tensor_tensor(blk_ge[:, 0:nr], iota_blk[:, 0:nr].rearrange("p (b a) -> p b a", a=1).broadcast_to([P, nr, E]),
                                          blk_cum[3][:, :].rearrange("p (a e) -> p a e", a=1).broadcast_to([P, nr, E]), ALU.is_ge))
                st.wait(dve.tensor_reduce(ord_f[:, 0:nr], blk_ge[:, 0:nr], axis=AX.X, op=ALU.add))
                st.wait(dve.tensor_scalar(ord_f[:, 0:nr], ord_f[:, 0:nr], float(E - 1), None, ALU.min))
                dve.tensor_copy(end_i[layer][:, m.slots:E], blk_cum[3][:, 0:E - m.slots])
                st.wait(dve.tensor_copy(ord_i[layer][:, 0:nr], ord_f[:, 0:nr]))
                dve.sem_inc(tables_ready, 1)

                o = m.blocks_before
                if layer:
                    for n in range(HALF * m.IC):
                        half, f = n // m.IC, n % m.IC
                        dve.wait_ge(shared_silu, n + 1)
                        dve.tensor_tensor(shared_hidT[:, f, half * BANK:(half + 1) * BANK], shared_gate[:, n % 2, :],
                                          PS[:, 2 * (n % 3) + 1, :], ALU.mult).then_inc(shared_hid, 1)
                    for t in range(NT):
                        dve.wait_ge(shared_y, t + 1)
                        dve.tensor_tensor(X[:, t, :], X[:, t, :], PS[:, 3 + t % 3, 0:C], ALU.add).then_inc(shared_added, 1)

                def copy_hT(b, par):
                    dve.wait_ge(hT_psum, b + (o + 1))
                    if not (isinstance(b, int) and b < 2):
                        dve.wait_ge(y_psum, b + (o - 1))
                    dve.tensor_copy(hidT[:, par, 3:6].rearrange("p k n -> p (k n)"),
                                    PS[:, 3 * par + 1, 0:3 * P]).then_inc(hT_copied, 1)

                def hidden(b, par):
                    I = m.I
                    if layer:
                        dve.wait_ge(gate_act, b + (o + 1))
                        if not (isinstance(b, int) and b < 2):
                            dve.wait_ge(hT_psum, b + (o - 1))
                        dve.tensor_tensor(hid[:, par, 0:I], gated[:, par, 0:I], flat(3 * par, 3)[:, I:2 * I],
                                          ALU.mult).then_inc(hid_done, 1)
                        return
                    q = dve.value_load(ord_i[layer][0:1, bass.ds(b, 1)], min_val=0, max_val=E - 1)
                    dve.wait_ge(gu_psum, b + 1)
                    s = q % m.slots
                    dve.wait_ge(w_in, (q + 1) * W_LOAD[layer])
                    st.wait(dve.tensor_tensor(pre[:, par, 0:2 * I], flat(3 * par, 2)[:, 0:2 * I],
                                              bgu[:, bass.ds(s, 1), :].rearrange("p a n -> p (a n)"), ALU.add))
                    st.wait(dve.tensor_scalar(pre[:, par, 0:I], pre[:, par, 0:I], LIMIT, None, ALU.min))
                    dve.tensor_scalar(pre[:, par, I:2 * I], pre[:, par, I:2 * I], LIMIT, -LIMIT, ALU.min, ALU.max).then_inc(pre_dve, 1)
                    dve.wait_ge(gate_act, b + 1)
                    if not (isinstance(b, int) and b < 2):
                        dve.wait_ge(hT_psum, b - 1)
                    st.wait(dve.tensor_tensor(gated[:, par, I:2 * I], gated[:, par, 0:I], pre[:, par, 0:I], ALU.mult))
                    dve.scalar_tensor_tensor(hid[:, par, 0:I], pre[:, par, I:2 * I], 1.0, gated[:, par, I:2 * I],
                                             ALU.add, ALU.mult).then_inc(hid_done, 1)

                def stored_before(b, par):
                    return b * 8 + (layer * 16 * ((m.blocks + 1 - par) // 2) - 8 * par)

                def copy_y(b, par):
                    if layer == 0:
                        q = dve.value_load(ord_i[layer][0:1, bass.ds(b, 1)], min_val=0, max_val=E - 1)
                    dve.wait_ge(y_psum, b + (o + 1))
                    if layer or not (isinstance(b, int) and b < 2):
                        dve.wait_ge(y_stored[par], stored_before(b, par))
                    if layer:
                        dve.tensor_copy(yb[:, par, :], PS[:, 7, 0:C]).then_inc(y_dve, 1)
                    else:
                        dve.tensor_tensor(yb[:, par, :], PS[:, 7, 0:C],
                                          bd[:, bass.ds(q % m.slots, 1), :].rearrange("p a n -> p (a n)"), ALU.add).then_inc(y_dve, 1)

                def step(b, place, more):
                    par = place % 2
                    if layer:
                        copy_hT(b, par)
                    if more >= 1:
                        hidden(b + 1, 1 - par)
                    copy_y(b, par)

                hidden(0, 0)
                for b in range(FIRST):
                    step(b, b, 4)
                with dve.Fori(0, TURNS) as i:
                    if layer == 0:
                        st.enter(i, 12)
                    for n in range(4):
                        step(i * 4 + (FIRST + n), (FIRST + n) % 4, 4)
                if layer == 0:
                    st.leave(TURNS)
                for b in range(LAST, m.blocks):
                    step(b, b % 4, m.blocks - 1 - b)
                if layer:
                    dve.wait_ge(shared_added, NT)
                for t in range(NT):
                    dve.wait_ge(got_in[t % 4], 64 * layer + 32 * (t // 4 + 1))
                    st.wait(dve.scalar_tensor_tensor(X[:, t, :], got[:, t % 4, 0, :], weight[:, 0, t:t + 1], X[:, t, :],
                                                     ALU.mult, ALU.add))
                    dve.scalar_tensor_tensor(X[:, t, :], got[:, t % 4, 1, :], weight[:, 1, t:t + 1], X[:, t, :],
                                             ALU.mult, ALU.add).then_inc(added, 1)
                    if layer == 0:
                        statistics(t, added, t + 1)
                        if t % (NT // 2) == NT // 2 - 1:
                            normalise(2, t // (NT // 2), 1e-6)

        @block.tensor
        def _(pe):
            pe.wait_ge(ident_ready, 1)

            def run_jobs(layer, first, end):
                pe.wait_ge(wqkv_in[layer], 16)
                for n, (kind, a, b) in list(enumerate(jobs(layer)))[first:end]:
                    bank = job_bank(n)
                    if n >= 8:
                        evacuated(pe, layer, n - 8)
                    if kind in ("q", "k"):
                        col = (0 if kind == "q" else C) + a * P
                        for kc in range(KC):
                            last = pe.matmul(PS[:, bank, :], Wqkv[:, kc, col:col + P], XnT[:, kc, b * BANK:(b + 1) * BANK],
                                             start=kc == 0, stop=kc == KC - 1)
                    else:
                        if a == 0 and kind == "relh":
                            evacuated(pe, layer, HALF * KC - 1)
                            pe.wait_ge(rel_ready, 1)
                        table = relh_bd if kind == "relh" else relw_bd
                        for r in range(4):
                            i = 4 * a + r
                            rhs = (q32[:, :, i * GRID:(i + 1) * GRID] if kind == "relh" else
                                   q32[:, :, :].rearrange("p c (h w) -> p c h w", w=GRID)[:, :, :, i])
                            last = pe.matmul(PS[:, bank, r * KC * GRID:(r + 1) * KC * GRID].rearrange("p (c n) -> p c n", c=KC),
                                             table[:, i:i + GRID, :].rearrange("p j g -> p (j g)"), rhs, start=r == 0, stop=r == 3, skip_group_check=True)
                    last.then_inc(job_psum, 1)

            def transposes(n):
                layer = n // 2
                for half in range(HALF):
                    if n % 2:
                        pe.wait_ge(proj_dve, NT * layer + 3 * (half + 1))
                    for kc in range(KC):
                        for t in range(4 * half, 4 * half + 4):
                            pe.wait_ge(xn_ready, NT * n + t + 1)
                            last = pe.transpose(PS[:, 3 * half + kc, (t % 4) * P:(t % 4 + 1) * P], Xn[:, t, kc * P:(kc + 1) * P], ident[:, :])
                        last.then_inc(xT_psum, 1)
                    pe.wait_ge(xT_act, 4 * n + 3 + half)
                    if half:
                        pe.wait_ge(xT_dve, 2 * (n + 1))
                    if n % 2:
                        pe.wait_ge(const_in, 16 * 4)
                        pe.wait_ge(proj_dve, NT * layer + 7 + half)
                        for kc in range(KC):
                            last = pe.matmul(PS[0:E, 6 + half, :], router_w[:, layer, kc, :], XnT[:, kc, half * BANK:(half + 1) * BANK],
                                             start=kc == 0, stop=kc == KC - 1)
                        last.then_inc(logits_psum, 1)
                    elif half == 0:
                        run_jobs(layer, 0, EARLY_JOBS[layer])
            for layer in range(2):
                transposes(2 * layer)
                run_jobs(layer, EARLY_JOBS[layer], JOBS[layer])
                v_col, v_width = (2 * C, C) if layer == 0 else (C + P, P)
                njobs = len(jobs(layer))
                for n in range(njobs - 8, njobs):
                    evacuated(pe, layer, n)

                def values(t):
                    if t >= 2:
                        pe.wait_ge(v_copied, NT * layer + t - 1)
                    for kc in range(KC):
                        last = pe.matmul(PS[:, 6 + t % 2, 0:v_width], XnT[:, kc, t * P:(t + 1) * P],
                                         Wqkv[:, kc, v_col:v_col + v_width], start=kc == 0, stop=kc == KC - 1)
                    last.then_inc(v_psum, 1)

                def max_tile(c, t):
                    g, qt = t // NT, t % NT
                    number = TILES * (KC * layer + c) + t
                    lo, hi = keys_of(layer, qt)
                    if c == 0:
                        bank = 2 * (t % 3)
                        if t >= 3:
                            pe.wait_ge(max_done, number - 2)
                    else:
                        bank = 4 if layer == 0 else 4 + qt % 2
                        pe.wait_ge(max_done, number if layer == 0 or t == 0 else number - 1)
                        if t == TILES // 2:
                            pe.wait_ge(nmax_act, 2 * (KC * layer + c) + 1)
                    for k0 in range(lo, hi, BANK):
                        k1 = min(k0 + BANK, hi)
                        last = pe.matmul(PS[:, bank + (k0 - lo) // BANK, 0:k1 - k0], QA[:, c % 2, g, qt * P:(qt + 1) * P],
                                         KA[:, c % 2 if layer == 0 else 0, g, k0:k1], start=True, stop=True)
                    last.then_inc(max_psum, 1)

                def maxima_rows(c, part):
                    pe.wait_ge(max_done, TILES * (KC * layer + c) + (TILES if c == 0 else TILES // 2 * (part + 1)))
                    for qt in range(NT):
                        for g in (2 * part, 2 * part + 1):
                            col = NT * g + qt
                            last = pe.matmul(PS[D * g:D * g + D, 4 + qt // 4, (qt % 4) * P:(qt % 4 + 1) * P],
                                             nmax[:, c, col:col + 1].broadcast_to([P, D]), ident[:, :],
                                             start=qt % 4 == 0, stop=qt % 4 == 3, skip_group_check=True)
                    last.then_inc(nmax_psum, 1)

                def scores(c, u, pair):
                    half, kt, lo, hi = units(layer)[u]
                    use = 2 * (PV_BEFORE[layer] + U[layer] * c + u) + pair
                    if u == 0:
                        pe.wait_ge(nmax_act, 2 * (KC * layer + c) + pair + 1)
                        pe.wait_ge(b_in[c % 2], placed(B_DMAS, layer, c))
                    if use >= 2:
                        pe.wait_ge(exp_done, use - 1)
                    for j in range(2):
                        g = 2 * pair + j
                        ks, keys = c % 2 if layer == 0 else 0, slice(kt * P, (kt + 1) * P)
                        queries = slice(half * BANK + lo, half * BANK + hi)
                        pe.matmul(PS[:, 2 * pair + j, lo:hi], KA[:, ks, g, keys], QA[:, c % 2, g, queries],
                                  start=True, stop=False)
                        last = pe.matmul(PS[:, 2 * pair + j, lo:hi], QKB[:, ks, 1, g, keys], QKB[:, c % 2, 0, g, queries],
                                         start=False, stop=True)
                    last.then_inc(score_psum, 1)

                def probabilities(u, g):
                    half, kt, lo, hi = units(layer)[u]
                    return expS[:, 2 * (u % 2) + g // 2, (g % 2) * BANK + lo:(g % 2) * BANK + hi]

                def weighted(c, u):
                    half, kt, lo, hi = units(layer)[u]
                    first, last_one = u % (U[layer] // 2) == 0, (u + 1) % (U[layer] // 2) == 0
                    pe.wait_ge(exp_done, 2 * (PV_BEFORE[layer] + U[layer] * c + u + 1))
                    if first and (layer or c or half):
                        pe.wait_ge(pv_copied, 2 * (2 * (KC * layer + c) + half))
                    for g in range(G):
                        vcol = P * c + D * g if layer == 0 else D * g
                        pe.matmul(PS[D * g:D * g + D, 6, lo:hi], V[:, kt, vcol:vcol + D], probabilities(u, g),
                                  start=first, stop=last_one, skip_group_check=True)

                def sums(c, u):
                    half, kt, lo, hi = units(layer)[u]
                    first, last_one = u % (U[layer] // 2) == 0, (u + 1) % (U[layer] // 2) == 0
                    for g in range(G):
                        last = pe.matmul(PS[D * g:D * g + D, 7, lo:hi], ones[:, 0:D], probabilities(u, g),
                                         start=first, stop=last_one, skip_group_check=True)
                    last.then_inc(pv_done, 1)

                for t in range(TILES):
                    if t % G == 0:
                        values(t // G)
                    if t == 0:
                        pe.wait_ge(a_in[0], placed(A_DMAS, layer, 0))
                    max_tile(0, t)
                pe.wait_ge(pool_const, 2)
                pe.wait_ge(v_copied, NT * (layer + 1))
                pe.wait_ge(v_biased, NT)
                maxima_rows(0, 0)
                maxima_rows(0, 1)
                scores(0, 0, 0)
                scores(0, 0, 1)
                for c in range(KC):
                    for u in range(U[layer]):
                        tiles = list(tiles_at(layer, u)) if c + 1 < KC else []
                        if tiles and tiles[0] == 0:
                            pe.wait_ge(a_in[(c + 1) % 2], placed(A_DMAS, layer, c + 1))
                        rows = rows_at(layer, u) if c + 1 < KC else None
                        if rows is not None:
                            maxima_rows(c + 1, rows)
                        after = (c, u + 1) if u + 1 < U[layer] else (c + 1, 0)
                        if after[0] < KC:
                            scores(*after, 0)
                        early = 0 if rows is not None else 2
                        for t in tiles[:early][:1]:
                            max_tile(c + 1, t)
                        if after[0] < KC and rows != 1:
                            scores(*after, 1)
                        weighted(c, u)
                        for t in tiles[:early][1:]:
                            max_tile(c + 1, t)
                        sums(c, u)
                        if after[0] < KC and rows == 1:
                            scores(*after, 1)
                        for t in tiles[early:]:
                            max_tile(c + 1, t)
                for t in range(NT):
                    pe.wait_ge(normalised, HALF * (KC * layer + KC - 1) + t // (NT // HALF) + 1)
                    if t == 0:
                        pe.wait_ge(wproj_in, 16 * (layer + 1))
                    for kc in range(KC):
                        last = pe.matmul(PS[:, t, 0:C], attT[:, kc, t * P:(t + 1) * P], Wproj[:, kc, :],
                                         start=kc == 0, stop=kc == KC - 1)
                    last.then_inc(proj_psum, 1)

                m = moes[layer]
                transposes(2 * layer + 1)
                pe.wait_ge(logits_act, 2 * (layer + 1))
                for t in range(NT):
                    last = pe.transpose(PS[:, 6, t * E:(t + 1) * E], logits_t[0:E, t * P:(t + 1) * P], ident[0:E, 0:E])
                last.then_inc(route_psum, 1)

                def ranks():
                    pe.wait_ge(picked_ready, layer + 1)
                    pk = picked[:, :, :].rearrange("p t e -> p (t e)")
                    pe.matmul(PS[:, 7, 0:NT * E], before[:, :], pk, start=True, stop=True)
                    pe.matmul(PS[:, 7, NT * E:2 * NT * E], ones[:, :], pk, start=True, stop=True).then_inc(rank_psum, 1)

                o = m.blocks_before
                if layer == 0:
                    ranks()
                else:
                    for n in range(HALF * m.IC):
                        half, f = n // m.IC, n % m.IC
                        cols = slice(half * BANK, (half + 1) * BANK)
                        pe.wait_ge(xn_lo_ready, KC * (half + 1))
                        pe.wait_ge(gu_lo_ready, f + 1)
                        if n >= 3:
                            pe.wait_ge(shared_hid, n - 2)
                        for up in range(2):
                            hidden = slice(up * m.I + f * P, up * m.I + (f + 1) * P)
                            products = [(w[:, kc, hidden], rows[:, cols]) for kc in range(KC) for w, rows in
                                        ((gu_hi, xn_hi[:, kc]), (gu_hi, xn_lo[kc]), (gu_lo, xn_hi[:, kc]))]
                            for i, (w, rows) in enumerate(products):
                                last = pe.matmul(PS[:, 2 * (n % 3) + up, :], w, rows, start=i == 0, stop=i == len(products) - 1)
                        last.then_inc(shared_psum, 1)
                        if n == 1:
                            ranks()
                    pe.wait_ge(shared_hid, HALF * m.IC)
                    for t in range(NT):
                        if t >= 3:
                            pe.wait_ge(shared_added, t - 2)
                        for f in range(m.IC):
                            last = pe.matmul(PS[:, 3 + t % 3, 0:C], shared_hidT[:, f, t * P:(t + 1) * P], shared_d[:, f, :],
                                             start=f == 0, stop=f == m.IC - 1)
                        last.then_inc(shared_y, 1)
                pe.wait_ge(tables_ready, layer + 1)

                def transpose_x(b, place):
                    before_layer = layer * ((m.blocks + 3 - place) // 4)
                    pe.wait_ge(xb_in[place], b * 4 + (16 + 16 * before_layer - 4 * place))
                    if not (isinstance(b, int) and b == 0):
                        pe.wait_ge(bT_act, b + o)
                    for kc in range(KC):
                        last = pe.transpose(PS[:, 6, kc * P:(kc + 1) * P], xb[:, place, kc * P:(kc + 1) * P], ident[:, :])
                    last.then_inc(bT_psum, 1)

                def gate_up(b, par):
                    q = pe.value_load(ord_i[layer][0:1, bass.ds(b, 1)], min_val=0, max_val=E - 1)
                    pe.wait_ge(bT_act, b + (o + 1))
                    pe.wait_ge(w_in, (q + 1) * W_LOAD[layer] + W_BEFORE[layer])
                    s = q % m.slots
                    width = 2 * m.I
                    for lo in range(0, width, BANK):
                        n = min(BANK, width - lo)
                        for kc in range(KC):
                            last = pe.matmul(PS[:, 3 * par + lo // BANK, 0:n], xbT[:, par, kc, :],
                                             Wgu[layer][:, bass.ds(s, 1), kc, lo:lo + n],
                                             start=kc == 0, stop=kc == KC - 1)
                    last.then_inc(gu_psum, 1)

                def transpose_h(b, par):
                    pe.wait_ge(hid_done, b + (o + 1))
                    for i in range(m.IC):
                        last = pe.transpose(PS[:, 3 * par + i // 3, (i % 3) * P:(i % 3 + 1) * P],
                                            hid[:, par, i * P:(i + 1) * P], ident[:, :])
                    last.then_inc(hT_psum, 1)

                def down(b, par):
                    per = 2 if layer else 1
                    q = pe.value_load(ord_i[layer][0:1, bass.ds(b, 1)], min_val=0, max_val=E - 1)
                    pe.wait_ge(hT_copied, b * per + (per + layer * ROUTED_BLOCKS))
                    if not (isinstance(b, int) and b == 0):
                        pe.wait_ge(y_dve, b + o)
                    s = q % m.slots
                    for i in range(m.IC):
                        last = pe.matmul(PS[:, 7, 0:C], hidT[:, par, i, :], Wd[layer][:, bass.ds(s, 1), i, :],
                                         start=i == 0, stop=i == m.IC - 1)
                    last.then_inc(y_psum, 1)

                def step(b, place, more):
                    par = place % 2
                    if more >= 1:
                        gate_up(b + 1, 1 - par)
                    transpose_h(b, par)
                    if more >= 2:
                        transpose_x(b + 2, (place + 2) % 4)
                    down(b, par)

                transpose_x(0, 0)
                gate_up(0, 0)
                transpose_x(1, 1)
                if layer:
                    pe.wait_ge(shared_added, NT)
                all_blocks(pe, step)


_OUT = ((1, 32, 32, 384), "float32")


def kernel(**inputs):
    import numpy as np
    import concourse.bacc as bacc
    from concourse.bass_utils import run_bass_kernel_spmd as run

    a = {k: np.ascontiguousarray(v) for k, v in inputs.items()}
    arrays = {
        "x": a["x"].reshape(T, C),
        "qkv_w": a["L0_conv_qkv_w"], 
        "qk_b": np.ascontiguousarray(a["L0_conv_qkv_b"][:2 * C].reshape(2 * KC, P).T),
        "v_b": np.ascontiguousarray(a["L0_conv_qkv_b"][2 * C:]),
        "proj_w": a["L0_conv_proj_w"], "proj_b": a["L0_conv_proj_b"],
        "rel_both": np.ascontiguousarray(np.stack([a["L0_conv_rel_pos_h"].T, a["L0_conv_rel_pos_w"].T], 1)),
        "Wr0": a["L0_ffn_Wr"], "br0": a["L0_ffn_br"], "Wgu0": a["L0_ffn_Wgu"], "bgu0": a["L0_ffn_bgu"],
        "Wd0": a["L0_ffn_Wd"], "bd0": a["L0_ffn_bd"],
        "w_qkv1": np.ascontiguousarray(a["L1_conv_w_qkv"].T),
        "w_out1": np.ascontiguousarray(a["L1_conv_w_out"].T),
        "Wg_s": a["L1_ffn_Wg_s"][0], "Wu_s": a["L1_ffn_Wu_s"][0], "Wd_s": a["L1_ffn_Wd_s"][0],
        "Wg_r": a["L1_ffn_Wg_r"], "Wu_r": a["L1_ffn_Wu_r"], "Wd_r": a["L1_ffn_Wd_r"],
        "Wr1": a["L1_ffn_W_router"], "br1": a["L1_ffn_expert_bias"],
    }
    nc = bacc.Bacc("TRN2", target_bir_lowering=False, num_devices=1)
    args = {k: nc.dram_tensor(f"in_{k}", v.shape, mybir.dt.from_np(v.dtype), kind="ExternalInput").ap()
            for k, v in arrays.items()}
    out = nc.dram_tensor("out_0", (T, C), mybir.dt.from_np(np.dtype(_OUT[1])), kind="ExternalOutput").ap()
    build(nc, out=out, **args)
    r = run(nc, [{f"in_{k}": v for k, v in arrays.items()}], core_ids=[0])
    return r.results[0]["out_0"].reshape(_OUT[0])
```
